# Optimizing a Trainium2 kernel written in Bass

```python
import numpy as np
import jax
import jax.numpy as jnp

def _softmax(x, axis=-1):
    return jax.nn.softmax(x, axis=axis)

def _gelu(x):
    return jax.nn.gelu(x, approximate=True)

def _silu(x):
    return jax.nn.silu(x)

def _sigmoid(x):
    return jax.nn.sigmoid(x)

def _layernorm(x, axis=-1, eps=1e-05):
    m = jnp.mean(x, axis=axis, keepdims=True)
    v = jnp.var(x, axis=axis, keepdims=True)
    return (x - m) / jnp.sqrt(v + eps)

def _scatter_add(tgt, idx, src, axis=0):
    return tgt.at[idx].add(src)

def _segment_sum(src, seg, n):
    return jax.ops.segment_sum(src, seg, n)
kernel_name = 'mk_audio_tower_d2_tok_audfeat512_r4_7dc85b'

def setup_inputs(seed: int=0):
    np.random.seed(seed)
    _w = jnp.asarray

    def _rec_inputs():
        import jax
        import jax.numpy as jnp
        _rk = jax.random.key(seed)
        x = -0.000125008 + 0.999885 * jax.random.normal(jax.random.fold_in(_rk, 1), (8, 64, 750), jnp.float32)
        return x
    x = _rec_inputs()

    def _L0_tok_setup():
        import jax, jax.numpy as jnp
        import numpy as np
        from jax import lax
        STRIDE = 1
        PADDING = 4
        key = jax.random.key(seed)
        k1, k2, k3 = jax.random.split(key, 3)
        B, C_IN, L = (32, 64, 1024)
        C_OUT, K = (128, 9)
        x = jax.random.normal(k1, (B, C_IN, L), dtype=jnp.float32)
        weight = jax.random.normal(k2, (C_OUT, C_IN, K), dtype=jnp.float32)
        bias = jax.random.normal(k3, (C_OUT,), dtype=jnp.float32)
        return {'x': x, 'weight': weight, 'bias': bias}
    _L0_tok_all = _L0_tok_setup()
    _L0_tok_in = {k: v for k, v in _L0_tok_all.items() if k in ('weight', 'bias')}
    del _L0_tok_all

    def _L0_attn_setup():
        import jax, jax.numpy as jnp
        import numpy as np
        B, S, D_MODEL, D_ATT = (4, 1024, 128, 64)
        EPS = 1e-05
        key = jax.random.key(seed)
        ks = jax.random.split(key, 10)
        s_in = 1.0 / np.sqrt(D_MODEL)
        return {'x': jax.random.normal(ks[0], (B, S, D_MODEL), jnp.float32), 'Wq': jax.random.uniform(ks[1], (D_MODEL, D_ATT), jnp.float32, -s_in, s_in), 'bq': jax.random.uniform(ks[2], (D_ATT,), jnp.float32, -s_in, s_in), 'Wk': jax.random.uniform(ks[3], (D_MODEL, D_ATT), jnp.float32, -s_in, s_in), 'bk': jax.random.uniform(ks[4], (D_ATT,), jnp.float32, -s_in, s_in), 'Wv': jax.random.uniform(ks[5], (D_MODEL, D_MODEL), jnp.float32, -s_in, s_in), 'bv': jax.random.uniform(ks[6], (D_MODEL,), jnp.float32, -s_in, s_in), 'gamma': jnp.ones((D_MODEL,), jnp.float32), 'beta': jnp.zeros((D_MODEL,), jnp.float32)}
    _L0_attn_all = _L0_attn_setup()
    _L0_attn_in = {k: v for k, v in _L0_attn_all.items() if k in ('Wq', 'bq', 'Wk', 'bk', 'Wv', 'bv', 'gamma', 'beta')}
    del _L0_attn_all

    def _L0_ffn_setup():
        import jax, jax.numpy as jnp
        import numpy as np
        B, T, D = (4, 2048, 128)
        E, F, CAP = (8, 512, 1024)
        key = jax.random.key(seed)
        ks = jax.random.split(key, 6)
        s = 0.02
        return {'x': jax.random.normal(ks[0], (B, T, D), dtype=jnp.float32), 'Wr': jax.random.normal(ks[1], (D, E), dtype=jnp.float32) * s, 'W1': jax.random.normal(ks[2], (E, D, F), dtype=jnp.float32) * s, 'b1': jax.random.normal(ks[3], (E, F), dtype=jnp.float32) * s, 'W2': jax.random.normal(ks[4], (E, F, D), dtype=jnp.float32) * s, 'b2': jax.random.normal(ks[5], (E, D), dtype=jnp.float32) * s}
    _L0_ffn_all = _L0_ffn_setup()
    _L0_ffn_in = {k: v for k, v in _L0_ffn_all.items() if k in ('Wr', 'W1', 'b1', 'W2', 'b2')}
    del _L0_ffn_all

    def _L1_attn_setup():
        import jax, jax.numpy as jnp
        import numpy as np
        EMBED_DIM = 128
        NUM_HEADS = 8
        HEAD_DIM = EMBED_DIM // NUM_HEADS
        SCALE = HEAD_DIM ** (-0.5)
        key = jax.random.key(seed)
        ks = jax.random.split(key, 9)
        B, S, D = (2, 1024, EMBED_DIM)
        init = 1.0 / np.sqrt(D)
        x = jax.random.normal(ks[0], (B, S, D), dtype=jnp.float32)
        Wq = jax.random.uniform(ks[1], (D, D), jnp.float32, -init, init)
        Wk = jax.random.uniform(ks[2], (D, D), jnp.float32, -init, init)
        Wv = jax.random.uniform(ks[3], (D, D), jnp.float32, -init, init)
        Wo = jax.random.uniform(ks[4], (D, D), jnp.float32, -init, init)
        bq = jax.random.uniform(ks[5], (D,), jnp.float32, -init, init)
        bk = jax.random.uniform(ks[6], (D,), jnp.float32, -init, init)
        bv = jax.random.uniform(ks[7], (D,), jnp.float32, -init, init)
        bo = jax.random.uniform(ks[8], (D,), jnp.float32, -init, init)
        return {'x': x, 'Wq': Wq, 'bq': bq, 'Wk': Wk, 'bk': bk, 'Wv': Wv, 'bv': bv, 'Wo': Wo, 'bo': bo}
    _L1_attn_all = _L1_attn_setup()
    _L1_attn_in = {k: v for k, v in _L1_attn_all.items() if k in ('Wq', 'bq', 'Wk', 'bk', 'Wv', 'bv', 'Wo', 'bo')}
    del _L1_attn_all

    def _L1_ffn_setup():
        import jax, jax.numpy as jnp
        import numpy as np
        B, S, D = (8, 1024, 128)
        H = 512
        O = 128
        E = 8
        TOP_K = 1
        key = jax.random.key(seed)
        ks = jax.random.split(key, 8)
        sc = 0.02
        return {'x': jax.random.normal(ks[0], (B, S, D), dtype=jnp.float32), 'Wr': jax.random.normal(ks[1], (D, E), dtype=jnp.float32) * sc, 'br': jnp.zeros((E,), dtype=jnp.float32), 'W1': jax.random.normal(ks[2], (E, D, H), dtype=jnp.float32) * sc, 'b1': jnp.zeros((E, H), dtype=jnp.float32), 'W2': jax.random.normal(ks[3], (E, H, O), dtype=jnp.float32) * sc, 'b2': jnp.zeros((E, O), dtype=jnp.float32)}
    _L1_ffn_all = _L1_ffn_setup()
    _L1_ffn_in = {k: v for k, v in _L1_ffn_all.items() if k in ('Wr', 'br', 'W1', 'b1', 'W2', 'b2')}
    del _L1_ffn_all
    return {'x': x, 'L0_tok_weight': _L0_tok_in['weight'], 'L0_tok_bias': _L0_tok_in['bias'], 'L0_attn_Wq': _L0_attn_in['Wq'], 'L0_attn_bq': _L0_attn_in['bq'], 'L0_attn_Wk': _L0_attn_in['Wk'], 'L0_attn_bk': _L0_attn_in['bk'], 'L0_attn_Wv': _L0_attn_in['Wv'], 'L0_attn_bv': _L0_attn_in['bv'], 'L0_attn_gamma': _L0_attn_in['gamma'], 'L0_attn_beta': _L0_attn_in['beta'], 'L0_ffn_Wr': _L0_ffn_in['Wr'], 'L0_ffn_W1': _L0_ffn_in['W1'], 'L0_ffn_b1': _L0_ffn_in['b1'], 'L0_ffn_W2': _L0_ffn_in['W2'], 'L0_ffn_b2': _L0_ffn_in['b2'], 'L1_attn_Wq': _L1_attn_in['Wq'], 'L1_attn_bq': _L1_attn_in['bq'], 'L1_attn_Wk': _L1_attn_in['Wk'], 'L1_attn_bk': _L1_attn_in['bk'], 'L1_attn_Wv': _L1_attn_in['Wv'], 'L1_attn_bv': _L1_attn_in['bv'], 'L1_attn_Wo': _L1_attn_in['Wo'], 'L1_attn_bo': _L1_attn_in['bo'], 'L1_ffn_Wr': _L1_ffn_in['Wr'], 'L1_ffn_br': _L1_ffn_in['br'], 'L1_ffn_W1': _L1_ffn_in['W1'], 'L1_ffn_b1': _L1_ffn_in['b1'], 'L1_ffn_W2': _L1_ffn_in['W2'], 'L1_ffn_b2': _L1_ffn_in['b2']}

def reference(x, L0_tok_weight, L0_tok_bias, L0_attn_Wq, L0_attn_bq, L0_attn_Wk, L0_attn_bk, L0_attn_Wv, L0_attn_bv, L0_attn_gamma, L0_attn_beta, L0_ffn_Wr, L0_ffn_W1, L0_ffn_b1, L0_ffn_W2, L0_ffn_b2, L1_attn_Wq, L1_attn_bq, L1_attn_Wk, L1_attn_bk, L1_attn_Wv, L1_attn_bv, L1_attn_Wo, L1_attn_bo, L1_ffn_Wr, L1_ffn_br, L1_ffn_W1, L1_ffn_b1, L1_ffn_W2, L1_ffn_b2):
    import jax
    import jax.numpy as jnp

    def _L0_tok_ref(x, weight, bias):
        import jax, jax.numpy as jnp
        import numpy as np
        from jax import lax
        STRIDE = 1
        PADDING = 4
        out = lax.conv_general_dilated(x, weight, window_strides=(STRIDE,), padding=[(PADDING, PADDING)], dimension_numbers=('NCH', 'OIH', 'NCH'))
        out = out + bias[None, :, None]
        return jnp.transpose(out, (0, 2, 1))

    def _L0_attn_ref(x, Wq, bq, Wk, bk, Wv, bv, gamma, beta):
        import jax, jax.numpy as jnp
        import numpy as np
        B, S, D_MODEL, D_ATT = (4, 1024, 128, 64)
        EPS = 1e-05
        q = jnp.einsum('bsd,de->bse', x, Wq) + bq
        k = jnp.einsum('bsd,de->bse', x, Wk) + bk
        v = jnp.einsum('bsd,de->bse', x, Wv) + bv
        scores = jnp.einsum('bqe,bke->bqk', q, k)
        seq = x.shape[1]
        causal = jnp.tril(jnp.ones((seq, seq), dtype=bool))
        scores = jnp.where(causal, scores, -jnp.inf)
        attn = jax.nn.softmax(scores, axis=-1)
        o = jnp.einsum('bqk,bkd->bqd', attn, v)
        y = x + o
        mu = jnp.mean(y, axis=-1, keepdims=True)
        var = jnp.mean(jnp.square(y - mu), axis=-1, keepdims=True)
        return (y - mu) * jax.lax.rsqrt(var + EPS) * gamma + beta

    def _L0_ffn_ref(x, Wr, W1, b1, W2, b2):
        import jax, jax.numpy as jnp
        import numpy as np
        B, T, D = (4, 2048, 128)
        E, F, CAP = (8, 512, 1024)
        Bb, Tt, Dd = x.shape
        N = Bb * Tt
        C = min(CAP, N)
        x_flat = x.reshape(N, Dd)
        logits = x_flat @ Wr
        probs = jax.nn.softmax(logits, axis=0)
        vals, idx = jax.lax.top_k(probs.T, C)
        selected = x_flat[idx]
        h = jax.nn.gelu(jnp.einsum('ecd,edf->ecf', selected, W1) + b1[:, None, :], approximate=False)
        out_e = jnp.einsum('ecf,efd->ecd', h, W2) + b2[:, None, :]
        weighted = vals[..., None] * out_e
        output = jnp.zeros_like(x_flat).at[idx.reshape(-1)].add(weighted.reshape(-1, Dd))
        return output.reshape(Bb, Tt, Dd)

    def _L1_attn_ref(x, Wq, bq, Wk, bk, Wv, bv, Wo, bo):
        import jax, jax.numpy as jnp
        import numpy as np
        EMBED_DIM = 128
        NUM_HEADS = 8
        HEAD_DIM = EMBED_DIM // NUM_HEADS
        SCALE = HEAD_DIM ** (-0.5)
        B, S, D = x.shape
        H, Hd = (NUM_HEADS, HEAD_DIM)
        q = (x @ Wq + bq).reshape(B, S, H, Hd).transpose(0, 2, 1, 3)
        k = (x @ Wk + bk).reshape(B, S, H, Hd).transpose(0, 2, 1, 3)
        v = (x @ Wv + bv).reshape(B, S, H, Hd).transpose(0, 2, 1, 3)
        attn = jax.nn.sigmoid(jnp.einsum('bhqd,bhkd->bhqk', q, k) * SCALE)
        out = jnp.einsum('bhqk,bhkd->bhqd', attn, v)
        out = out.transpose(0, 2, 1, 3).reshape(B, S, D)
        return out @ Wo + bo

    def _L1_ffn_ref(x, Wr, br, W1, b1, W2, b2):
        import jax, jax.numpy as jnp
        import numpy as np
        B, S, D = (8, 1024, 128)
        H = 512
        O = 128
        E = 8
        TOP_K = 1
        b, s, d = x.shape
        xf = x.reshape(-1, d)
        router_logits = xf @ Wr + br
        topk_logits, topk_idx = jax.lax.top_k(router_logits, TOP_K)
        topk_gates = jax.nn.softmax(topk_logits, axis=1)
        out = jnp.zeros((xf.shape[0], O), dtype=x.dtype)
        for k in range(TOP_K):
            idx_k = topk_idx[:, k]
            gate_k = topk_gates[:, k:k + 1]
            for e in range(E):
                h = jax.nn.relu(xf @ W1[e] + b1[e])
                oe = h @ W2[e] + b2[e]
                mask = (idx_k == e)[:, None]
                out = out + jnp.where(mask, gate_k * oe, 0.0)
        return out.reshape(b, s, O)
    h = _L0_tok_ref(x, L0_tok_weight, L0_tok_bias)
    h = h + _L0_attn_ref(_layernorm(h, axis=-1), L0_attn_Wq, L0_attn_bq, L0_attn_Wk, L0_attn_bk, L0_attn_Wv, L0_attn_bv, L0_attn_gamma, L0_attn_beta)
    h = h + _L0_ffn_ref(_layernorm(h, axis=-1), L0_ffn_Wr, L0_ffn_W1, L0_ffn_b1, L0_ffn_W2, L0_ffn_b2)
    h = h + _L1_attn_ref(_layernorm(h, axis=-1), L1_attn_Wq, L1_attn_bq, L1_attn_Wk, L1_attn_bk, L1_attn_Wv, L1_attn_bv, L1_attn_Wo, L1_attn_bo)
    h = h + _L1_ffn_ref(_layernorm(h, axis=-1), L1_ffn_Wr, L1_ffn_br, L1_ffn_W1, L1_ffn_b1, L1_ffn_W2, L1_ffn_b2)
    return h

_drawn_inputs = setup_inputs


def setup_inputs(seed=0):
    import zlib

    import numpy as np

    out = dict(_drawn_inputs(seed))
    spreads = {'L0_attn_gamma': (1.0, 0.6),
     'L0_attn_beta': (0.0, 0.493),
     'L1_ffn_br': (0.0, 0.8),
     'L1_ffn_b1': (0.0, 0.8),
     'L1_ffn_b2': (0.0, 2.0)}
    factors = {'L0_attn_Wq': 6.088,
     'L0_attn_bq': 8.0,
     'L0_attn_Wk': 5.829,
     'L0_attn_bk': 64.0,
     'L0_attn_Wv': 4.569,
     'L0_attn_bv': 5.208,
     'L0_ffn_Wr': 64.0,
     'L0_ffn_W1': 64.0,
     'L0_ffn_b1': 64.0,
     'L0_ffn_W2': 64.0,
     'L0_ffn_b2': 64.0,
     'L1_attn_bq': 7.438,
     'L1_attn_bk': 7.828,
     'L1_attn_bo': 8.0,
     'L1_ffn_Wr': 8.0,
     'L1_ffn_W1': 8.0,
     'L1_ffn_W2': 8.0}
    for name, (base, spread) in spreads.items():
        noise = np.random.default_rng([zlib.crc32(name.encode()), seed]).standard_normal(out[name].shape)
        drawn = base * np.exp(spread * noise) if base else spread * noise
        out[name] = jnp.asarray(drawn.astype(out[name].dtype))
    for name, factor in factors.items():
        out[name] = (out[name] * factor).astype(out[name].dtype)
    return out
```

```python
from contextlib import ExitStack

import concourse.bass as bass
import concourse.mybir as mybir
import numpy as np

F32, BF16, FP16 = mybir.dt.float32, mybir.dt.bfloat16, mybir.dt.float16
I32 = mybir.dt.int32
ALU = mybir.AluOpType
ACT = mybir.ActivationFunctionType
AX = mybir.AxisListType

class Tensors:
    pass


BATCH, C_IN, SEQ = 8, 64, 750
D = 128
TAPS, PAD = 9, 4
TAP_PAIRS = (TAPS + 1) // 2
TILE = 125
TILES = SEQ // TILE
PAIRS = TILES // 2
HALF = SEQ // 2
TOKENS = BATCH * SEQ
ALL_TILES = BATCH * TILES
D_ATT = 64
LN_EPS = 1e-5
MASKED = -1e30
EXPERTS = 8
CAPACITY = 1024
CHUNKS = 16
REGION = 6144
ROW1 = 2 * D + 1
NO_TOKEN = 8191
MAX_TILES = TOKENS // 128 + EXPERTS
STEPS_OF_GROUP = 12
HEADS, HEAD_D = 8, 16
PARTS, SLOTS = 3, 6
ROW0 = D + EXPERTS
HIDDEN = 512
F_TILES = HIDDEN // 128
SLOT_TILES = CAPACITY // 128
SEARCH_BITS = 30
CHUNK_BITS, CAPACITY_BITS = CHUNKS.bit_length() - 1, CAPACITY.bit_length() - 1


def tile_layout(rows):
    return rows.rearrange("(i p) d -> p i d", p=TILE)


def constants(nc, ctx):
    T = Tensors()
    T.resid = ctx.enter_context(nc.sbuf_tensor("resid", [TILE, ALL_TILES, D], F32))
    T.ident = ctx.enter_context(nc.sbuf_tensor("ident", [128, 128], F32))
    T.ident16 = ctx.enter_context(nc.sbuf_tensor("ident16", [128, 128], BF16))
    T.minus_half = ctx.enter_context(nc.sbuf_tensor("minus_half", [128, 8], F32))
    T.expert_start = ctx.enter_context(nc.sbuf_tensor("expert_start", [128, 1], I32))
    T.partition = ctx.enter_context(nc.sbuf_tensor("partition", [128, 1], I32))
    T.chunk_of = ctx.enter_context(nc.sbuf_tensor("chunk_of", [128, 1], I32))
    T.start_of = ctx.enter_context(nc.sbuf_tensor("start_of", [128, EXPERTS], F32))
    T.steps = ctx.enter_context(nc.sbuf_tensor("steps", [128, HALF + 1], FP16))
    T.blank = ctx.enter_context(nc.sbuf_tensor("blank", [128, ROW1], F32))
    T.ends = ctx.enter_context(nc.sbuf_tensor("ends", [128, EXPERTS], F32))
    T.zeros = ctx.enter_context(nc.sbuf_tensor("zeros", [128, 128], F32))
    return T


def prepare(nc, T):
    with ExitStack() as ctx:
        filled = ctx.enter_context(nc.semaphore("filled"))
        made = ctx.enter_context(nc.semaphore("identities_made"))
        block = ctx.enter_context(nc.Block())

        @block.gpsimd
        def _(pool):
            pool.memset(T.zeros[:], 0.0).then_inc(filled, 1)
            pool.memset(T.minus_half[:], -0.5).then_inc(made, 1)
            pool.wait_ge(filled, 1)
            for m in (T.ident, T.ident16):
                pool.affine_select(out=m[:], in_=T.zeros[:], compare_op=ALU.not_equal, fill=1.0, base=0,
                                   pattern=[[-1, 128]], channel_multiplier=1).then_inc(made, 1)
            pool.iota(T.partition[:], pattern=[[0, 1]], base=0, channel_multiplier=1).then_inc(made, 1)
            pool.wait_ge(made, 4)

        @block.vector
        def _(dve):
            dve.wait_ge(made, 4)
            dve.tensor_scalar(T.expert_start[:], T.partition[:], CHUNK_BITS, CAPACITY_BITS,
                              ALU.logical_shift_right, ALU.logical_shift_left)
            dve.tensor_scalar(T.chunk_of[:], T.partition[:], CHUNKS - 1, None, ALU.bitwise_and)
            dve.drain()


def conv_and_causal_attention(nc, T, x, conv_w, conv_b, wq, bq, wk, bk, wv, bv, gamma, beta, wr,
                              h2_rows, x2_rows, logits_rows):
    with ExitStack() as ctx:
        def sb(name, shape, dt=F32):
            return ctx.enter_context(nc.sbuf_tensor(name, shape, dt))

        def sem(name):
            return ctx.enter_context(nc.semaphore(name))

        LOADS = 12

        xpad = sb("xpad", [128, SEQ + 2 * PAD])
        w_conv = sb("w_conv", [128, TAP_PAIRS, D])
        b_conv = sb("b_conv", [TILE, D])
        w_q = sb("w_q", [D, D_ATT])
        w_k = sb("w_k", [D, D_ATT])
        w_v = sb("w_v", [D, D])
        b_q = sb("b_q", [D_ATT, 1])
        b_k = sb("b_k", [D_ATT, 1])
        b_v = sb("b_v", [TILE, D])
        gam = sb("gam", [TILE, D])
        bet = sb("bet", [TILE, D])
        w_r = sb("w_r", [D, 8])
        causal = sb("causal", [128, TILE], BF16)

        xn = sb("xn", [TILE, TILES, D])
        xn_kept = sb("xn_kept", [TILE, 2, TILES, D])
        xnT = sb("xnT", [D, SEQ])
        qT = sb("qT", [D_ATT, SEQ])
        kT = sb("kT", [D_ATT, SEQ])
        v = sb("v", [TILE, 2, TILES, D])
        probs = sb("probs", [TILE, TILES, TILE])
        probsT = sb("probsT", [TILE, TILES, TILE])
        neg_max = sb("neg_max", [TILE, TILES])
        row_sum = sb("row_sum", [TILE, TILES])
        row_inv = sb("row_inv", [TILE, TILES])
        y = sb("y", [TILE, TILES, D])
        z = sb("z", [TILE, 2, D])
        hb = sb("hb", [TILE, TILES, D])
        x2 = sb("x2", [TILE, TILES, D])
        x2T = sb("x2T", [D, SEQ])
        logits = sb("logits", [8, 2, HALF])
        st1 = sb("st1", [TILE, TILES, 6])
        mv1 = sb("mv1", [TILE, TILES, 2])
        ve1 = sb("ve1", [TILE, TILES])
        rs1 = sb("rs1", [TILE, TILES])
        st2 = sb("st2", [TILE, TILES, 6])
        mv2 = sb("mv2", [TILE, TILES, 2])
        ve2 = sb("ve2", [TILE, TILES])
        rs2 = sb("rs2", [TILE, TILES])
        st3 = sb("st3", [TILE, TILES, 6])
        mv3 = sb("mv3", [TILE, TILES, 2])
        ve3 = sb("ve3", [TILE, TILES])
        rs3 = sb("rs3", [TILE, TILES])

        ps = ctx.enter_context(nc.psum_tensor("ps", [128, 8, 512], F32))
        ps_conv = ps[0:TILE, 0, 0:2 * D].rearrange("p (s d) -> p s d", d=D)
        ps_scores = ps[:, 1:3, :].rearrange("p a (s d) -> p (a s) d", d=128)
        ps_probsT = ps[:, 3:5, :].rearrange("p a (s d) -> p (a s) d", d=128)
        ps_out = ps[0:TILE, 5, 0:D]
        ps_x2T = ps[:, 6, 0:256].rearrange("p (s d) -> p s d", d=128)
        ps_xnT = ps[:, 7, 0:256].rearrange("p (s d) -> p s d", d=128)
        ps_proj = ps[:, 6:8, 0:HALF]

        weights_loaded = sem("weights_loaded")
        pads_zero = sem("pads_zero")
        mask_made = sem("mask_made")
        x_loaded = sem("x_loaded")
        conv_done = sem("conv_done")
        h1_ready = sem("h1_ready")
        ve1_done = sem("ve1_done")
        rs1_done = sem("rs1_done")
        xn_ready = sem("xn_ready")
        xn_kept_ready = sem("xn_kept_ready")
        xnT_done = sem("xnT_done")
        xnT_ready = sem("xnT_ready")
        q_done, k_done, v_done = sem("q_done"), sem("k_done"), sem("v_done")
        q_ready, k_ready, v_ready = sem("q_ready"), sem("k_ready"), sem("v_ready")
        scores_done = sem("scores_done")
        max_done = sem("max_done")
        probs_ready = sem("probs_ready")
        probsT_done = sem("probsT_done")
        probsT_ready = sem("probsT_ready")
        pv_done = sem("pv_done")
        inv_done = sem("inv_done")
        y_ready = sem("y_ready")
        ve2_done, rs2_done = sem("ve2_done"), sem("rs2_done")
        z_done = sem("z_done")
        hb_ready = sem("hb_ready")
        h2_ready = sem("h2_ready")
        ve3_done, rs3_done = sem("ve3_done"), sem("rs3_done")
        x2_ready = sem("x2_ready")
        x2T_done, x2T_ready = sem("x2T_done"), sem("x2T_ready")
        logits_done, logits_ready = sem("logits_done"), sem("logits_ready")
        h2_stored, x2_stored, logits_stored = sem("h2_stored"), sem("x2_stored"), sem("logits_stored")

        block = ctx.enter_context(nc.Block())

        def wait(eng, semaphore, value):
            if not isinstance(value, int) or value > 0:
                eng.wait_ge(semaphore, value)

        def capped(value, most):
            return min(value, most) if isinstance(value, int) else value

        def x_rows(b):
            return x[bass.ds(b, 1)].rearrange("a c t -> (a c) t")

        def load_x(sp, src):
            sp.dma_start(xpad[0:C_IN, PAD:PAD + SEQ], src).then_inc(x_loaded, 16)
            sp.dma_start(xpad[C_IN:128, PAD - 1:PAD - 1 + SEQ], src).then_inc(x_loaded, 16)

        @block.sync
        def _(sp):
            loads = [(b_conv[:], conv_b.partition_broadcast(TILE)), (w_q[:], wq), (w_k[:], wk), (w_v[:], wv),
                     (b_q[:], bq.rearrange("(p a) -> p a", a=1)), (b_k[:], bk.rearrange("(p a) -> p a", a=1)),
                     (b_v[:], bv.partition_broadcast(TILE)), (gam[:], gamma.partition_broadcast(TILE)),
                     (bet[:], beta.partition_broadcast(TILE)), (w_r[:], wr)]
            sp.wait_ge(pads_zero, 1)
            for n, (dst, src) in enumerate(
                    [(w_conv[:, 0:4, :], conv_w[0:512, :].rearrange("(m p) d -> p m d", p=128)),
                     (w_conv[0:64, 4, :], conv_w[512:576, :])] + loads):
                if n == 2:
                    load_x(sp, x_rows(0))
                sp.dma_start(dst, src).then_inc(weights_loaded, 16)

            def step(b, has_make, has_attend, has_close):
                if has_make:
                    if not (isinstance(b, int) and b == BATCH - 2):
                        src = x_rows(b + 2)
                        sp.wait_ge(conv_done, PAIRS * (b + 2))
                        load_x(sp, src)
                if has_close:
                    c = b - 1
                    row, tile = sp.snap(SEQ * c), sp.snap(TILES * c)
                    sp.wait_ge(x2_ready, TILES * (c + 1))
                    sp.dma_start(tile_layout(x2_rows[bass.ds(row, SEQ), :]), x2[:]).then_inc(x2_stored, 16)
                    sp.dma_start(tile_layout(h2_rows[bass.ds(row, SEQ), :]),
                                 T.resid[:, bass.ds(tile, TILES), :]).then_inc(h2_stored, 16)

            step(-1, True, False, False)
            step(0, True, True, False)
            step(1, True, True, True)
            with sp.Fori(2, BATCH - 2) as b:
                step(b, True, True, True)
            step(BATCH - 2, True, True, True)
            step(BATCH - 1, False, True, True)
            step(BATCH, False, False, True)
            sp.wait_ge(x2_stored, 16 * BATCH)
            sp.wait_ge(h2_stored, 16 * BATCH)
            sp.wait_ge(logits_stored, 16 * BATCH)

        @block.tensor
        def _(pe):
            def conv(b, g):
                wait(pe, h1_ready, PAIRS * b + g)
                for i in (2 * g, 2 * g + 1):
                    for m in range(TAP_PAIRS):
                        rows = 128 if m < TAP_PAIRS - 1 else C_IN
                        at = TILE * i + 2 * m
                        mm = pe.matmul(ps_conv[:, i % 2, :], xpad[0:rows, at:at + TILE], w_conv[0:rows, m, :],
                                       start=(m == 0), stop=(m == TAP_PAIRS - 1))
                mm.then_inc(conv_done, 1)

            def turn_xn(b, g):
                if g == 0:
                    wait(pe, k_ready, b)
                wait(pe, xnT_ready, PAIRS * b + g)
                pe.wait_ge(xn_ready, TILES * b + 2 * g + 2)
                for i in (2 * g, 2 * g + 1):
                    mm = pe.transpose(ps_xnT[:, i % 2, 0:TILE], xn[:, i, :], T.ident[0:TILE, 0:TILE])
                mm.then_inc(xnT_done, 1)

            def make(b, i):
                if i == 0:
                    pe.wait_ge(x_loaded, 32 * (b + 1))
                if i < PAIRS:
                    conv(b, i)
                if 2 <= i <= 4:
                    turn_xn(b, i - 2)

            def project(b):
                pe.wait_ge(xnT_ready, PAIRS * (b + 1))
                for h in range(2):
                    mm = pe.matmul(ps_proj[0:D_ATT, h, :], w_q[:], xnT[:, h * HALF:(h + 1) * HALF], start=True, stop=True)
                mm.then_inc(q_done, 1)
                wait(pe, probs_ready, TILES * b)
                for i in range(TILES):
                    mm = pe.matmul(ps_scores[0:TILE, i, :], xnT[:, i * TILE:(i + 1) * TILE], w_v[:], start=True, stop=True)
                mm.then_inc(v_done, 1)
                pe.wait_ge(q_ready, b + 1)
                for h in range(2):
                    mm = pe.matmul(ps_proj[0:D_ATT, h, :], w_k[:], xnT[:, h * HALF:(h + 1) * HALF], start=True, stop=True)
                mm.then_inc(k_done, 1)

            def scores(b, i):
                n = TILES * b + i
                if i == 0:
                    pe.wait_ge(q_ready, b + 1)
                    pe.wait_ge(k_ready, b + 1)
                    pe.wait_ge(v_ready, b + 1)
                wait(pe, probs_ready, n)
                for lo, hi in ((0, min(4, i + 1)), (4, i + 1)):
                    if lo >= hi:
                        continue
                    pe.matmul(ps_scores[0:TILE, lo:hi, 0:TILE], qT[:, i * TILE:(i + 1) * TILE],
                              kT[:, lo * TILE:hi * TILE], start=True, stop=(hi <= i))
                pe.matmul(ps_scores[0:TILE, i, 0:TILE], T.ident16[0:TILE, 0:TILE], causal[0:TILE, :],
                          start=False, stop=True).then_inc(scores_done, 1)

            def turn_probs(b, i):
                n = TILES * b + i
                pe.wait_ge(probs_ready, n + 1)
                wait(pe, probsT_ready, n)
                for j in range(i + 1):
                    mm = pe.transpose(ps_probsT[0:TILE, j, 0:TILE], probs[:, j, :], T.ident[0:TILE, 0:TILE])
                mm.then_inc(probsT_done, 1)

            def values(b, i):
                n = TILES * b + i
                pe.wait_ge(probsT_ready, n + 1)
                wait(pe, y_ready, n)
                for j in range(i + 1):
                    mm = pe.matmul(ps_out, probsT[:, j, :],
                                   v[:, bass.ds(b % 2, 1), j, :].rearrange("p a d -> p (a d)"),
                                   start=(j == 0), stop=(j == i))
                mm.then_inc(pv_done, 1)

            def close(b, i):
                if i < 3:
                    return
                g = i - 3
                if g == 0:
                    pe.wait_ge(k_ready, capped(b + 2, BATCH))
                    wait(pe, logits_ready, b)
                pe.wait_ge(x2_ready, TILES * b + 2 * g + 2)
                wait(pe, x2T_ready, PAIRS * b + g)
                for t in (2 * g, 2 * g + 1):
                    mm = pe.transpose(ps_x2T[:, t % 2, 0:TILE], x2[:, t, :], T.ident[0:TILE, 0:TILE])
                mm.then_inc(x2T_done, 1)

            def router(b):
                pe.wait_ge(xnT_ready, capped(PAIRS * (b + 2), PAIRS * BATCH))
                pe.wait_ge(x2T_ready, PAIRS * (b + 1))
                for h in range(2):
                    mm = pe.matmul(ps_proj[0:8, h, :], w_r[:], x2T[:, h * HALF:(h + 1) * HALF], start=True, stop=True)
                mm.then_inc(logits_done, 1)

            def step(b, has_make, has_attend, has_close):
                for i in range(TILES):
                    if has_attend:
                        scores(b, i)
                        if i > 0:
                            values(b, i - 1)
                    if has_make:
                        make(b + 1, i)
                    if has_close:
                        close(b - 1, i)
                    if has_attend:
                        turn_probs(b, i)
                if has_close:
                    router(b - 1)
                if has_make:
                    if has_close:
                        pe.wait_ge(logits_ready, b)
                    project(b + 1)
                if has_attend:
                    values(b, TILES - 1)

            pe.wait_ge(weights_loaded, 16 * LOADS)
            pe.wait_ge(mask_made, 2)
            step(-1, True, False, False)
            step(0, True, True, False)
            step(1, True, True, True)
            with pe.Fori(2, BATCH - 1) as b:
                step(b, True, True, True)
            step(BATCH - 1, False, True, True)
            step(BATCH, False, False, True)

        @block.scalar
        def _(act):
            def move_pair(done, count, to, bank, g, ready):
                act.wait_ge(done, count)
                act.copy(to[:, 2 * g * TILE:(2 * g + 2) * TILE].rearrange("p (s t) -> p s t", s=2), bank[:, :, 0:TILE])\
                   .then_inc(ready, 1)

            def step(b, has_make, has_attend, has_close):
                for i in range(TILES):
                    if has_attend:
                        n = TILES * b + i
                        act.wait_ge(max_done, n + 1)
                        act.activation(probs[:, 0:i + 1, :], ps_scores[0:TILE, 0:i + 1, 0:TILE], ACT.Exp,
                                       bias=neg_max[:, i:i + 1], accum_out=row_sum[:, i:i + 1]).then_inc(probs_ready, 1)
                    if has_make and 2 <= i <= 4:
                        move_pair(xnT_done, PAIRS * (b + 1) + i - 1, xnT, ps_xnT, i - 2, xnT_ready)
                    if has_close and i >= 3:
                        move_pair(x2T_done, PAIRS * (b - 1) + i - 2, x2T, ps_x2T, i - 3, x2T_ready)
                    if has_attend:
                        act.wait_ge(probsT_done, n + 1)
                        act.copy(probsT[:, 0:i + 1, :], ps_probsT[0:TILE, 0:i + 1, 0:TILE]).then_inc(probsT_ready, 1)
                if has_close:
                    act.wait_ge(logits_done, b)
                    wait(act, logits_stored, 16 * (b - 1))
                    act.copy(logits[:], ps_proj[0:8]).then_inc(logits_ready, 1)
                    act.wait_ge(logits_ready, b)
                    act.dma_start(logits_rows[:, bass.ds(SEQ * (b - 1), SEQ)],
                                  logits[:].rearrange("e a t -> e (a t)")).then_inc(logits_stored, 16)
                if has_make:
                    act.wait_ge(q_done, b + 2)
                    act.activation(qT[:].rearrange("p (a t) -> p a t", a=2), ps_proj[0:D_ATT], ACT.Identity,
                                   bias=b_q[:, 0:1]).then_inc(q_ready, 1)
                    act.wait_ge(k_done, b + 2)
                    act.activation(kT[:].rearrange("p (a t) -> p a t", a=2), ps_proj[0:D_ATT], ACT.Identity,
                                   bias=b_k[:, 0:1]).then_inc(k_ready, 1)

            act.wait_ge(weights_loaded, 16 * LOADS)
            step(-1, True, False, False)
            step(0, True, True, False)
            step(1, True, True, True)
            with act.Fori(2, BATCH - 1) as b:
                step(b, True, True, True)
            step(BATCH - 1, False, True, True)
            step(BATCH, False, False, True)

        @block.gpsimd
        def _(pool):
            pool.memset(xpad[:], 0.0).then_inc(pads_zero, 1)
            pool.memset(causal[:], 0.0).then_inc(mask_made, 1)
            pool.wait_ge(mask_made, 1)
            pool.affine_select(out=causal[:], in_=causal[:], compare_op=ALU.is_ge, fill=MASKED, base=0,
                               pattern=[[-1, TILE]], channel_multiplier=1).then_inc(mask_made, 1)
            pool.wait_ge(weights_loaded, 16 * LOADS)

            def rsqrt(var_done, count, rs, ve, g, done):
                pool.wait_ge(var_done, count)
                pool.tensor_tensor(rs[:, 2 * g:2 * g + 2], ve[:, 2 * g:2 * g + 2],
                                   T.minus_half[0:TILE, 0:2], ALU.pow).then_inc(done, 1)

            def make(b, i):
                if 1 <= i <= 3:
                    g = i - 1
                    rsqrt(ve1_done, 3 * b + g + 1, rs1, ve1, g, rs1_done)
                if i == 4:
                    pool.wait_ge(xn_ready, TILES * (b + 1))
                    pool.tensor_copy(xn_kept[:, bass.ds(b % 2, 1), :, :].rearrange("p a i d -> p (a i) d"), xn[:])\
                        .then_inc(xn_kept_ready, 1)

            def close(b, i):
                if i < 3:
                    rsqrt(ve2_done, 3 * b + i + 1, rs2, ve2, i, rs2_done)
                if i == 0:
                    wait(pool, h2_ready, TILES * b)
                    pool.tensor_tensor(hb[:], T.resid[:, bass.ds(TILES * b, TILES), :],
                                       bet[:, :].unsqueeze(1).to_broadcast([TILE, TILES, D]), ALU.add).then_inc(hb_ready, 1)
                if 1 <= i <= 3:
                    g = i - 1
                    rsqrt(ve3_done, 3 * b + g + 1, rs3, ve3, g, rs3_done)

            def step(b, has_make, has_attend, has_close):
                for i in range(TILES):
                    if has_close:
                        close(b - 1, i)
                    if has_make:
                        make(b + 1, i)

            step(-1, True, False, False)
            step(0, True, True, False)
            step(1, True, True, True)
            with pool.Fori(2, BATCH - 1) as b:
                step(b, True, True, True)
            step(BATCH - 1, False, True, True)
            step(BATCH, False, False, True)

        @block.vector
        def _(dve):
            def resid_tile(n):
                return T.resid[:, bass.ds(n, 1), :].rearrange("p a d -> p (a d)")

            def stats(src_of, g, st, mv, ve, ve_done):
                dve.drain()
                for t in (2 * g, 2 * g + 1):
                    dve.bn_stats(st[:, t, :], src_of(t))
                dve.drain()
                for t in (2 * g, 2 * g + 1):
                    dve.bn_aggr(mv[:, t, :], st[:, t, :])
                dve.drain()
                dve.tensor_scalar(ve[:, 2 * g:2 * g + 2], mv[:, 2 * g:2 * g + 2, 1], LN_EPS, None, ALU.add)\
                    .then_inc(ve_done, 1)

            def normalize(to, mv, rs, rs_done, ready, b, g):
                dve.wait_ge(rs_done, PAIRS * b + g + 1)
                for t in (2 * g, 2 * g + 1):
                    dve.tensor_scalar(to[:, t, :], resid_tile(TILES * b + t), mv[:, t, 0:1], rs[:, t:t + 1],
                                      ALU.subtract, ALU.mult).then_inc(ready, 1)

            def make(b, i):
                if i < 3:
                    dve.wait_ge(conv_done, PAIRS * b + i + 1)
                    dve.tensor_tensor(T.resid[:, bass.ds(TILES * b + 2 * i, 2), :], ps_conv,
                                      b_conv[:, :].unsqueeze(1).to_broadcast([TILE, 2, D]), ALU.add).then_inc(h1_ready, 1)
                    stats(lambda t: resid_tile(TILES * b + t), i, st1, mv1, ve1, ve1_done)
                if 1 <= i <= 3:
                    g = i - 1
                    if g == 0:
                        wait(dve, xn_kept_ready, b)
                        wait(dve, xnT_done, PAIRS * b)
                    normalize(xn, mv1, rs1, rs1_done, xn_ready, b, g)

            def project(b):
                dve.wait_ge(v_done, b + 1)
                wait(dve, pv_done, TILES * (b - 1))
                dve.tensor_tensor(v[:, bass.ds(b % 2, 1), :, :].rearrange("p a i d -> p (a i) d"), ps_scores[0:TILE, 0:TILES, :],
                                  b_v[:, :].unsqueeze(1).to_broadcast([TILE, TILES, D]), ALU.add).then_inc(v_ready, 1)

            def negmax(b, i):
                dve.wait_ge(scores_done, TILES * b + i + 1)
                dve.tensor_reduce(neg_max[:, i:i + 1], ps_scores[0:TILE, 0:i + 1, 0:TILE], AX.XY, ALU.max, negate=True)\
                    .then_inc(max_done, 1)

            def finish(b, i):
                n = TILES * b + i
                dve.wait_ge(probs_ready, n + 1)
                dve.reciprocal(row_inv[:, i:i + 1], row_sum[:, i:i + 1]).then_inc(inv_done, 1)
                if i == 0:
                    dve.wait_ge(xn_kept_ready, b + 1)
                wait(dve, z_done, n - TILES + 1)
                dve.wait_ge(pv_done, n + 1)
                dve.wait_ge(inv_done, n + 1)
                dve.scalar_tensor_tensor(y[:, i, :], ps_out, row_inv[:, i:i + 1],
                                         xn_kept[:, bass.ds(b % 2, 1), i, :].rearrange("p a d -> p (a d)"),
                                         ALU.mult, ALU.add).then_inc(y_ready, 1)

            def close(b, i):
                if i < 3:
                    stats(lambda t: y[:, t, :], i, st2, mv2, ve2, ve2_done)
                if 1 <= i <= 3:
                    g = i - 1
                    for t in (2 * g, 2 * g + 1):
                        dve.scalar_tensor_tensor(z[:, t % 2, :], y[:, t, :], mv2[:, t, 0:1], gam[:], ALU.subtract, ALU.mult)\
                            .then_inc(z_done, 1)
                    dve.wait_ge(rs2_done, 3 * b + g + 1)
                    dve.wait_ge(hb_ready, b + 1)
                    for t in (2 * g, 2 * g + 1):
                        dve.wait_ge(z_done, TILES * b + t + 1)
                        dve.scalar_tensor_tensor(resid_tile(TILES * b + t), z[:, t % 2, :], rs2[:, t:t + 1], hb[:, t, :],
                                                 ALU.mult, ALU.add).then_inc(h2_ready, 1)
                    stats(lambda t: resid_tile(TILES * b + t), g, st3, mv3, ve3, ve3_done)
                if 2 <= i <= 4:
                    g = i - 2
                    if g == 0:
                        wait(dve, x2_stored, 16 * b)
                        wait(dve, x2T_done, PAIRS * b)
                    normalize(x2, mv3, rs3, rs3_done, x2_ready, b, g)

            def step(b, has_make, has_attend, has_close):
                for i in range(TILES):
                    if has_attend:
                        negmax(b, i)
                    if has_close:
                        close(b - 1, i)
                    if has_attend and i > 0:
                        finish(b, i - 1)
                    if has_make:
                        make(b + 1, i)
                if has_attend:
                    if not has_make:
                        finish(b, TILES - 1)
                if has_make:
                    project(b + 1)
                    if has_attend:
                        finish(b, TILES - 1)

            dve.wait_ge(weights_loaded, 16 * LOADS)
            step(-1, True, False, False)
            step(0, True, True, False)
            step(1, True, True, True)
            with dve.Fori(2, BATCH - 1) as b:
                step(b, True, True, True)
            step(BATCH - 1, False, True, True)
            step(BATCH, False, False, True)


def select_tokens(nc, T, logits_rows, x2_rows):
    with ExitStack() as ctx:
        def sb(name, shape, dt=F32):
            return ctx.enter_context(nc.sbuf_tensor(name, shape, dt))

        def sem(name):
            return ctx.enter_context(nc.semaphore(name))

        p = sb("p_tokens", [128, HALF])
        junk = sb("p_junk", [128, HALF], BF16)
        own_max = sb("own_max", [128, 1])
        max_row = sb("max_row", [1, EXPERTS])
        max_spread = sb("max_spread", [1, EXPERTS, CHUNKS])
        neg_max = sb("p_neg_max", [128, 1])
        part_sum = sb("part_sum", [128, 1])
        inv_sum = sb("inv_sum", [128, 1])
        ones = sb("p_ones", [128, 128])
        same = sb("same_expert", [128, EXPERTS, CHUNKS])
        same16 = sb("same_expert16", [128, 128], FP16)
        before = sb("chunks_before", [128, EXPERTS, CHUNKS])
        step_back = sb("step_back", [128, 128])
        ones_i = sb("ones_i", [128, SEARCH_BITS], I32)
        shifts = sb("shifts", [128, SEARCH_BITS], I32)
        bits = sb("bits", [128, SEARCH_BITS + 1], I32)
        found = sb("found", [128, 1], I32)
        trial = sb("trial", [128, 1], I32)
        trial_next = sb("trial_next", [128, 1], I32)
        enough = sb("enough", [128, 1], I32)
        count16 = sb("count16", [128, 1], FP16)
        above = sb("above", [128, HALF])
        equal = sb("equal", [128, HALF])
        n_above = sb("n_above", [128, 1])
        limit = sb("limit", [128, 1])
        need = sb("need", [128, 1])
        zeros = sb("p_zeros", [128, HALF])
        rank = sb("rank", [128, HALF])
        chosen = sb("chosen", [128, HALF])
        table = sb("p_table", [128, HALF + 1])
        expert_start_f = sb("expert_start_f", [128, 1])
        starts = sb("starts", [128, 1])
        slot_base = sb("slot_base", [128, EXPERTS], I32)
        slot_base_f = sb("slot_base_f", [128, EXPERTS])
        by_token = sb("by_token", [TILE, CHUNKS, 3, EXPERTS])

        ps = ctx.enter_context(nc.psum_tensor("p_ps", [128, 8, 512], F32))

        loaded = sem("p_loaded")
        consts = sem("p_consts")
        d = sem("p_vector_steps")
        pe_s = sem("p_products")
        exp_done = sem("p_exp_done")
        neg_max_ready = sem("p_neg_max_ready")
        counted = sem("counted")
        summed = sem("summed")
        stored = sem("p_stored")
        block = ctx.enter_context(nc.Block())

        @block.sync
        def _(sp):
            sp.dma_start(p[:], logits_rows.rearrange("e (c j) -> (e c) j", c=CHUNKS)).then_inc(loaded, 16)
            sp.wait_ge(d, 4)
            with nc.allow_non_contiguous_dma(reason="8 probabilities beside each token's features"):
                sp.dma_start(x2_rows[:, D:ROW0].rearrange("(i q) e -> q i e", q=TILE),
                             by_token[:].rearrange("q c k e -> q (c k) e")).then_inc(stored, 16)
            sp.wait_ge(stored, 16)

        @block.gpsimd
        def _(pool):
            pool.memset(ones[:], 1.0).then_inc(consts, 1)
            pool.memset(zeros[:], 0.0).then_inc(consts, 1)
            pool.memset(ones_i[:], 1).then_inc(consts, 1)
            pool.iota(shifts[:], pattern=[[-1, SEARCH_BITS]], base=SEARCH_BITS - 1, channel_multiplier=0).then_inc(consts, 1)
            pool.iota(slot_base[:], pattern=[[CAPACITY, EXPERTS]], base=0, channel_multiplier=0).then_inc(consts, 1)
            pool.wait_ge(consts, 5)
            blocks = ones[:].rearrange("p (e c) -> p e c", e=EXPERTS)
            pool.affine_select(out=same[:], in_=blocks, compare_op=ALU.is_ge, fill=0.0, base=0,
                               pattern=[[-CHUNKS, EXPERTS], [0, CHUNKS]], channel_multiplier=1).then_inc(consts, 1)
            pool.wait_ge(consts, 6)
            pool.affine_select(out=same[:], in_=same[:], compare_op=ALU.is_ge, fill=0.0, base=CHUNKS - 1,
                               pattern=[[CHUNKS, EXPERTS], [0, CHUNKS]], channel_multiplier=-1).then_inc(consts, 1)
            pool.wait_ge(consts, 7)
            pool.affine_select(out=before[:], in_=same[:], compare_op=ALU.is_gt, fill=0.0, base=0,
                               pattern=[[CHUNKS, EXPERTS], [1, CHUNKS]], channel_multiplier=-1).then_inc(consts, 1)
            pool.tensor_copy(same16[:], same[:].rearrange("p e c -> p (e c)")).then_inc(consts, 1)
            pool.affine_select(out=step_back[:], in_=T.ident[:], compare_op=ALU.not_equal, fill=-1.0, base=1,
                               pattern=[[-1, 128]], channel_multiplier=1).then_inc(consts, 1)

        @block.tensor
        def _(pe):
            pe.wait_ge(d, 1)
            pe.transpose(ps[0:1, 0, 0:128], own_max[:], T.ident[:]).then_inc(pe_s, 1)
            pe.wait_ge(consts, 10)
            pe.wait_ge(d, 2)
            pe.matmul(ps[:, 1, 0:1], max_spread[:].rearrange("a e c -> a (e c)"), ones[0:1, 0:1],
                      start=True, stop=True).then_inc(pe_s, 1)
            pe.wait_ge(exp_done, 1)
            pe.matmul(ps[:, 2, 0:1], same[:].rearrange("p e c -> p (e c)"), part_sum[:], start=True, stop=True).then_inc(pe_s, 1)
            pe.wait_ge(d, 3)
            for k in range(3):
                mm = pe.transpose(ps[0:TILE, 3, 128 * k:128 * k + 128], p[:, k * TILE:(k + 1) * TILE], T.ident[:])
            mm.then_inc(pe_s, 1)
            with pe.Fori(0, SEARCH_BITS) as k:
                pe.wait_ge(counted, k + 1)
                pe.matmul(ps[:, 4, 0:1], same16[:], count16[:], start=True, stop=True).then_inc(summed, 1)
            pe.wait_ge(d, 5)
            pe.matmul(ps[:, 5, 0:1], same[:].rearrange("p e c -> p (e c)"), n_above[:], start=True, stop=True).then_inc(pe_s, 1)
            pe.wait_ge(d, 6)
            pe.matmul(ps[:, 6, 0:1], before[:].rearrange("p e c -> p (e c)"), rank[:, HALF - 1:HALF],
                      start=True, stop=True).then_inc(pe_s, 1)
            pe.wait_ge(d, 7)
            pe.matmul(ps[:, 7, 0:1], before[:].rearrange("p e c -> p (e c)"), rank[:, HALF - 1:HALF],
                      start=True, stop=True).then_inc(pe_s, 1)
            pe.wait_ge(d, 8)
            pe.matmul(ps[:, 0, 0:HALF + 1], step_back[:], table[:], start=True, stop=True).then_inc(pe_s, 1)

        @block.scalar
        def _(act):
            act.wait_ge(neg_max_ready, 1)
            act.activation(p[:], p[:], ACT.Exp, bias=neg_max[:, 0:1], accum_out=part_sum[:]).then_inc(exp_done, 1)

        @block.vector
        def _(dve):
            dve.wait_ge(loaded, 16)
            dve.tensor_reduce(own_max[:], p[:], AX.X, ALU.max).then_inc(d, 1)
            dve.wait_ge(pe_s, 1)
            dve.tensor_reduce(max_row[:], ps[0:1, 0, 0:128].rearrange("a (e c) -> a e c", e=EXPERTS), AX.X, ALU.max)
            dve.drain()
            dve.tensor_copy(max_spread[:], max_row[:, :].unsqueeze(2).to_broadcast([1, EXPERTS, CHUNKS])).then_inc(d, 1)
            dve.wait_ge(pe_s, 2)
            dve.tensor_scalar(neg_max[:], ps[:, 1, 0:1], -1.0, None, ALU.mult).then_inc(neg_max_ready, 1)
            dve.wait_ge(consts, 10)
            dve.memset(bits[:, SEARCH_BITS:], 0)
            dve.tensor_tensor(bits[:, 0:SEARCH_BITS], ones_i[:], shifts[:], ALU.logical_shift_left)
            dve.memset(found[:], 0)
            dve.tensor_copy(slot_base_f[:], slot_base[:])
            dve.wait_ge(pe_s, 3)
            dve.reciprocal(inv_sum[:], ps[:, 2, 0:1])
            dve.drain()
            dve.tensor_scalar(p[:], p[:], inv_sum[:, 0:1], None, ALU.mult).then_inc(d, 1)
            dve.tensor_copy(trial[:], bits[:, 0:1])
            dve.wait_ge(pe_s, 4)
            dve.tensor_copy(by_token[:].rearrange("q c k e -> q k e c"),
                            ps[0:TILE, 3, 0:384].rearrange("q (k e c) -> q k e c", k=3, e=EXPERTS)).then_inc(d, 1)

            with dve.Fori(0, SEARCH_BITS) as k:
                dve.drain()
                dve.tensor_scalar(junk[:], p[:], trial[:].bitcast(F32)[:, 0:1], None, ALU.is_ge, ALU.add,
                                  accum_out=count16[:]).then_inc(counted, 1)
                dve.tensor_tensor(trial_next[:], found[:], bits[:, bass.ds(k + 1, 1)], ALU.bitwise_or)
                dve.wait_ge(summed, k + 1)
                dve.tensor_scalar(enough[:], ps[:, 4, 0:1], float(CAPACITY), -1.0, ALU.is_ge, ALU.mult)
                dve.drain()
                dve.scalar_tensor_tensor(trial[:], enough[:], bits[:, bass.ds(k, 1)], trial_next[:],
                                         ALU.bitwise_and, ALU.bitwise_or)
                dve.scalar_tensor_tensor(found[:], enough[:], bits[:, bass.ds(k, 1)], found[:],
                                         ALU.bitwise_and, ALU.bitwise_or)
            dve.drain()
            least = found[:].bitcast(F32)
            dve.tensor_scalar(above[:], p[:], least[:, 0:1], None, ALU.is_gt, ALU.add, accum_out=n_above[:]).then_inc(d, 1)
            dve.tensor_scalar(equal[:], p[:], least[:, 0:1], None, ALU.is_equal)
            dve.wait_ge(pe_s, 5)
            dve.tensor_scalar(need[:], ps[:, 5, 0:1], -1.0, float(CAPACITY), ALU.mult, ALU.add)
            dve.drain()
            dve.tensor_tensor_scan(rank[:], equal[:], zeros[:], 0.0, ALU.add, ALU.add).then_inc(d, 1)
            dve.wait_ge(pe_s, 6)
            dve.scalar_tensor_tensor(limit[:], ps[:, 6, 0:1], -1.0, need[:], ALU.mult, ALU.add)
            dve.drain()
            dve.scalar_tensor_tensor(chosen[:], rank[:], limit[:, 0:1], equal[:], ALU.is_le, ALU.mult)
            dve.drain()
            dve.tensor_tensor(chosen[:], chosen[:], above[:], ALU.add)
            dve.drain()
            dve.tensor_tensor_scan(rank[:], chosen[:], zeros[:], 0.0, ALU.add, ALU.add).then_inc(d, 1)
            dve.tensor_copy(expert_start_f[:], T.expert_start[:])
            dve.tensor_copy(table[:, HALF:HALF + 1], T.chunk_of[:])
            dve.wait_ge(pe_s, 7)
            dve.drain()
            dve.tensor_tensor(starts[:], ps[:, 7, 0:1], expert_start_f[:], ALU.add)
            dve.drain()
            dve.tensor_scalar(table[:, 0:HALF], rank[:], starts[:, 0:1], None, ALU.add).then_inc(d, 1)
            dve.tensor_scalar(T.start_of[:], slot_base_f[:], -1.0, starts[:, 0:1], ALU.mult, ALU.add)
            dve.wait_ge(pe_s, 8)
            dve.tensor_copy(T.steps[:], ps[:, 0, 0:HALF + 1])
            dve.drain()


def experts_by_token_choice(nc, T, x2_rows, h2_rows, w1, b1, w2, b2):
    GROUP = 4
    GROUPS = EXPERTS * CAPACITY // (GROUP * 128)
    TURN = 4
    LOOK_AHEAD, GATHER_AHEAD = 2, 3
    with ExitStack() as ctx:
        def sb(name, shape, dt=F32):
            return ctx.enter_context(nc.sbuf_tensor(name, shape, dt))

        def sem(name):
            return ctx.enter_context(nc.semaphore(name))

        w1_sb = [sb(f"c_w1_{i}", [D, HIDDEN]) for i in range(2)]
        w2_sb = [sb(f"c_w2_{i}", [128, F_TILES, D]) for i in range(2)]
        b2_sb = [sb(f"c_b2_{i}", [128, D]) for i in range(2)]
        b1_sb = [sb(f"c_b1_{i}", [128, F_TILES]) for i in range(2)]
        slot_row = sb("slot_row", [128, CAPACITY])
        slot_col = sb("slot_col", [128, EXPERTS * SLOT_TILES])
        reached = [sb(f"reached_{i}", [128, CAPACITY], FP16) for i in range(2)]
        junk = sb("c_junk", [128, HALF], BF16)
        count = sb("c_count", [128, 2])
        ids = sb("c_ids", [128, TURN, GROUP], I32)
        ids_out = sb("c_ids_out", [128, TURN, GROUP], I32)
        xs = sb("c_xs", [128, TURN, GROUP, ROW0])
        xsT = sb("c_xsT", [D, GROUP * 128])
        hT = sb("c_hT", [128, 2, F_TILES, GROUP * 128])
        ysum = sb("c_ysum", [128, GROUP, D])
        ys = sb("c_ys", [128, TURN, GROUP, D])

        ps = ctx.enter_context(nc.psum_tensor("c_ps", [128, 8, 512], F32))
        ps_look = ps[:, 0:2, 0:HALF + 1]
        ps_x = ps[:, 2, :]
        ps_h = ps[:, 4:6, :]
        ps_y = ps[:, 6:8, :]

        rows_made = sem("c_rows_made")
        w_loaded = [sem(f"c_w_loaded_{i}") for i in range(2)]
        reached_ready = sem("c_reached_ready")
        look_done, ids_ready = sem("c_look_done"), sem("c_ids_ready")
        gathered = [sem(f"c_gathered_{i}") for i in range(TURN)]
        scattered = [sem(f"c_scattered_{i}") for i in range(TURN)]
        xT_done, xT_ready = sem("c_xT_done"), sem("c_xT_ready")
        h_done, h_ready = sem("c_h_done"), sem("c_h_ready")
        y_done, y_read, y_scaled = sem("c_y_done"), sem("c_y_read"), sem("c_y_scaled")
        block = ctx.enter_context(nc.Block())

        def wait(eng, semaphore, value):
            if not isinstance(value, int) or value > 0:
                eng.wait_ge(semaphore, value)

        def turns(eng, turn):
            turn(0, True, False)
            with eng.Fori(1, GROUPS // TURN - 1) as it:
                turn(it, False, False)
            turn(GROUPS // TURN - 1, False, True)

        @block.sync
        def _(sp):
            def load(e, parity):
                e = bass.ds(e, 1)
                sp.dma_start(b1_sb[parity][:], b1[e].rearrange("a p f -> (a p) f")).then_inc(w_loaded[parity], 16)
                sp.dma_start(w1_sb[parity][:], w1[e].rearrange("a d f -> (a d) f")).then_inc(w_loaded[parity], 16)
                sp.dma_start(w2_sb[parity][:], w2[e].rearrange("a (f p) d -> p (a f) d", p=128)).then_inc(w_loaded[parity], 16)
                sp.dma_start(b2_sb[parity][:], b2[e, :].rearrange("a d -> (a d)").partition_broadcast(128)).then_inc(w_loaded[parity], 16)

            load(0, 0)
            load(1, 1)
            with sp.Fori(1, GROUPS // TURN) as it:
                for parity in range(2):
                    sp.wait_ge(y_read, TURN * (it - 1) + 2 * parity + 2)
                    load(2 * it + parity, parity)

        @block.gpsimd
        def _(pool):
            pool.iota(slot_row[:], pattern=[[1, CAPACITY]], base=0, channel_multiplier=0,
                      allow_small_or_imprecise_dtypes=True).then_inc(rows_made, 1)
            pool.iota(slot_col[:], pattern=[[128, EXPERTS * SLOT_TILES]], base=0, channel_multiplier=1,
                      allow_small_or_imprecise_dtypes=True).then_inc(rows_made, 1)

            found_next = pool.alloc_register("found_next")
            scaled_next = pool.alloc_register("scaled_next")
            pool.reg_mov(found_next, GROUP)
            pool.reg_mov(scaled_next, 1)

            def gather(it, j):
                G = TURN * it + j
                wait(pool, y_scaled, G - TURN + 1)
                pool.wait_ge(ids_ready, found_next)
                pool.reg_add(found_next, found_next, GROUP)
                for i in range(GROUP):
                    pool.indirect_dma_start(
                        out=xs[:, j, i, :], out_offset=None, in_=x2_rows[:, :],
                        in_offset=bass.IndirectOffsetOnAxis(ap=ids[:, j, i:i + 1], axis=0)).then_inc(gathered[j], 16)

            def scatter(it, j):
                G = TURN * it + j
                if j % 2 == 0:
                    before = (j - 1) % TURN
                    for last in (before, before - 1):
                        wait(pool, scattered[last], 64 * (it + 1 if j else it))
                pool.wait_ge(y_scaled, G + 1 if isinstance(G, int) and it else scaled_next)
                pool.reg_add(scaled_next, scaled_next, 1)
                for i in range(GROUP):
                    pool.indirect_dma_start(
                        out=h2_rows[:, :], out_offset=bass.IndirectOffsetOnAxis(ap=ids_out[:, j, i:i + 1], axis=0),
                        in_=ys[:, j, i, :], in_offset=None, compute_op=ALU.add).then_inc(scattered[j], 16)

            def turn(it, first, last):
                for j in range(TURN):
                    if not (last and j + GATHER_AHEAD >= TURN):
                        ahead = j + GATHER_AHEAD
                        gather(it + ahead // TURN, ahead % TURN)
                    scatter(it, j)

            for j in range(GATHER_AHEAD):
                gather(0, j)
            turns(pool, turn)
            for j in range(TURN):
                pool.wait_ge(scattered[j], 64 * (GROUPS // TURN))

        @block.tensor
        def _(pe):
            def look(it, j, i):
                G = TURN * it + j
                t = GROUP * G + i
                if i == 0 and j % 2 == 0:
                    pe.wait_ge(reached_ready, 2 * it + j // 2 + 1)
                wait(pe, ids_ready, t - 1)
                at = 128 * (GROUP * (j % 2) + i)
                pe.matmul(ps_look[:, i % 2, :], reached[j // 2][:, at:at + 128], T.steps[:], start=True, stop=True)\
                    .then_inc(look_done, 1)

            def turn_x(it, j):
                G = TURN * it + j
                pe.wait_ge(gathered[j], 64 * (it + 1))
                wait(pe, xT_ready, G)
                for i in range(GROUP):
                    mm = pe.transpose(ps_x[:, 128 * i:128 * i + 128], xs[:, j, i, 0:D], T.ident[:])
                mm.then_inc(xT_done, 1)

            def hidden(it, j, f):
                G = TURN * it + j
                n = F_TILES * G + f
                if f == 0:
                    pe.wait_ge(xT_ready, G + 1)
                    pe.wait_ge(w_loaded[j // 2], 64 * (it + 1))
                wait(pe, h_ready, n - 1)
                pe.matmul(ps_h[:, f % 2, :], w1_sb[j // 2][:, 128 * f:128 * f + 128], xsT[:], start=True, stop=True)\
                    .then_inc(h_done, 1)

            def output(it, j):
                G = TURN * it + j
                pe.wait_ge(h_ready, F_TILES * (G + 1))
                wait(pe, y_read, G - 1)
                for i in range(GROUP):
                    for f in range(F_TILES):
                        mm = pe.matmul(ps_y[:, j % 2, 128 * i:128 * i + 128], hT[:, j % 2, f, 128 * i:128 * i + 128],
                                       w2_sb[j // 2][:, f, :], start=(f == 0), stop=(f == F_TILES - 1))
                mm.then_inc(y_done, 1)

            def turn(it, first, last):
                for j in range(TURN):
                    for f in range(F_TILES):
                        hidden(it, j, f)
                        if not (last and j + LOOK_AHEAD >= TURN):
                            ahead = j + LOOK_AHEAD
                            look(it + ahead // TURN, ahead % TURN, f)
                    if not (last and j == TURN - 1):
                        turn_x(it + (j + 1) // TURN, (j + 1) % TURN)
                    if not (first and j == 0):
                        output(it - (j == 0), (j - 1) % TURN)

            for j in range(LOOK_AHEAD):
                for i in range(GROUP):
                    look(0, j, i)
            turn_x(0, 0)
            turns(pe, turn)
            output(GROUPS // TURN - 1, TURN - 1)

        @block.scalar
        def _(act):
            def move_x(it, j):
                act.wait_ge(xT_done, TURN * it + j + 1)
                act.copy(xsT[:], ps_x).then_inc(xT_ready, 1)

            def turn(it, first, last):
                for j in range(TURN):
                    G = TURN * it + j
                    for f in range(F_TILES):
                        if f == 0:
                            wait(act, y_done, G - 1)
                        act.wait_ge(h_done, F_TILES * G + f + 1)
                        act.activation(hT[:, j % 2, f, :], ps_h[:, f % 2, :], ACT.Gelu,
                                       bias=b1_sb[j // 2][:, f:f + 1]).then_inc(h_ready, 1)
                    if not (last and j == TURN - 1):
                        move_x(it + (j + 1) // TURN, (j + 1) % TURN)

            move_x(0, 0)
            turns(act, turn)

        @block.vector
        def _(dve):
            dve.wait_ge(rows_made, 2)

            def reach(it, parity):
                e = 2 * it + parity
                wait(dve, look_done, SLOT_TILES * (e - 1))
                dve.tensor_scalar(reached[parity][:], slot_row[:], T.start_of[:, bass.ds(e, 1)], None, ALU.is_ge)\
                    .then_inc(reached_ready, 1)

            def find(it, j):
                G = TURN * it + j
                for i in range(GROUP):
                    t = GROUP * G + i
                    dve.wait_ge(look_done, t + 1)
                    dve.tensor_scalar(junk[:], ps_look[:, i % 2, 0:HALF], slot_col[:, bass.ds(t, 1)], None,
                                      ALU.is_le, ALU.add, accum_out=count[:, i % 2:i % 2 + 1])
                    dve.drain()
                    if i == 0:
                        wait(dve, gathered[j], 64 * it)
                    dve.scalar_tensor_tensor(ids[:, j, i:i + 1], ps_look[:, i % 2, HALF:HALF + 1], float(HALF),
                                             count[:, i % 2:i % 2 + 1], ALU.mult, ALU.add).then_inc(ids_ready, 1)

            def scale(it, j):
                G = TURN * it + j
                wait(dve, y_scaled, G)
                dve.wait_ge(y_done, G + 1)
                dve.tensor_tensor(ysum[:], ps_y[:, j % 2, :].rearrange("p (i d) -> p i d", d=D),
                                  b2_sb[j // 2][:, :].unsqueeze(1).to_broadcast([128, GROUP, D]), ALU.add).then_inc(y_read, 1)
                dve.drain()
                wait(dve, scattered[j], 64 * it)
                dve.tensor_copy(ids_out[:, j, :], ids[:, j, :])
                dve.tensor_tensor(ys[:, j], ysum[:], xs[:, j, :, bass.ds(D + 2 * it + j // 2, 1)].to_broadcast([128, GROUP, D]),
                                  ALU.mult).then_inc(y_scaled, 1)

            def turn(it, first, last):
                for j in range(TURN):
                    if not (last and j + LOOK_AHEAD >= TURN):
                        ahead = j + LOOK_AHEAD
                        if ahead % 2 == 0:
                            reach(it + ahead // TURN, ahead % TURN // 2)
                        find(it + ahead // TURN, ahead % TURN)
                    if not (first and j == 0):
                        scale(it - (j == 0), (j - 1) % TURN)

            for j in range(LOOK_AHEAD):
                if j % 2 == 0:
                    reach(0, j // 2)
                find(0, j)
            turns(dve, turn)
            scale(GROUPS // TURN - 1, TURN - 1)


def sigmoid_attention(nc, T, h3_rows, w_q, b_q, w_k, b_k, w_v, b_v, w_o, b_o, w_r, b_r, split_q, split_k, moe_rows,
                      w1, w1_sb, w2, w2_sb):
    with ExitStack() as ctx:
        def sb(name, shape, dt=F32):
            return ctx.enter_context(nc.sbuf_tensor(name, shape, dt))

        def sem(name):
            return ctx.enter_context(nc.semaphore(name))

        STEPS = 2 * STEPS_OF_GROUP
        GROUP_HEADS = HEADS // 2
        WEIGHT_RING = 3
        CUT = 188
        MAKE_AT = (5, 6, 7, 8, 9, 10, 11, 12, 13)
        CLOSE_AT = (2, 3, 4, 6, 7, 8, 10, 12)
        SPLIT_AT = ((9, 10), (14, 15))
        MAKES, CLOSES = 9, 8
        LOADS = 10

        wq_sb, wk_sb, wv_sb = sb("d_w_q", [D, D]), sb("d_w_k", [D, D]), sb("d_w_v", [D, D])
        bq_sb, bk_sb = sb("d_b_q", [D, 1]), sb("d_b_k", [D, 1])
        bv_sb, bo_sb = sb("d_b_v", [TILE, D]), sb("d_b_o", [TILE, D])
        wo_sb = sb("d_w_o", [128, 2, D])
        wr_sb = sb("d_w_r", [D, 64])
        br_sb = sb("d_b_r", [TILE, EXPERTS])

        xn = sb("d_xn", [TILE, TILES, D])
        xnT = sb("d_xnT", [D, SEQ])
        qk = sb("d_qk", [D, 2, SEQ])
        rest = sb("d_rest", [D, SEQ])
        parts = sb("d_parts", [D, 2, PARTS, SEQ], BF16)
        qs = sb("d_qs", [HEAD_D * SLOTS, HEADS, SEQ], BF16)
        ks = sb("d_ks", [HEAD_D * SLOTS, HEADS, SEQ], BF16)
        v = sb("d_v", [TILE, TILES, D])
        v_wide = sb("d_v_wide", [TILE, TILES, HEADS, 32])
        weights = sb("d_weights", [TILE, WEIGHT_RING, GROUP_HEADS, HALF])
        ao = sb("d_ao", [128, 2, SEQ])
        hb = sb("d_hb", [TILE, TILES, D])
        rows = sb("d_rows", [TILE, TILES, ROW1])
        x4T = sb("d_x4T", [D, SEQ])
        st1, st2 = sb("d_st1", [TILE, TILES, 6]), sb("d_st2", [TILE, TILES, 6])
        mv1, mv2 = sb("d_mv1", [TILE, TILES, 2]), sb("d_mv2", [TILE, TILES, 2])
        ve1, ve2 = sb("d_ve1", [TILE, TILES]), sb("d_ve2", [TILE, TILES])
        rs1, rs2 = sb("d_rs1", [TILE, TILES]), sb("d_rs2", [TILE, TILES])
        logits = sb("d_logits", [TILE, TILES, EXPERTS])
        best = sb("d_best", [TILE, TILES])
        first = sb("d_first", [TILE, TILES, EXPERTS])
        backwards = sb("d_backwards", [TILE, EXPERTS])
        chosen = sb("d_chosen", [TILE, TILES, EXPERTS], BF16)
        filled = sb("d_filled", [128, TILES + 1, EXPERTS])
        place_f = sb("d_place_f", [TILE, TILES])
        place = sb("d_place", [TILE, TILES], I32)
        region_i = sb("d_region_i", [128, EXPERTS], I32)
        backwards_i = sb("d_backwards_i", [TILE, EXPERTS], I32)
        token_i = sb("d_token_i", [TILE, TILES], I32)
        earlier = sb("d_earlier", [TILE, TILE], BF16)
        ones = sb("d_ones", [TILE, 128], BF16)

        ps = ctx.enter_context(nc.psum_tensor("d_ps", [128, 8, 512], F32))
        ps_scores = [ps[0:TILE, 2 * u:2 * u + 2, 0:HALF] for u in range(2)]
        ps_ao = [ps[:, 4 + m, 0:HALF] for m in range(2)]
        ps_make, ps_close = ps[:, 6, :], ps[:, 7, :]

        loaded = sem("d_loaded")
        h3_first_loaded, h3_loaded = sem("d_h3_first_loaded"), sem("d_h3_loaded")
        experts_loaded = sem("d_experts_loaded")
        zeroed, consts = sem("d_zeroed"), sem("d_consts")
        ve1_done, rs1_done = sem("d_ve1_done"), sem("d_rs1_done")
        ve2_done, rs2_done = sem("d_ve2_done"), sem("d_rs2_done")
        xn_ready = sem("d_xn_ready")
        make_done, make_read = sem("d_make_done"), sem("d_make_read")
        close_done, close_read = sem("d_close_done"), sem("d_close_read")
        split_ready = sem("d_split_ready")
        split_stored = sem("d_split_stored")
        stack_loaded = [sem(f"d_stack_loaded_{g}") for g in range(2)]
        v_ready = sem("d_v_ready")
        scores_done, weights_ready = sem("d_scores_done"), sem("d_weights_ready")
        av_done, ao_ready = sem("d_av_done"), sem("d_ao_ready")
        hb_ready, h4_ready = sem("d_hb_ready"), sem("d_h4_ready")
        x4_ready, chosen_ready = sem("d_x4_ready"), sem("d_chosen_ready")
        place_ready, placed = sem("d_place_ready"), sem("d_placed")
        block = ctx.enter_context(nc.Block())

        def wait(eng, semaphore, value):
            if not isinstance(value, int) or value > 0:
                eng.wait_ge(semaphore, value)

        def sequences(eng, step, needs_residual=False):
            step(-1, True, False, False)
            if needs_residual:
                eng.wait_ge(h3_loaded, 16 * (BATCH - 1))
            step(0, True, True, False)
            step(1, True, True, True)
            with eng.Fori(2, BATCH - 1) as b:
                step(b, True, True, True)
            step(BATCH - 1, False, True, True)
            step(BATCH, False, False, True)

        @block.sync
        def _(sp):
            for n in range(BATCH):
                sp.dma_start(T.resid[:, n * TILES:(n + 1) * TILES, :], tile_layout(h3_rows[n * SEQ:(n + 1) * SEQ, :]))\
                    .then_inc(h3_loaded if n else h3_first_loaded, 16)
                if n == 0:
                    sp.dma_start(wq_sb[:], w_q[:, :]).then_inc(loaded, 16)
                    sp.dma_start(wk_sb[:], w_k[:, :]).then_inc(loaded, 16)
                    sp.dma_start(wv_sb[:], w_v[:, :]).then_inc(loaded, 16)
                    sp.dma_start(bq_sb[:], b_q[:, :]).then_inc(loaded, 16)
                    sp.dma_start(bk_sb[:], b_k[:, :]).then_inc(loaded, 16)
                    sp.dma_start(bv_sb[:], b_v.partition_broadcast(TILE)).then_inc(loaded, 16)
                    sp.dma_start(bo_sb[:], b_o.partition_broadcast(TILE)).then_inc(loaded, 16)
                    sp.dma_start(br_sb[:], b_r.partition_broadcast(TILE)).then_inc(loaded, 16)
                    sp.wait_ge(zeroed, 3)
                    sp.dma_start(wo_sb[:], w_o[:, :, :]).then_inc(loaded, 16)
                    with nc.allow_non_contiguous_dma(reason="8 columns of 64"):
                        sp.dma_start(wr_sb[:, 0:EXPERTS], w_r[:, :]).then_inc(loaded, 16)

            def store_split(b):
                wait(sp, stack_loaded[0], 96 * b)
                wait(sp, stack_loaded[1], 96 * b)
                for n, to in enumerate((split_q, split_k)):
                    sp.wait_ge(split_ready, 2 * b + n + 1)
                    sp.dma_start(to.rearrange("s r t -> r s t"), parts[:, n]).then_inc(split_stored, 16)

            def load_stack(b, g):
                sp.wait_ge(split_stored, 32 * (b + 1))
                wait(sp, scores_done, 2 * (STEPS * (b - 1) + STEPS_OF_GROUP * (g + 1)))
                heads = slice(GROUP_HEADS * g, GROUP_HEADS * (g + 1))
                q_rows = split_q.rearrange("s (r h) t -> (s r) h t", h=HEADS)
                k_rows = split_k.rearrange("s (r h) t -> (s r) h t", h=HEADS)
                R = HEAD_D
                for at, n, k_from in ((0, 3, 0), (3, 2, 1), (5, 1, 2)):
                    sp.dma_start(qs[R * at:R * (at + n), heads, :], q_rows[0:R * n, heads, :]).then_inc(stack_loaded[g], 16)
                    sp.dma_start(ks[R * at:R * (at + n), heads, :], k_rows[R * k_from:R * (k_from + n), heads, :])\
                        .then_inc(stack_loaded[g], 16)

            def step(b, has_make, has_attend, has_close):
                if has_make:
                    store_split(b + 1)
                    load_stack(b + 1, 0)
                    load_stack(b + 1, 1)

            step(-1, True, False, False)
            sp.dma_start(w1_sb[:].rearrange("p (e f) -> p e f", e=EXPERTS), w1.rearrange("e p f -> p e f"))\
                .then_inc(experts_loaded, 16)
            sp.dma_start(w2_sb[:].rearrange("p (e f d) -> p e f d", e=EXPERTS, f=F_TILES),
                         w2.rearrange("e (f p) d -> p e f d", p=128)).then_inc(experts_loaded, 16)
            step(0, True, True, False)
            step(1, True, True, True)
            with sp.Fori(2, BATCH - 1) as b:
                step(b, True, True, True)
            sp.wait_ge(experts_loaded, 32)

        @block.tensor
        def _(pe):
            def make(b, n):
                wait(pe, make_read, MAKES * b + n)
                if n < 3:
                    pe.wait_ge(xn_ready, PAIRS * b + n + 1)
                    for i in (2 * n, 2 * n + 1):
                        mm = pe.transpose(ps_make[:, 128 * (i % 2):128 * (i % 2) + TILE], xn[:, i, :], T.ident[0:TILE, 0:TILE])
                elif n < 7:
                    w, h = (wq_sb, wk_sb)[(n - 3) // 2], (n - 3) % 2
                    mm = pe.matmul(ps_make[:, 0:HALF], w[:], xnT[:, h * HALF:(h + 1) * HALF], start=True, stop=True)
                else:
                    for i in range(3):
                        at = TILE * (3 * (n - 7) + i)
                        mm = pe.matmul(ps_make[0:TILE, 128 * i:128 * i + 128], xnT[:, at:at + TILE], wv_sb[:], start=True, stop=True)
                mm.then_inc(make_done, 1)

            def close(b, n):
                wait(pe, close_read, CLOSES * b + n)
                if n < 3:
                    pe.wait_ge(ao_ready, 4 * (b + 1))
                    for i in (2 * n, 2 * n + 1):
                        for g in range(2):
                            mm = pe.matmul(ps_close[0:TILE, 128 * (i % 2):128 * (i % 2) + 128], ao[:, g, i * TILE:(i + 1) * TILE],
                                           wo_sb[:, g, :], start=(g == 0), stop=(g == 1))
                elif n < 6:
                    pe.wait_ge(x4_ready, PAIRS * b + n - 2)
                    for i in (2 * n - 6, 2 * n - 5):
                        mm = pe.transpose(ps_close[:, 128 * (i % 2):128 * (i % 2) + TILE], rows[:, i, 0:D], T.ident[0:TILE, 0:TILE])
                elif n == 6:
                    for i in range(TILES):
                        mm = pe.matmul(ps_close[0:TILE, 64 * i:64 * i + 64], x4T[:, i * TILE:(i + 1) * TILE], wr_sb[:], start=True, stop=True)
                else:
                    pe.wait_ge(chosen_ready, b + 1)
                    which = chosen[:].rearrange("p i e -> p (i e)")
                    pe.matmul(ps_close[0:TILE, 0:TILES * EXPERTS], earlier[:], which, start=True, stop=True)
                    mm = pe.matmul(ps_close[:, 64:64 + TILES * EXPERTS], ones[:], which, start=True, stop=True)
                mm.then_inc(close_done, 1)

            def scores(b, s, u):
                g, half, i = s // STEPS_OF_GROUP, s % STEPS_OF_GROUP // TILES, s % TILES
                if s % STEPS_OF_GROUP == 0 and u == 0:
                    pe.wait_ge(stack_loaded[g], 96 * (b + 1))
                wait(pe, weights_ready, 2 * (STEPS * b + s) + u - 1)
                for j in range(2):
                    head = GROUP_HEADS * g + 2 * u + j
                    mm = pe.matmul(ps_scores[u][:, j, :], ks[:, head, i * TILE:(i + 1) * TILE],
                                   qs[:, head, half * HALF:(half + 1) * HALF], start=True, stop=True)
                mm.then_inc(scores_done, 1)

            def values(b, s, u):
                g, i = s // STEPS_OF_GROUP, s % TILES
                m = s // TILES
                if u == 0:
                    if s % STEPS_OF_GROUP == 0:
                        pe.wait_ge(v_ready, 2 * b + g + 1)
                    if i == 0:
                        wait(pe, ao_ready, 4 * b + m - 1)
                    pe.wait_ge(weights_ready, 2 * (STEPS * b + s) + 2)
                columns = (slice(0, CUT), slice(CUT, HALF))[u]
                if i == 0:
                    if u == 1:
                        return
                    columns = slice(0, HALF)
                for j in range(GROUP_HEADS):
                    mm = pe.matmul(ps_ao[m % 2][32 * j:32 * j + 32, columns], v_wide[:, i, GROUP_HEADS * g + j, :],
                                   weights[:, s % WEIGHT_RING, j, columns], start=(i == 0), stop=(i == TILES - 1 and u == 1),
                                   tile_position=(0, 32 * j))
                if u == 1 or i == 0:
                    mm.then_inc(av_done, 1)

            def step(b, has_make, has_attend, has_close):
                for s in range(STEPS):
                    for u in range(2):
                        if has_attend and s < STEPS - 1:
                            scores(b, s + 1, u)
                        elif has_attend and has_make:
                            scores(b + 1, 0, u)
                        if s == 0 and has_close:
                            values(b - 1, STEPS - 1, u)
                        if s > 0 and has_attend:
                            values(b, s - 1, u)
                    if has_make and s in MAKE_AT:
                        make(b + 1, MAKE_AT.index(s))
                    if has_close and s in CLOSE_AT:
                        close(b - 1, CLOSE_AT.index(s))
                if has_make and not has_attend:
                    for u in range(2):
                        scores(b + 1, 0, u)

            pe.wait_ge(loaded, 16 * LOADS)
            pe.wait_ge(consts, 5)
            sequences(pe, step)

        @block.scalar
        def _(act):
            def step(b, has_make, has_attend, has_close):
                if not has_attend:
                    return
                for s in range(STEPS):
                    n = STEPS * b + s
                    for u in range(2):
                        if u == 0:
                            wait(act, av_done, n - WEIGHT_RING + 1)
                        act.wait_ge(scores_done, 2 * n + u + 1)
                        act.activation(weights[:, s % WEIGHT_RING, 2 * u:2 * u + 2, :], ps_scores[u], ACT.Sigmoid, scale=HEAD_D ** -0.5)\
                            .then_inc(weights_ready, 1)

            sequences(act, step)

        @block.gpsimd
        def _(pool):
            for to in (wo_sb, wr_sb, v_wide):
                pool.memset(to[:], 0.0).then_inc(zeroed, 1)
            pool.memset(ones[:], 1.0).then_inc(zeroed, 1)
            pool.iota(region_i[:], pattern=[[REGION, EXPERTS]], base=0, channel_multiplier=0).then_inc(consts, 1)
            pool.iota(backwards_i[:], pattern=[[-1, EXPERTS]], base=EXPERTS, channel_multiplier=0).then_inc(consts, 1)
            pool.iota(token_i[:], pattern=[[TILE, TILES]], base=0, channel_multiplier=1).then_inc(consts, 1)
            pool.wait_ge(zeroed, 4)
            pool.affine_select(out=earlier[:], in_=ones[:, 0:TILE], compare_op=ALU.is_gt, fill=0.0, base=0,
                               pattern=[[1, TILE]], channel_multiplier=-1).then_inc(consts, 1)
            pool.memset(T.blank[:], 0.0).then_inc(zeroed, 1)
            pool.wait_ge(zeroed, 5)
            pool.memset(T.blank[:, 2 * D:ROW1], float(NO_TOKEN)).then_inc(consts, 1)
            pool.wait_ge(loaded, 16 * LOADS)

            place_next = pool.alloc_register("place_next")
            pool.reg_mov(place_next, 1)

            def step(b, has_make, has_attend, has_close):
                if has_close:
                    c = b - 1
                    wait(pool, h4_ready, PAIRS * c)
                    pool.tensor_tensor(hb[:], T.resid[:, bass.ds(TILES * c, TILES), :],
                                       bo_sb[:, :].unsqueeze(1).to_broadcast([TILE, TILES, D]), ALU.add).then_inc(hb_ready, 1)
                if has_make:
                    pool.wait_ge(ve1_done, b + 2)
                    pool.tensor_tensor(rs1[:], ve1[:], T.minus_half[0:TILE, 0:TILES], ALU.pow).then_inc(rs1_done, 1)
                if has_close:
                    c = b - 1
                    for g in range(PAIRS):
                        pool.wait_ge(ve2_done, PAIRS * c + g + 1)
                        pool.tensor_tensor(rs2[:, 2 * g:2 * g + 2], ve2[:, 2 * g:2 * g + 2],
                                           T.minus_half[0:TILE, 0:2], ALU.pow).then_inc(rs2_done, 1)
                    pool.wait_ge(place_ready, b if isinstance(b, int) and b == BATCH else place_next)
                    pool.reg_add(place_next, place_next, 1)
                    for i in range(TILES):
                        pool.indirect_dma_start(
                            out=moe_rows[:, :], out_offset=bass.IndirectOffsetOnAxis(ap=place[:, i:i + 1], axis=0),
                            in_=rows[:, i, :], in_offset=None,
                            bounds_check=EXPERTS * REGION - 1, oob_is_err=False).then_inc(placed, 16)

            sequences(pool, step, needs_residual=True)
            pool.wait_ge(placed, 16 * ALL_TILES)

        @block.vector
        def _(dve):
            def resid_tile(n):
                return T.resid[:, bass.ds(n, 1), :].rearrange("p a d -> p (a d)")

            def pair(ap, g):
                return ap[:, 2 * g:2 * g + 2]

            def make_stats(b):
                dve.drain()
                for t in range(TILES):
                    dve.bn_stats(st1[:, t, :], resid_tile(TILES * b + t))
                dve.drain()
                for t in range(TILES):
                    dve.bn_aggr(mv1[:, t, :], st1[:, t, :])
                dve.drain()
                dve.tensor_scalar(ve1[:], mv1[:, :, 1], LN_EPS, None, ALU.add).then_inc(ve1_done, 1)

            def make_norm(b):
                dve.wait_ge(rs1_done, b + 1)
                wait(dve, make_done, MAKES * (b - 1) + PAIRS)
                for t in range(TILES):
                    norm = dve.tensor_scalar(xn[:, t, :], resid_tile(TILES * b + t), mv1[:, t, 0:1], rs1[:, t:t + 1],
                                             ALU.subtract, ALU.mult)
                    if t % 2:
                        norm.then_inc(xn_ready, 1)

            def make(b, n):
                dve.wait_ge(make_done, MAKES * b + n + 1)
                if n < 3:
                    dve.tensor_copy(xnT[:, 2 * n * TILE:(2 * n + 2) * TILE].rearrange("p (s t) -> p s t", s=2),
                                    ps_make[:, 0:256].rearrange("p (s t) -> p s t", s=2)[:, :, 0:TILE]).then_inc(make_read, 1)
                elif n < 7:
                    which, h = (n - 3) // 2, (n - 3) % 2
                    dve.tensor_scalar(qk[:, which, h * HALF:(h + 1) * HALF], ps_make[:, 0:HALF], (bq_sb, bk_sb)[which][:, 0:1],
                                      None, ALU.add).then_inc(make_read, 1)
                else:
                    i = 3 * (n - 7)
                    dve.tensor_tensor(v[:, i:i + 3, :], ps_make[0:TILE, 0:3 * D].rearrange("p (i d) -> p i d", d=D),
                                      bv_sb[:, :].unsqueeze(1).to_broadcast([TILE, 3, D]), ALU.add).then_inc(make_read, 1)

            def split(b, which, stage):
                order = (0, 1, 2) if which == 0 else (2, 1, 0)
                part = [parts[:, which, n, :] for n in order]
                dve.drain()
                if stage == 0:
                    wait(dve, split_stored, 32 * b)
                    dve.tensor_copy(part[0], qk[:, which, :])
                    dve.drain()
                    dve.tensor_tensor(rest[:], qk[:, which, :], part[0], ALU.subtract)
                else:
                    dve.tensor_copy(part[1], rest[:])
                    dve.drain()
                    dve.tensor_tensor(part[2], rest[:], part[1], ALU.subtract).then_inc(split_ready, 1)

            def widen_v(b, g):
                dve.drain()
                wait(dve, av_done, STEPS * (b - 1) + STEPS_OF_GROUP * (g + 1))
                dve.tensor_copy(v_wide[:, :, GROUP_HEADS * g:GROUP_HEADS * (g + 1), 0:HEAD_D],
                                v[:, :, 64 * g:64 * g + 64].rearrange("p i (h d) -> p i h d", d=HEAD_D)).then_inc(v_ready, 1)

            def take_ao(b, m):
                dve.wait_ge(av_done, STEPS * b + TILES * (m + 1))
                if m == 0:
                    wait(dve, close_done, CLOSES * (b - 1) + PAIRS)
                g, half = m // 2, m % 2
                dve.tensor_copy(ao[:, g, half * HALF:(half + 1) * HALF], ps_ao[half]).then_inc(ao_ready, 1)

            def close(b, n):
                dve.wait_ge(close_done, CLOSES * b + n + 1)
                if n < 3:
                    if n == 0:
                        dve.wait_ge(hb_ready, b + 1)
                        wait(dve, placed, 16 * TILES * b)
                    dve.tensor_tensor(pair(rows, n)[:, :, D:2 * D], ps_close[0:TILE, 0:256].rearrange("p (i d) -> p i d", d=D),
                                      pair(hb, n), ALU.add).then_inc(close_read, 1)
                    dve.drain()
                    for t in (2 * n, 2 * n + 1):
                        stats = dve.bn_stats(st2[:, t, :], rows[:, t, D:2 * D])
                    stats.then_inc(h4_ready, 1)
                    dve.drain()
                    for t in (2 * n, 2 * n + 1):
                        dve.bn_aggr(mv2[:, t, :], st2[:, t, :])
                    dve.drain()
                    dve.tensor_scalar(pair(ve2, n), mv2[:, 2 * n:2 * n + 2, 1], LN_EPS, None, ALU.add).then_inc(ve2_done, 1)
                elif n < 6:
                    g = n - 3
                    dve.tensor_copy(x4T[:, 2 * g * TILE:(2 * g + 2) * TILE].rearrange("p (s t) -> p s t", s=2),
                                    ps_close[:, 0:256].rearrange("p (s t) -> p s t", s=2)[:, :, 0:TILE]).then_inc(close_read, 1)
                elif n == 6:
                    dve.tensor_tensor(logits[:], ps_close[0:TILE, 0:384].rearrange("p (i e) -> p i e", e=64)[:, :, 0:EXPERTS],
                                      br_sb[:, :].unsqueeze(1).to_broadcast([TILE, TILES, EXPERTS]), ALU.add).then_inc(close_read, 1)
                    wide = [TILE, TILES, EXPERTS]
                    dve.drain()
                    dve.tensor_reduce(best[:], logits[:], AX.X, ALU.max)
                    dve.drain()
                    dve.tensor_tensor(first[:], logits[:], best[:, :].unsqueeze(2).to_broadcast(wide), ALU.is_equal)
                    dve.drain()
                    dve.tensor_tensor(first[:], first[:], backwards[:, :].unsqueeze(1).to_broadcast(wide), ALU.mult)
                    dve.drain()
                    dve.tensor_reduce(best[:], first[:], AX.X, ALU.max)
                    dve.drain()
                    dve.tensor_tensor(chosen[:], first[:], best[:, :].unsqueeze(2).to_broadcast(wide), ALU.is_equal)\
                        .then_inc(chosen_ready, 1)
                else:
                    for i in range(TILES):
                        dve.tensor_tensor(filled[:, i + 1, :], filled[:, i, :],
                                          ps_close[:, 64 + EXPERTS * i:64 + EXPERTS * (i + 1)], ALU.add)
                        dve.drain()
                    dve.tensor_tensor(first[:], filled[0:TILE, 0:TILES, :],
                                      ps_close[0:TILE, 0:TILES * EXPERTS].rearrange("p (i e) -> p i e", e=EXPERTS), ALU.add)\
                        .then_inc(close_read, 1)
                    dve.drain()
                    dve.tensor_tensor(first[:], first[:], chosen[:], ALU.mult)
                    dve.tensor_copy(filled[:, 0, :], filled[:, TILES, :])
                    dve.tensor_scalar(rows[:, :, 2 * D], rows[:, :, 2 * D], float(SEQ), None, ALU.add)
                    dve.drain()
                    dve.tensor_reduce(place_f[:], first[:], AX.X, ALU.add)
                    dve.drain()
                    dve.tensor_copy(place[:], place_f[:]).then_inc(place_ready, 1)

            def close_norm(b, g):
                dve.wait_ge(rs2_done, PAIRS * b + g + 1)
                for t in (2 * g, 2 * g + 1):
                    norm = dve.tensor_scalar(rows[:, t, 0:D], rows[:, t, D:2 * D], mv2[:, t, 0:1], rs2[:, t:t + 1],
                                             ALU.subtract, ALU.mult)
                norm.then_inc(x4_ready, 1)


            def step(b, has_make, has_attend, has_close):
                for s in range(STEPS):
                    if s == 0 and has_make:
                        make_stats(b + 1)
                    if s == 1 and has_close:
                        take_ao(b - 1, 3)
                        if has_attend:
                            widen_v(b, 1)
                    if s == 1 and has_make:
                        make_norm(b + 1)
                    if has_attend and s in (7, 13, 19):
                        take_ao(b, s // 6 - 1)
                    if has_make:
                        if s in MAKE_AT:
                            make(b + 1, MAKE_AT.index(s))
                        if s == 14:
                            widen_v(b + 1, 0)
                            if not has_attend:
                                widen_v(b + 1, 1)
                    if has_close:
                        if s in CLOSE_AT:
                            close(b - 1, CLOSE_AT.index(s))
                        if s in (3, 4, 5):
                            close_norm(b - 1, s - 3)
                    if has_make:
                        for which in range(2):
                            if s in SPLIT_AT[which]:
                                split(b + 1, which, SPLIT_AT[which].index(s))

            dve.wait_ge(consts, 5)
            dve.wait_ge(zeroed, 4)
            dve.wait_ge(loaded, 16 * LOADS)
            dve.wait_ge(h3_first_loaded, 16)
            dve.tensor_copy(filled[:, 0, :], region_i[:])
            dve.tensor_copy(backwards[:], backwards_i[:])
            dve.tensor_scalar(rows[:, :, 2 * D], token_i[:], 1.0, float(-SEQ), ALU.mult, ALU.add)
            sequences(dve, step, needs_residual=True)
            dve.drain()
            dve.tensor_copy(T.ends[:], filled[:, 0, :])
            dve.drain()


def experts_by_router(nc, T, moe_rows, w1_sb, w2_sb, b1, b2, out_rows):
    RING = 6
    TURNS = MAX_TILES // RING
    assert TURNS * RING == MAX_TILES
    with ExitStack() as ctx:
        def sb(name, shape, dt=F32):
            return ctx.enter_context(nc.sbuf_tensor(name, shape, dt))

        def sem(name):
            return ctx.enter_context(nc.semaphore(name))

        b1_sb = sb("e_b1", [128, EXPERTS * F_TILES])
        b2_sb = sb("e_b2", [128, EXPERTS * D])
        region_i = sb("e_region_i", [1, EXPERTS], I32)
        region = sb("e_region", [1, EXPERTS])
        tile_i = sb("e_tile_i", [1, MAX_TILES], I32)
        tile_f = sb("e_tile_f", [1, MAX_TILES])
        blank_i = sb("e_blank_i", [128, EXPERTS + 1], I32)
        partition_f = sb("e_partition_f", [128, 1])
        tiles = sb("e_tiles", [1, EXPERTS])
        tiles_i = sb("e_tiles_i", [1, EXPERTS], I32)
        tiles_to = sb("e_tiles_to", [1, EXPERTS])
        nought = sb("e_nought", [1, EXPERTS])
        passed = sb("e_passed", [1, MAX_TILES, EXPERTS])
        passed_tiles = sb("e_passed_tiles", [1, MAX_TILES, EXPERTS])
        expert_f = sb("e_expert_f", [1, MAX_TILES])
        before_f = sb("e_before_f", [1, MAX_TILES])
        row_f = sb("e_row_f", [1, MAX_TILES])
        expert_of = sb("e_expert_of", [1, MAX_TILES], I32)
        row_of = sb("e_row_of", [1, MAX_TILES], I32)

        rows = [sb(f"e_rows_{r}", [128, ROW1]) for r in range(RING)]
        xT = sb("e_xT", [D, 128])
        h = sb("e_h", [128, HIDDEN])
        hT = sb("e_hT", [128, F_TILES, 128])
        base = sb("e_base", [128, D])
        out = [sb(f"e_out_{r}", [128, D]) for r in range(RING)]
        token = [sb(f"e_token_{r}", [128, 1], I32) for r in range(RING)]

        ps = ctx.enter_context(nc.psum_tensor("e_ps", [128, 8, 512], F32))
        ps_x, ps_h, ps_hT = ps[:, 0, 0:128], ps[:, 1, :], ps[:, 2, :]
        ps_y = [ps[:, 3 + n, 0:D] for n in range(2)]

        loaded, consts = sem("e_loaded"), sem("e_consts")
        table_ready, blank_ready, blanks_stored = sem("e_table_ready"), sem("e_blank_ready"), sem("e_blanks_stored")
        rows_loaded = [sem(f"e_rows_loaded_{r}") for r in range(RING)]
        stored = [sem(f"e_stored_{r}") for r in range(RING)]
        x_done, x_ready = sem("e_x_done"), sem("e_x_ready")
        h_done, h_ready = sem("e_h_done"), sem("e_h_ready")
        hT_done, hT_ready = sem("e_hT_done"), sem("e_hT_ready")
        y_done, out_ready = sem("e_y_done"), sem("e_out_ready")
        block = ctx.enter_context(nc.Block())

        def wait(eng, semaphore, value):
            if not isinstance(value, int) or value > 0:
                eng.wait_ge(semaphore, value)

        def turns(eng, turn):
            turn(0, True, False)
            with eng.Fori(1, TURNS - 1) as it:
                turn(it, False, False)
            turn(TURNS - 1, False, True)

        def expert(eng, j):
            return eng.value_load(expert_of[0:1, bass.ds(j, 1)], min_val=0, max_val=EXPERTS - 1)

        @block.sync
        def _(sp):
            sp.dma_start(b1_sb[:].rearrange("p (e f) -> p e f", f=F_TILES), b1.rearrange("e p f -> p e f")).then_inc(loaded, 16)
            sp.dma_start(b2_sb[:], b2.rearrange("e d -> (e d)").partition_broadcast(128)).then_inc(loaded, 16)
            sp.wait_ge(table_ready, 1)
            sp.wait_ge(blanks_stored, 16 * (EXPERTS + 1))

            def turn(it, first, last):
                for r in range(RING):
                    j = RING * it + r
                    at = sp.value_load(row_of[0:1, bass.ds(j, 1)], min_val=0, max_val=EXPERTS * REGION)
                    src = moe_rows[bass.ds(at, 128), :]
                    wait(sp, out_ready, j - RING + 1)
                    sp.dma_start(rows[r][:], src).then_inc(rows_loaded[r], 16)

            turns(sp, turn)

        @block.gpsimd
        def _(pool):
            pool.iota(region_i[:], pattern=[[REGION, EXPERTS]], base=0, channel_multiplier=0).then_inc(consts, 1)
            pool.iota(tile_i[:], pattern=[[1, MAX_TILES]], base=0, channel_multiplier=0).then_inc(consts, 1)
            pool.memset(nought[:], 0.0).then_inc(consts, 1)
            pool.wait_ge(blank_ready, 1)
            for e in range(EXPERTS + 1):
                pool.indirect_dma_start(
                    out=moe_rows[:, :], out_offset=bass.IndirectOffsetOnAxis(ap=blank_i[:, e:e + 1], axis=0),
                    in_=T.blank[:], in_offset=None, bounds_check=EXPERTS * REGION + 127, oob_is_err=False)\
                    .then_inc(blanks_stored, 16)

            out_next = pool.alloc_register("out_next")
            pool.reg_mov(out_next, 1)

            def turn(it, first, last):
                for r in range(RING):
                    j = RING * it + r
                    pool.wait_ge(out_ready, j + 1 if isinstance(j, int) else out_next)
                    pool.reg_add(out_next, out_next, 1)
                    pool.indirect_dma_start(
                        out=out_rows[:, :], out_offset=bass.IndirectOffsetOnAxis(ap=token[r][:], axis=0),
                        in_=out[r][:], in_offset=None, bounds_check=TOKENS - 1, oob_is_err=False).then_inc(stored[r], 16)

            turns(pool, turn)
            for r in range(RING):
                pool.wait_ge(stored[r], 16 * TURNS)

        @block.tensor
        def _(pe):
            def turn_x(it, r):
                pe.wait_ge(rows_loaded[r], 16 * (it + 1))
                pe.transpose(ps_x, rows[r][:, 0:D], T.ident[:]).then_inc(x_done, 1)

            def hidden(it, r, e):
                j = RING * it + r
                pe.wait_ge(x_ready, j + 1)
                pe.matmul(ps_h, xT[:], w1_sb[:, bass.ds(e * HIDDEN, HIDDEN)], start=True, stop=True).then_inc(h_done, 1)

            def turn_h(it, r):
                j = RING * it + r
                pe.wait_ge(h_ready, j + 1)
                for f in range(F_TILES):
                    mm = pe.transpose(ps_hT[:, 128 * f:128 * f + 128], h[:, 128 * f:128 * f + 128], T.ident[:])
                mm.then_inc(hT_done, 1)

            def output(it, r, e):
                j = RING * it + r
                pe.wait_ge(hT_ready, j + 1)
                wait(pe, out_ready, j - 1)
                for f in range(F_TILES):
                    mm = pe.matmul(ps_y[r % 2], hT[:, f, :], w2_sb[:, bass.ds(e * (F_TILES * D) + f * D, D)],
                                   start=(f == 0), stop=(f == F_TILES - 1))
                mm.then_inc(y_done, 1)

            def turn(it, first, last):
                for r in range(RING):
                    j = RING * it + r
                    hidden(it, r, expert(pe, j))
                    if not (last and r == RING - 1):
                        turn_x(it + (r + 1) // RING, (r + 1) % RING)
                    if not (first and r == 0):
                        output(it - (r == 0), (r - 1) % RING, expert(pe, j - 1))
                    turn_h(it, r)

            pe.wait_ge(table_ready, 1)
            turn_x(0, 0)
            turns(pe, turn)
            output(TURNS - 1, RING - 1, expert(pe, MAX_TILES - 1))

        @block.scalar
        def _(act):
            def move_x(j):
                act.wait_ge(x_done, j + 1)
                act.copy(xT[:], ps_x).then_inc(x_ready, 1)

            def turn(it, first, last):
                for r in range(RING):
                    j = RING * it + r
                    act.wait_ge(h_done, j + 1)
                    act.copy(h[:], ps_h).then_inc(h_ready, 1)
                    if not (last and r == RING - 1):
                        move_x(j + 1)

            move_x(0)
            turns(act, turn)

        @block.vector
        def _(dve):
            dve.wait_ge(consts, 3)
            dve.tensor_copy(partition_f[:], T.partition[:])
            dve.tensor_copy(region[:], region_i[:])
            dve.tensor_copy(tile_f[:], tile_i[:])
            dve.drain()
            dve.tensor_scalar(blank_i[:, 0:EXPERTS], T.ends[:], partition_f[:, 0:1], None, ALU.add)
            dve.tensor_scalar(blank_i[:, EXPERTS:], partition_f[:], float(EXPERTS * REGION), None, ALU.add).then_inc(blank_ready, 1)
            dve.tensor_tensor(tiles[:], T.ends[0:1, :], region[:], ALU.subtract)
            dve.drain()
            dve.tensor_scalar(tiles_i[:], tiles[:], 127.0, None, ALU.add)
            dve.drain()
            dve.tensor_scalar(tiles_i[:], tiles_i[:], 7, None, ALU.logical_shift_right)
            dve.drain()
            dve.tensor_copy(tiles[:], tiles_i[:])
            dve.drain()
            dve.tensor_tensor_scan(tiles_to[:], tiles[:], nought[:], 0.0, ALU.add, ALU.add)
            dve.drain()
            wide = [1, MAX_TILES, EXPERTS]
            dve.tensor_tensor(passed[:], tiles_to[:, :].unsqueeze(1).to_broadcast(wide),
                              tile_f[:, :].unsqueeze(2).to_broadcast(wide), ALU.is_le)
            dve.drain()
            dve.tensor_tensor(passed_tiles[:], passed[:], tiles[:, :].unsqueeze(1).to_broadcast(wide), ALU.mult)
            dve.tensor_reduce(expert_f[:], passed[:], AX.X, ALU.add)
            dve.drain()
            dve.tensor_reduce(before_f[:], passed_tiles[:], AX.X, ALU.add)
            dve.tensor_scalar(expert_of[:], expert_f[:], float(EXPERTS - 1), None, ALU.min)
            dve.drain()
            dve.tensor_tensor(row_f[:], tile_f[:], before_f[:], ALU.subtract)
            dve.drain()
            dve.tensor_scalar(row_f[:], row_f[:], 128.0, None, ALU.mult)
            dve.drain()
            dve.scalar_tensor_tensor(row_f[:], expert_f[:], float(REGION), row_f[:], ALU.mult, ALU.add)
            dve.drain()
            dve.tensor_scalar(row_of[:], row_f[:], float(EXPERTS * REGION), None, ALU.min)
            dve.drain()
            dve.sem_inc(table_ready, 1)
            dve.wait_ge(loaded, 32)

            def relu(it, r, e):
                j = RING * it + r
                dve.wait_ge(hT_done, j + 1)
                for f in range(F_TILES):
                    step = dve.tensor_scalar(hT[:, f, :], ps_hT[:, 128 * f:128 * f + 128], b1_sb[:, bass.ds(e * F_TILES + f, 1)],
                                             0.0, ALU.add, ALU.max)
                step.then_inc(hT_ready, 1)

            def finish(it, r, e):
                j = RING * it + r
                dve.drain()
                wait(dve, stored[r], 16 * it)
                dve.tensor_tensor(base[:], rows[r][:, D:2 * D], b2_sb[:, bass.ds(e * D, D)], ALU.add)
                dve.tensor_copy(token[r][:], rows[r][:, 2 * D:ROW1])
                dve.drain()
                dve.wait_ge(y_done, j + 1)
                dve.tensor_tensor(out[r][:], ps_y[r % 2], base[:], ALU.add).then_inc(out_ready, 1)

            def turn(it, first, last):
                for r in range(RING):
                    j = RING * it + r
                    relu(it, r, expert(dve, j))
                    if not (first and r == 0):
                        finish(it - (r == 0), (r - 1) % RING, expert(dve, j - 1))

            turns(dve, turn)
            finish(TURNS - 1, RING - 1, expert(dve, MAX_TILES - 1))


def build(nc, x, conv_w, conv_b, a0, f0, a1, f1, out_rows):
    def scratch(name, shape, dt=F32):
        return nc.dram_tensor(name, shape, dt, kind="Internal").ap()

    x2_rows = scratch("x2_rows", [TOKENS, ROW0])
    residual_rows = scratch("residual_rows", [TOKENS, D])
    logits_rows = scratch("logits_rows", [EXPERTS, TOKENS])
    split_q = scratch("split_q", [PARTS, D, SEQ], BF16)
    split_k = scratch("split_k", [PARTS, D, SEQ], BF16)
    moe_rows = scratch("moe_rows", [EXPERTS * REGION + 128, ROW1])
    with ExitStack() as ctx:
        T = constants(nc, ctx)
        prepare(nc, T)
        conv_and_causal_attention(nc, T, x, conv_w, conv_b, a0["Wq"], a0["bq"], a0["Wk"], a0["bk"], a0["Wv"], a0["bv"],
                                  a0["gamma"], a0["beta"], f0["Wr"], residual_rows, x2_rows[:, 0:D], logits_rows)
        select_tokens(nc, T, logits_rows, x2_rows)
        experts_by_token_choice(nc, T, x2_rows, residual_rows, f0["W1"], f0["b1"], f0["W2"], f0["b2"])
        w1_sb = ctx.enter_context(nc.sbuf_tensor("experts_w1", [D, EXPERTS * HIDDEN], F32))
        w2_sb = ctx.enter_context(nc.sbuf_tensor("experts_w2", [128, EXPERTS * F_TILES * D], F32))
        sigmoid_attention(nc, T, residual_rows, a1["Wq"], a1["bq"], a1["Wk"], a1["bk"], a1["Wv"], a1["bv"],
                          a1["Wo"], a1["bo"], f1["Wr"], f1["br"], split_q, split_k, moe_rows,
                          f1["W1"], w1_sb, f1["W2"], w2_sb)
        experts_by_router(nc, T, moe_rows, w1_sb, w2_sb, f1["b1"], f1["b2"], out_rows)


def by_head_dimension(w):
    return np.ascontiguousarray(w.reshape(-1, HEADS, HEAD_D).transpose(0, 2, 1).reshape(-1, D))


def hidden_on_partitions(b):
    return np.ascontiguousarray(b.reshape(EXPERTS, F_TILES, 128).transpose(0, 2, 1))


def heads_apart(w):
    apart = np.zeros((4, 32, 2, D), w.dtype)
    apart[:, 0:HEAD_D] = w.reshape(2, 4, HEAD_D, D).transpose(1, 2, 0, 3)
    return apart.reshape(128, 2, D)


def kernel(**inputs):
    import concourse.bacc as bacc
    from concourse.bass_utils import run_bass_kernel_spmd

    inputs = {name: np.asarray(a) for name, a in inputs.items()}
    arrays = {"x": inputs["x"], "conv_b": inputs["L0_tok_bias"],
              "conv_w": np.ascontiguousarray(inputs["L0_tok_weight"].transpose(2, 1, 0).reshape(TAPS * C_IN, D))}
    for layer in ("L0_attn", "L0_ffn", "L1_attn", "L1_ffn"):
        arrays.update({name: a for name, a in inputs.items() if name.startswith(layer)})
    for name in ("L0_ffn_b1", "L1_ffn_b1"):
        arrays[name] = hidden_on_partitions(arrays[name])
    for name in ("L1_attn_Wq", "L1_attn_Wk"):
        arrays[name] = by_head_dimension(arrays[name])
    for name in ("L1_attn_bq", "L1_attn_bk"):
        arrays[name] = by_head_dimension(arrays[name]).reshape(D, 1)
    arrays["L1_attn_Wo"] = heads_apart(arrays["L1_attn_Wo"])

    nc = bacc.Bacc("TRN2", target_bir_lowering=False, num_devices=1)
    aps = {name: nc.dram_tensor(name, a.shape, mybir.dt.from_np(a.dtype), kind="ExternalInput").ap()
           for name, a in arrays.items()}
    out = nc.dram_tensor("out", [TOKENS, D], F32, kind="ExternalOutput").ap()

    def of(layer):
        return {name[len(layer) + 1:]: ap for name, ap in aps.items() if name.startswith(layer)}

    build(nc, aps["x"], aps["conv_w"], aps["conv_b"], of("L0_attn"), of("L0_ffn"), of("L1_attn"), of("L1_ffn"), out)
    got = run_bass_kernel_spmd(nc, [arrays], core_ids=[0])
    return got.results[0]["out"].reshape(BATCH, SEQ, D)
```

```python
from contextlib import ExitStack

import concourse.bass as bass
import concourse.mybir as mybir
import numpy as np

F32, BF16, FP16 = mybir.dt.float32, mybir.dt.bfloat16, mybir.dt.float16
I32 = mybir.dt.int32
ALU = mybir.AluOpType
ACT = mybir.ActivationFunctionType
AX = mybir.AxisListType

class Tensors:
    pass


BATCH, C_IN, SEQ = 8, 64, 750
D = 128
TAPS, PAD = 9, 4
TAP_PAIRS = (TAPS + 1) // 2
TILE = 125
TILES = SEQ // TILE
PAIRS = TILES // 2
HALF = SEQ // 2
TOKENS = BATCH * SEQ
ALL_TILES = BATCH * TILES
D_ATT = 64
LN_EPS = 1e-5
MASKED = -1e30
EXPERTS = 8
CAPACITY = 1024
CHUNKS = 16
REGION = 6144
ROW1 = 2 * D + 1
NO_TOKEN = 8191
MAX_TILES = TOKENS // 128 + EXPERTS
STEPS_OF_GROUP = 12
HEADS, HEAD_D = 8, 16
PARTS, SLOTS = 3, 6
ROW0 = D + EXPERTS
HIDDEN = 512
F_TILES = HIDDEN // 128
SLOT_TILES = CAPACITY // 128
SEARCH_BITS = 30
SEARCHES = SEARCH_BITS // 2
CHUNK_BITS, CAPACITY_BITS = CHUNKS.bit_length() - 1, CAPACITY.bit_length() - 1


def tile_layout(rows):
    return rows.rearrange("(i p) d -> p i d", p=TILE)


def constants(nc, ctx):
    T = Tensors()
    T.resid = ctx.enter_context(nc.sbuf_tensor("resid", [TILE, ALL_TILES, D], F32))
    T.ident = ctx.enter_context(nc.sbuf_tensor("ident", [128, 128], F32))
    T.ident16 = ctx.enter_context(nc.sbuf_tensor("ident16", [128, 128], BF16))
    T.minus_half = ctx.enter_context(nc.sbuf_tensor("minus_half", [128, 8], F32))
    T.expert_start = ctx.enter_context(nc.sbuf_tensor("expert_start", [128, 1], I32))
    T.partition = ctx.enter_context(nc.sbuf_tensor("partition", [128, 1], I32))
    T.chunk_of = ctx.enter_context(nc.sbuf_tensor("chunk_of", [128, 1], I32))
    T.start_of = ctx.enter_context(nc.sbuf_tensor("start_of", [128, EXPERTS], F32))
    T.steps = ctx.enter_context(nc.sbuf_tensor("steps", [128, HALF + 1], FP16))
    T.slot_row = ctx.enter_context(nc.sbuf_tensor("slot_row", [128, CAPACITY], F32))
    T.slot_col = ctx.enter_context(nc.sbuf_tensor("slot_col", [128, EXPERTS * SLOT_TILES], F32))
    T.blank = ctx.enter_context(nc.sbuf_tensor("blank", [128, ROW1], F32))
    T.ends = ctx.enter_context(nc.sbuf_tensor("ends", [1, EXPERTS], I32))
    T.zeros = ctx.enter_context(nc.sbuf_tensor("zeros", [128, 128], F32))
    return T


def prepare(nc, T):
    with ExitStack() as ctx:
        filled = ctx.enter_context(nc.semaphore("filled"))
        made = ctx.enter_context(nc.semaphore("identities_made"))
        block = ctx.enter_context(nc.Block())

        @block.gpsimd
        def _(pool):
            pool.memset(T.zeros[:], 0.0).then_inc(filled, 1)
            pool.memset(T.minus_half[:], -0.5).then_inc(made, 1)
            pool.wait_ge(filled, 1)
            for m in (T.ident, T.ident16):
                pool.affine_select(out=m[:], in_=T.zeros[:], compare_op=ALU.not_equal, fill=1.0, base=0,
                                   pattern=[[-1, 128]], channel_multiplier=1).then_inc(made, 1)
            pool.iota(T.partition[:], pattern=[[0, 1]], base=0, channel_multiplier=1).then_inc(made, 1)
            pool.wait_ge(made, 4)

        @block.vector
        def _(dve):
            dve.wait_ge(made, 4)
            dve.tensor_scalar(T.expert_start[:], T.partition[:], CHUNK_BITS, CAPACITY_BITS,
                              ALU.logical_shift_right, ALU.logical_shift_left)
            dve.tensor_scalar(T.chunk_of[:], T.partition[:], CHUNKS - 1, None, ALU.bitwise_and)
            dve.drain()


def conv_and_causal_attention(nc, T, x, conv_w, conv_b, wq, bq, wk, bk, wv, bv, gamma, beta, wr,
                              h2_rows, x2_rows, logits_rows):
    with ExitStack() as ctx:
        def sb(name, shape, dt=F32):
            return ctx.enter_context(nc.sbuf_tensor(name, shape, dt))

        def sem(name):
            return ctx.enter_context(nc.semaphore(name))

        CONV_LOADS, LOADS = 3, 9

        xpad = sb("xpad", [128, SEQ + 2 * PAD])
        w_conv = sb("w_conv", [128, TAP_PAIRS, D])
        b_conv = sb("b_conv", [TILE, D])
        w_qk = sb("w_qk", [D, 2 * D_ATT])
        w_v = sb("w_v", [D, D])
        b_qk = sb("b_qk", [2 * D_ATT, 1])
        b_v = sb("b_v", [TILE, D])
        gam = sb("gam", [TILE, D])
        bet = sb("bet", [TILE, D])
        w_r = sb("w_r", [D, 8])
        causal = sb("causal", [128, TILE], BF16)

        xn = sb("xn", [TILE, TILES, D])
        xn_kept = sb("xn_kept", [TILE, 2, TILES, D])
        xnT = sb("xnT", [D, SEQ])
        qT = sb("qT", [D_ATT, SEQ])
        kT = sb("kT", [D_ATT, SEQ])
        v = sb("v", [TILE, 2, TILES, D])
        probs = sb("probs", [TILE, 2, TILES, TILE])
        probsT = sb("probsT", [TILE, TILES, TILE])
        neg_max = sb("neg_max", [TILE, TILES])
        row_sum = sb("row_sum", [TILE, TILES])
        row_inv = sb("row_inv", [TILE, TILES])
        y = sb("y", [TILE, 2 * TILES, D])
        z = sb("z", [TILE, TILES, D])
        hb = sb("hb", [TILE, TILES, D])
        x2 = sb("x2", [TILE, TILES, D])
        x2T = sb("x2T", [D, SEQ])
        logits = sb("logits", [8, 2, HALF])
        st1 = sb("st1", [TILE, TILES, 6])
        mv1 = sb("mv1", [TILE, TILES, 2])
        ve1 = sb("ve1", [TILE, TILES])
        rs1 = sb("rs1", [TILE, TILES])
        nm1 = sb("nm1", [TILE, TILES])
        shift1 = sb("shift1", [TILE, TILES])
        st2 = sb("st2", [TILE, TILES, 6])
        mv2 = sb("mv2", [TILE, TILES, 2])
        ve2 = sb("ve2", [TILE, TILES])
        rs2 = sb("rs2", [TILE, TILES])
        st3 = sb("st3", [TILE, TILES, 6])
        mv3 = sb("mv3", [TILE, TILES, 2])
        ve3 = sb("ve3", [TILE, TILES])
        rs3 = sb("rs3", [TILE, TILES])

        ps = ctx.enter_context(nc.psum_tensor("ps", [128, 8, 512], F32))
        ps_scores = [ps[:, 2 * n:2 * n + 2, :].rearrange("p a (s d) -> p (a s) d", d=128) for n in range(2)]
        ps_probsT = ps[0:TILE, 4, :].rearrange("p (s d) -> p s d", d=128)
        ps_probsT_last = ps[0:TILE, 7, 0:256].rearrange("p (s d) -> p s d", d=128)
        ps_out = ps[0:TILE, 5, 0:D]
        ps_v = ps[0:TILE, 4:6, 0:3 * D]
        ps_make, ps_close = ps[:, 6, :], ps[:, 7, :]
        MAKES, CLOSES = 8, 5

        conv_loaded, weights_loaded = sem("conv_loaded"), sem("weights_loaded")
        pads_zero = sem("pads_zero")
        mask_made = sem("mask_made")
        x_loaded = sem("x_loaded")
        make_done, make_read = sem("make_done"), sem("make_read")
        close_done, close_read = sem("close_done"), sem("close_read")
        ve1_done = sem("ve1_done")
        rs1_done = sem("rs1_done")
        xn_ready = sem("xn_ready")
        xn_kept_ready = sem("xn_kept_ready")
        v_done, v_ready = sem("v_done"), sem("v_ready")
        scores_done = sem("scores_done")
        max_done = sem("max_done")
        probs_ready = sem("probs_ready")
        probsT_done = sem("probsT_done")
        probsT_ready = sem("probsT_ready")
        pv_done = sem("pv_done")
        y_ready = sem("y_ready")
        ve2_done, rs2_done = sem("ve2_done"), sem("rs2_done")
        hb_ready = sem("hb_ready")
        h2_ready = sem("h2_ready")
        ve3_done, rs3_done = sem("ve3_done"), sem("rs3_done")
        x2_ready = sem("x2_ready")
        h2_stored, x2_stored, logits_stored = sem("h2_stored"), sem("x2_stored"), sem("logits_stored")

        block = ctx.enter_context(nc.Block())

        def wait(eng, semaphore, value):
            if not isinstance(value, int) or value > 0:
                eng.wait_ge(semaphore, value)

        def make_bank(n):
            return {1: ps_close, 5: ps[:, 3, :], 7: ps[:, 2, :]}.get(n, ps_make)

        def x_rows(b):
            return x[bass.ds(b, 1)].rearrange("a c t -> (a c) t")

        def load_x(sp, src):
            sp.dma_start(xpad[0:C_IN, PAD:PAD + SEQ], src).then_inc(x_loaded, 16)
            sp.dma_start(xpad[C_IN:128, PAD - 1:PAD - 1 + SEQ], src).then_inc(x_loaded, 16)

        @block.sync
        def _(sp):
            sp.wait_ge(pads_zero, 1)
            load_x(sp, x_rows(0))
            for dst, src in ((w_conv[:, 0:4, :], conv_w[0:512, :].rearrange("(m p) d -> p m d", p=128)),
                             (w_conv[0:64, 4, :], conv_w[512:576, :]),
                             (b_conv[:], conv_b.partition_broadcast(TILE))):
                sp.dma_start(dst, src).then_inc(conv_loaded, 16)
            for dst, src in ((w_qk[:, 0:D_ATT], wq), (w_qk[:, D_ATT:], wk), (w_v[:], wv),
                             (b_qk[0:D_ATT, :], bq.rearrange("(p a) -> p a", a=1)),
                             (b_qk[D_ATT:, :], bk.rearrange("(p a) -> p a", a=1)),
                             (b_v[:], bv.partition_broadcast(TILE)), (gam[:], gamma.partition_broadcast(TILE)),
                             (bet[:], beta.partition_broadcast(TILE)), (w_r[:], wr)):
                sp.dma_start(dst, src).then_inc(weights_loaded, 16)

            def step(b, has_make, has_attend, has_close):
                if has_make:
                    if not (isinstance(b, int) and b == BATCH - 2):
                        src = x_rows(b + 2)
                        sp.wait_ge(make_done, MAKES * (b + 1) + PAIRS)
                        load_x(sp, src)
                if has_close:
                    c = b - 1
                    row, tile = sp.snap(SEQ * c), sp.snap(TILES * c)
                    sp.wait_ge(x2_ready, PAIRS * (c + 1))
                    sp.dma_start(tile_layout(x2_rows[bass.ds(row, SEQ), :]), x2[:]).then_inc(x2_stored, 16)
                    sp.dma_start(tile_layout(h2_rows[bass.ds(row, SEQ), :]),
                                 T.resid[:, bass.ds(tile, TILES), :]).then_inc(h2_stored, 16)

            step(-1, True, False, False)
            step(0, True, True, False)
            step(1, True, True, True)
            with sp.Fori(2, BATCH - 2) as b:
                step(b, True, True, True)
            step(BATCH - 2, True, True, True)
            step(BATCH - 1, False, True, True)
            step(BATCH, False, False, True)
            sp.wait_ge(x2_stored, 16 * BATCH)
            sp.wait_ge(h2_stored, 16 * BATCH)
            sp.wait_ge(logits_stored, 16 * BATCH)

        @block.tensor
        def _(pe):
            def make(b, n):
                bank = make_bank(n)
                if n < 2:
                    wait(pe, close_read, CLOSES * (b - 2))
                wait(pe, make_read, MAKES * b + (0, 0, 1, 3, 4, 4, 6, 6)[n])
                if n < 3:
                    if n == 0:
                        pe.wait_ge(x_loaded, 32 * (b + 1))
                    for i in (2 * n, 2 * n + 1):
                        for m in range(TAP_PAIRS):
                            rows = 128 if m < TAP_PAIRS - 1 else C_IN
                            at = TILE * i + 2 * m
                            mm = pe.matmul(bank[0:TILE, D * (i % 2):D * (i % 2) + D], xpad[0:rows, at:at + TILE],
                                           w_conv[0:rows, m, :], start=(m == 0), stop=(m == TAP_PAIRS - 1))
                elif n < 6:
                    g = n - 3
                    pe.wait_ge(xn_ready, PAIRS * b + g + 1)
                    for i in (2 * g, 2 * g + 1):
                        mm = pe.transpose(bank[:, 128 * (i % 2):128 * (i % 2) + TILE], xn[:, i, :], T.ident[0:TILE, 0:TILE])
                else:
                    h = n - 6
                    mm = pe.matmul(bank[:, 0:HALF], w_qk[:], xnT[:, h * HALF:(h + 1) * HALF], start=True, stop=True)
                mm.then_inc(make_done, 1)

            def close(b, n):
                wait(pe, close_read, CLOSES * b + min(n, 3))
                if n < 3:
                    pe.wait_ge(x2_ready, PAIRS * b + n + 1)
                    for i in (2 * n, 2 * n + 1):
                        mm = pe.transpose(ps_close[:, 128 * (i % 2):128 * (i % 2) + TILE], x2[:, i, :], T.ident[0:TILE, 0:TILE])
                else:
                    h = n - 3
                    mm = pe.matmul((ps_close, ps_make)[h][0:8, 0:HALF], w_r[:], x2T[:, h * HALF:(h + 1) * HALF], start=True, stop=True)
                mm.then_inc(close_done, 1)

            def project_v(b):
                wait(pe, probsT_ready, TILES * b)
                wait(pe, y_ready, TILES * b - 1)
                for i in range(TILES):
                    mm = pe.matmul(ps_v[:, i // 3, D * (i % 3):D * (i % 3) + D], xnT[:, i * TILE:(i + 1) * TILE], w_v[:],
                                   start=True, stop=True)
                mm.then_inc(v_done, 1)

            def scores(b, i):
                n = TILES * b + i
                if i == 0:
                    pe.wait_ge(make_read, MAKES * (b + 1))
                wait(pe, probs_ready, n - 1)
                bank = ps_scores[i % 2]
                for lo, hi in ((0, min(4, i + 1)), (4, i + 1)):
                    if lo >= hi:
                        continue
                    pe.matmul(bank[0:TILE, lo:hi, 0:TILE], qT[:, i * TILE:(i + 1) * TILE],
                              kT[:, lo * TILE:hi * TILE], start=True, stop=(hi <= i))
                pe.matmul(bank[0:TILE, i, 0:TILE], T.ident16[0:TILE, 0:TILE], causal[0:TILE, :],
                          start=False, stop=True).then_inc(scores_done, 1)

            def turn_probs(b, i):
                n = TILES * b + i
                if i == 0:
                    pe.wait_ge(v_ready, b + 1)
                pe.wait_ge(probs_ready, n + 1)
                wait(pe, probsT_ready, n)
                for j in range(min(4, i + 1)):
                    mm = pe.transpose(ps_probsT[:, j, 0:TILE], probs[:, i % 2, j, :], T.ident[0:TILE, 0:TILE])
                if i == 4:
                    wait(pe, close_read, CLOSES * (b - 1))
                    if not (isinstance(b, int) and b == BATCH - 1):
                        pe.wait_ge(make_read, MAKES * (b + 1) + PAIRS)
                for j in range(4, i + 1):
                    mm = pe.transpose(ps_probsT_last[:, j - 4, 0:TILE], probs[:, i % 2, j, :], T.ident[0:TILE, 0:TILE])
                mm.then_inc(probsT_done, 1)

            def values(b, i):
                n = TILES * b + i
                if i == TILES - 1 and not (isinstance(b, int) and b == BATCH - 1):
                    pe.wait_ge(v_ready, b + 2)
                pe.wait_ge(probsT_ready, n + 1)
                wait(pe, y_ready, n)
                for j in range(i + 1):
                    mm = pe.matmul(ps_out, probsT[:, j, :],
                                   v[:, bass.ds(b % 2, 1), j, :].rearrange("p a d -> p (a d)"),
                                   start=(j == 0), stop=(j == i))
                mm.then_inc(pv_done, 1)

            def step(b, has_make, has_attend, has_close):
                for i in range(TILES):
                    if has_attend and i < TILES - 1:
                        scores(b, i + 1)
                    if i > 0 and has_attend:
                        values(b, i - 1)
                    if i == 0 and has_close:
                        values(b - 1, TILES - 1)
                    if has_make and i < 3:
                        make(b + 1, i)
                    if has_make and i == 5:
                        make(b + 1, 3)
                    if has_attend:
                        turn_probs(b, i)
                if not has_attend and has_make:
                    pe.wait_ge(weights_loaded, 16 * LOADS)
                if has_attend and has_close:
                    pe.wait_ge(probsT_ready, TILES * (b + 1))
                for n in (4, 5, 6, 7):
                    if has_make:
                        make(b + 1, n)
                    if has_close and n < 7:
                        close(b - 1, n - 4)
                if has_make:
                    project_v(b + 1)
                    scores(b + 1, 0)
                if has_close:
                    close(b - 1, 3)
                    close(b - 1, 4)

            pe.wait_ge(conv_loaded, 16 * CONV_LOADS)
            pe.wait_ge(mask_made, 2)
            step(-1, True, False, False)
            step(0, True, True, False)
            step(1, True, True, True)
            with pe.Fori(2, BATCH - 1) as b:
                step(b, True, True, True)
            step(BATCH - 1, False, True, True)
            step(BATCH, False, False, True)

        @block.scalar
        def _(act):
            def move_pair(done, count, to, bank, g, read):
                act.wait_ge(done, count)
                act.copy(to[:, 2 * g * TILE:(2 * g + 2) * TILE].rearrange("p (s t) -> p s t", s=2),
                         bank[:, 0:256].rearrange("p (s t) -> p s t", s=2)[:, :, 0:TILE]).then_inc(read, 1)

            def exp(b, i):
                act.wait_ge(max_done, TILES * b + i + 1)
                act.activation(probs[:, i % 2, 0:i + 1, :], ps_scores[i % 2][0:TILE, 0:i + 1, 0:TILE], ACT.Exp,
                               bias=neg_max[:, i:i + 1], accum_out=row_sum[:, i:i + 1]).then_inc(probs_ready, 1)

            def norm(b, to, rs, shift, rs_done, ready):
                act.wait_ge(rs_done, b + 1)
                first = act.snap(TILES * b)
                for t in range(TILES):
                    step = act.activation(to[:, t, :], T.resid[:, bass.ds(first + t, 1), :].rearrange("p a d -> p (a d)"),
                                          ACT.Identity, bias=shift[:, t:t + 1], scale=rs[:, t:t + 1])
                    if t % 2:
                        step.then_inc(ready, 1)

            def step(b, has_make, has_attend, has_close):
                for i in range(TILES):
                    if has_make and i == 5:
                        move_pair(make_done, MAKES * (b + 1) + 4, xnT, ps_make, 0, make_read)
                    if has_attend:
                        act.wait_ge(probsT_done, TILES * b + i + 1)
                        m = min(4, i + 1)
                        copy = act.copy(probsT[:, 0:m, :], ps_probsT[:, 0:m, 0:TILE])
                        if i >= 4:
                            copy = act.copy(probsT[:, 4:i + 1, :], ps_probsT_last[:, 0:i - 3, 0:TILE])
                        copy.then_inc(probsT_ready, 1)
                    if has_attend and i < TILES - 1:
                        exp(b, i + 1)
                    if has_make and i == 4:
                        wait(act, xn_kept_ready, b + 1)
                        wait(act, make_done, MAKES * b + 6)
                        norm(b + 1, xn, rs1, shift1, rs1_done, xn_ready)
                for n in (4, 5, 6, 7):
                    if has_make and n < 6:
                        move_pair(make_done, MAKES * (b + 1) + n + 1, xnT, make_bank(n), n - 3, make_read)
                    if has_make and n >= 6:
                        columns = slice((n - 6) * HALF, (n - 5) * HALF)
                        act.wait_ge(make_done, MAKES * (b + 1) + n + 1)
                        act.activation(qT[:, columns], make_bank(n)[0:D_ATT, 0:HALF], ACT.Identity, bias=b_qk[0:D_ATT, 0:1])
                        act.activation(kT[:, columns], make_bank(n)[D_ATT:, 0:HALF], ACT.Identity, bias=b_qk[D_ATT:, 0:1])\
                            .then_inc(make_read, 1)
                    if has_close and n < 7:
                        move_pair(close_done, CLOSES * (b - 1) + n - 3, x2T, ps_close, n - 4, close_read)
                if has_make:
                    exp(b + 1, 0)
                if has_close:
                    wait(act, logits_stored, 16 * (b - 1))
                    for h in range(2):
                        act.wait_ge(close_done, CLOSES * (b - 1) + 4 + h)
                        act.copy(logits[:, h, :], (ps_close, ps_make)[h][0:8, 0:HALF]).then_inc(close_read, 1)
                    act.wait_ge(close_read, CLOSES * b)
                    act.dma_start(logits_rows[:, bass.ds(SEQ * (b - 1), SEQ)],
                                  logits[:].rearrange("e a t -> e (a t)")).then_inc(logits_stored, 16)

            act.wait_ge(weights_loaded, 16 * LOADS)
            step(-1, True, False, False)
            step(0, True, True, False)
            step(1, True, True, True)
            with act.Fori(2, BATCH - 1) as b:
                step(b, True, True, True)
            step(BATCH - 1, False, True, True)
            step(BATCH, False, False, True)

        @block.gpsimd
        def _(pool):
            pool.memset(xpad[:], 0.0).then_inc(pads_zero, 1)
            pool.memset(causal[:], 0.0).then_inc(mask_made, 1)
            pool.wait_ge(mask_made, 1)
            pool.affine_select(out=causal[:], in_=causal[:], compare_op=ALU.is_ge, fill=MASKED, base=0,
                               pattern=[[-1, TILE]], channel_multiplier=1).then_inc(mask_made, 1)

            def rsqrt(var_done, count, rs, ve, done, nm=None, shift=None):
                pool.wait_ge(var_done, count)
                last = pool.tensor_tensor(rs[:], ve[:], T.minus_half[0:TILE, 0:TILES], ALU.pow)
                if nm is not None:
                    pool.drain()
                    last = pool.tensor_tensor(shift[:], nm[:], rs[:], ALU.mult)
                last.then_inc(done, 1)

            def step(b, has_make, has_attend, has_close):
                if has_close:
                    c = b - 1
                    wait(pool, h2_ready, TILES * c)
                    pool.tensor_tensor(hb[:], T.resid[:, bass.ds(TILES * c, TILES), :],
                                       bet[:, :].unsqueeze(1).to_broadcast([TILE, TILES, D]), ALU.add).then_inc(hb_ready, 1)
                    rsqrt(ve2_done, b, rs2, ve2, rs2_done)
                if has_make:
                    rsqrt(ve1_done, b + 2, rs1, ve1, rs1_done, nm1, shift1)
                if has_close:
                    rsqrt(ve3_done, b, rs3, ve3, rs3_done)
                if has_make:
                    pool.wait_ge(xn_ready, PAIRS * (b + 2))
                    pool.tensor_copy(xn_kept[:, bass.ds((b + 1) % 2, 1), :, :].rearrange("p a i d -> p (a i) d"), xn[:])\
                        .then_inc(xn_kept_ready, 1)

            step(-1, True, False, False)
            pool.wait_ge(weights_loaded, 16 * LOADS)
            step(0, True, True, False)
            step(1, True, True, True)
            with pool.Fori(2, BATCH - 1) as b:
                step(b, True, True, True)
            step(BATCH - 1, False, True, True)
            step(BATCH, False, False, True)

        @block.vector
        def _(dve):
            def resid_tile(n):
                return T.resid[:, bass.ds(n, 1), :].rearrange("p a d -> p (a d)")

            def stats(src_of, tiles, st):
                dve.drain()
                for t in tiles:
                    dve.bn_stats(st[:, t, :], src_of(t))

            def collect(st, mv, ve, ve_done, nm=None):
                dve.drain()
                for t in range(TILES):
                    dve.bn_aggr(mv[:, t, :], st[:, t, :])
                dve.drain()
                if nm is not None:
                    dve.tensor_scalar(nm[:], mv[:, :, 0], -1.0, None, ALU.mult)
                dve.tensor_scalar(ve[:], mv[:, :, 1], LN_EPS, None, ALU.add).then_inc(ve_done, 1)

            def take_conv(b, i):
                if 1 <= i <= 3:
                    g = i - 1
                    dve.wait_ge(make_done, MAKES * b + g + 1)
                    dve.tensor_tensor(T.resid[:, bass.ds(TILES * b + 2 * g, 2), :],
                                      (ps_close if g == 1 else ps_make)[0:TILE, 0:2 * D].rearrange("p (s d) -> p s d", d=D),
                                      b_conv[:, :].unsqueeze(1).to_broadcast([TILE, 2, D]), ALU.add).then_inc(make_read, 1)
                    stats(lambda t: resid_tile(TILES * b + t), (2 * g, 2 * g + 1), st1)

            def project(b):
                dve.wait_ge(v_done, b + 1)
                wait(dve, pv_done, TILES * (b - 1))
                dve.tensor_tensor(v[:, bass.ds(b % 2, 1), :, :].rearrange("p a (s i) d -> p (a s) i d", s=2),
                                  ps_v.rearrange("p s (i d) -> p s i d", d=D),
                                  b_v[:, :].unsqueeze(1).unsqueeze(1).to_broadcast([TILE, 2, 3, D]), ALU.add).then_inc(v_ready, 1)

            def negmax(b, i):
                dve.wait_ge(scores_done, TILES * b + i + 1)
                dve.tensor_reduce(neg_max[:, i:i + 1], ps_scores[i % 2][0:TILE, 0:i + 1, 0:TILE], AX.XY, ALU.max, negate=True)\
                    .then_inc(max_done, 1)

            def y_tile(b, i):
                return y[:, bass.ds(b % 2 * TILES + i, 1), :].rearrange("p a d -> p (a d)")

            def finish(b, i):
                n = TILES * b + i
                dve.wait_ge(probs_ready, n + 1)
                dve.reciprocal(row_inv[:, i:i + 1], row_sum[:, i:i + 1])
                if i == 0:
                    dve.drain()
                else:
                    stats(lambda t: y_tile(b, t), (i - 1,), st2)
                if i == 0:
                    dve.wait_ge(xn_kept_ready, b + 1)
                dve.wait_ge(pv_done, n + 1)
                dve.scalar_tensor_tensor(y_tile(b, i), ps_out, row_inv[:, i:i + 1],
                                         xn_kept[:, bass.ds(b % 2, 1), i, :].rearrange("p a d -> p (a d)"),
                                         ALU.mult, ALU.add).then_inc(y_ready, 1)

            def close(b, i):
                if i == 0:
                    stats(lambda t: y_tile(b, t), (TILES - 1,), st2)
                    collect(st2, mv2, ve2, ve2_done)
                    for t in range(TILES):
                        dve.scalar_tensor_tensor(z[:, t, :], y_tile(b, t), mv2[:, t, 0:1], gam[:], ALU.subtract, ALU.mult)
                if i == 1:
                    dve.drain()
                    dve.wait_ge(rs2_done, b + 1)
                    dve.wait_ge(hb_ready, b + 1)
                    for t in range(TILES):
                        dve.scalar_tensor_tensor(resid_tile(TILES * b + t), z[:, t, :], rs2[:, t:t + 1], hb[:, t, :],
                                                 ALU.mult, ALU.add).then_inc(h2_ready, 1)
                if i == 2:
                    stats(lambda t: resid_tile(TILES * b + t), range(TILES), st3)
                if i == 4:
                    collect(st3, mv3, ve3, ve3_done)
                if i == 5:
                    dve.wait_ge(rs3_done, b + 1)
                    wait(dve, x2_stored, 16 * b)
                    wait(dve, close_done, CLOSES * (b - 1) + 3)
                    for t in range(TILES):
                        norm = dve.tensor_scalar(x2[:, t, :], resid_tile(TILES * b + t), mv3[:, t, 0:1], rs3[:, t:t + 1],
                                                 ALU.subtract, ALU.mult)
                        if t % 2:
                            norm.then_inc(x2_ready, 1)

            def step(b, has_make, has_attend, has_close):
                for i in range(TILES):
                    if has_attend and i < TILES - 1:
                        negmax(b, i + 1)
                    if has_attend and i > 0:
                        finish(b, i - 1)
                    if has_close and i == 0:
                        finish(b - 1, TILES - 1)
                    if has_make:
                        take_conv(b + 1, i)
                    if has_close:
                        close(b - 1, i)
                    if has_make and i == 3:
                        collect(st1, mv1, ve1, ve1_done, nm1)
                if has_make:
                    if not has_attend:
                        dve.wait_ge(weights_loaded, 16 * LOADS)
                    project(b + 1)
                    negmax(b + 1, 0)

            dve.wait_ge(conv_loaded, 16 * CONV_LOADS)
            step(-1, True, False, False)
            step(0, True, True, False)
            step(1, True, True, True)
            with dve.Fori(2, BATCH - 1) as b:
                step(b, True, True, True)
            step(BATCH - 1, False, True, True)
            step(BATCH, False, False, True)


def select_tokens(nc, T, logits_rows, x2_rows):
    with ExitStack() as ctx:
        def sb(name, shape, dt=F32):
            return ctx.enter_context(nc.sbuf_tensor(name, shape, dt))

        def sem(name):
            return ctx.enter_context(nc.semaphore(name))

        p = sb("p_tokens", [128, HALF])
        junk = [sb(f"p_junk_{m}", [128, HALF], BF16) for m in range(3)]
        own_max = sb("own_max", [128, 1])
        max_row = sb("max_row", [1, EXPERTS])
        max_spread = sb("max_spread", [1, EXPERTS, CHUNKS])
        neg_max = sb("p_neg_max", [128, 1])
        part_sum = sb("part_sum", [128, 1])
        inv_sum = sb("inv_sum", [128, 1])
        ones = sb("p_ones", [128, 128])
        same = sb("same_expert", [128, EXPERTS, CHUNKS])
        same16 = sb("same_expert16", [128, 128], FP16)
        before = sb("chunks_before", [128, EXPERTS, CHUNKS])
        step_back = sb("step_back", [128, 128])
        steps = sb("steps_of_search", [128, 3], I32)
        step_f = sb("step_f", [128, 1])
        found = sb("found", [128, 1], I32)
        trials = sb("trials", [128, 3], I32)
        reached = sb("p_reached", [128, 3])
        digit = sb("digit", [128, 1])
        digit_bits = sb("digit_bits", [128, 1], I32)
        counts16 = sb("counts16", [128, 3], FP16)
        above = sb("above", [128, HALF])
        equal = sb("equal", [128, HALF])
        n_above = sb("n_above", [128, 1])
        limit = sb("limit", [128, 1])
        need = sb("need", [128, 1])
        zeros = sb("p_zeros", [128, HALF])
        rank = sb("rank", [128, HALF])
        chosen = sb("chosen", [128, HALF])
        table = sb("p_table", [128, HALF + 1])
        expert_start_f = sb("expert_start_f", [128, 1])
        starts = sb("starts", [128, 1])
        slot_base = sb("slot_base", [128, EXPERTS], I32)
        slot_base_f = sb("slot_base_f", [128, EXPERTS])
        by_token = sb("by_token", [TILE, CHUNKS, 3, EXPERTS])

        TURN = 3

        ps = ctx.enter_context(nc.psum_tensor("p_ps", [128, 8, 512], F32))

        loaded = sem("p_loaded")
        consts = sem("p_consts")
        rows_made = sem("p_rows_made")
        d = sem("p_vector_steps")
        pe_s = sem("p_products")
        exp_done = sem("p_exp_done")
        neg_max_ready = sem("p_neg_max_ready")
        counted = sem("counted")
        summed = sem("summed")
        stored = sem("p_stored")
        block = ctx.enter_context(nc.Block())

        @block.sync
        def _(sp):
            sp.dma_start(p[:], logits_rows.rearrange("e (c j) -> (e c) j", c=CHUNKS)).then_inc(loaded, 16)
            sp.wait_ge(d, 4)
            with nc.allow_non_contiguous_dma(reason="8 probabilities beside each token's features"):
                sp.dma_start(x2_rows[:, D:ROW0].rearrange("(i q) e -> q i e", q=TILE),
                             by_token[:].rearrange("q c k e -> q (c k) e")).then_inc(stored, 16)
            sp.wait_ge(stored, 16)

        @block.gpsimd
        def _(pool):
            pool.memset(ones[:], 1.0).then_inc(consts, 1)
            pool.memset(zeros[:], 0.0).then_inc(consts, 1)
            pool.iota(steps[:], pattern=[[1, 3]], base=1, channel_multiplier=0).then_inc(consts, 1)
            pool.memset(step_f[:], float(1 << SEARCH_BITS)).then_inc(consts, 1)
            pool.iota(slot_base[:], pattern=[[CAPACITY, EXPERTS]], base=0, channel_multiplier=0).then_inc(consts, 1)
            pool.wait_ge(consts, 5)
            blocks = ones[:].rearrange("p (e c) -> p e c", e=EXPERTS)
            pool.affine_select(out=same[:], in_=blocks, compare_op=ALU.is_ge, fill=0.0, base=0,
                               pattern=[[-CHUNKS, EXPERTS], [0, CHUNKS]], channel_multiplier=1).then_inc(consts, 1)
            pool.wait_ge(consts, 6)
            pool.affine_select(out=same[:], in_=same[:], compare_op=ALU.is_ge, fill=0.0, base=CHUNKS - 1,
                               pattern=[[CHUNKS, EXPERTS], [0, CHUNKS]], channel_multiplier=-1).then_inc(consts, 1)
            pool.wait_ge(consts, 7)
            pool.affine_select(out=before[:], in_=same[:], compare_op=ALU.is_gt, fill=0.0, base=0,
                               pattern=[[CHUNKS, EXPERTS], [1, CHUNKS]], channel_multiplier=-1).then_inc(consts, 1)
            pool.tensor_copy(same16[:], same[:].rearrange("p e c -> p (e c)")).then_inc(consts, 1)
            pool.affine_select(out=step_back[:], in_=T.ident[:], compare_op=ALU.not_equal, fill=-1.0, base=1,
                               pattern=[[-1, 128]], channel_multiplier=1).then_inc(consts, 1)
            pool.iota(T.slot_row[:], pattern=[[1, CAPACITY]], base=0, channel_multiplier=0,
                      allow_small_or_imprecise_dtypes=True).then_inc(rows_made, 1)
            pool.iota(T.slot_col[:], pattern=[[128, EXPERTS * SLOT_TILES]], base=0, channel_multiplier=1,
                      allow_small_or_imprecise_dtypes=True).then_inc(rows_made, 1)
            pool.wait_ge(rows_made, 2)

        @block.tensor
        def _(pe):
            pe.wait_ge(d, 1)
            pe.transpose(ps[0:1, 0, 0:128], own_max[:], T.ident[:]).then_inc(pe_s, 1)
            pe.wait_ge(consts, 10)
            pe.wait_ge(d, 2)
            pe.matmul(ps[:, 1, 0:1], max_spread[:].rearrange("a e c -> a (e c)"), ones[0:1, 0:1],
                      start=True, stop=True).then_inc(pe_s, 1)
            pe.wait_ge(exp_done, 1)
            pe.matmul(ps[:, 2, 0:1], same[:].rearrange("p e c -> p (e c)"), part_sum[:], start=True, stop=True).then_inc(pe_s, 1)
            pe.wait_ge(d, 3)
            for k in range(3):
                mm = pe.transpose(ps[0:TILE, 3, 128 * k:128 * k + 128], p[:, k * TILE:(k + 1) * TILE], T.ident[:])
            mm.then_inc(pe_s, 1)
            with pe.Fori(0, SEARCHES // TURN) as it:
                for j in range(TURN):
                    pe.wait_ge(counted, TURN * it + j + 1)
                    pe.matmul(ps[:, 4, 0:3], same16[:], counts16[:], start=True, stop=True).then_inc(summed, 1)
            pe.wait_ge(d, 5)
            pe.matmul(ps[:, 5, 0:1], same[:].rearrange("p e c -> p (e c)"), n_above[:], start=True, stop=True).then_inc(pe_s, 1)
            pe.wait_ge(d, 6)
            pe.matmul(ps[:, 6, 0:1], before[:].rearrange("p e c -> p (e c)"), rank[:, HALF - 1:HALF],
                      start=True, stop=True).then_inc(pe_s, 1)
            pe.wait_ge(d, 7)
            pe.matmul(ps[:, 7, 0:1], before[:].rearrange("p e c -> p (e c)"), rank[:, HALF - 1:HALF],
                      start=True, stop=True).then_inc(pe_s, 1)
            pe.wait_ge(d, 8)
            pe.matmul(ps[:, 0, 0:HALF + 1], step_back[:], table[:], start=True, stop=True).then_inc(pe_s, 1)

        @block.scalar
        def _(act):
            act.wait_ge(neg_max_ready, 1)
            act.activation(p[:], p[:], ACT.Exp, bias=neg_max[:, 0:1], accum_out=part_sum[:]).then_inc(exp_done, 1)

        @block.vector
        def _(dve):
            dve.wait_ge(loaded, 16)
            dve.tensor_reduce(own_max[:], p[:], AX.X, ALU.max).then_inc(d, 1)
            dve.wait_ge(pe_s, 1)
            dve.tensor_reduce(max_row[:], ps[0:1, 0, 0:128].rearrange("a (e c) -> a e c", e=EXPERTS), AX.X, ALU.max)
            dve.drain()
            dve.tensor_copy(max_spread[:], max_row[:, :].unsqueeze(2).to_broadcast([1, EXPERTS, CHUNKS])).then_inc(d, 1)
            dve.wait_ge(pe_s, 2)
            dve.tensor_scalar(neg_max[:], ps[:, 1, 0:1], -1.0, None, ALU.mult).then_inc(neg_max_ready, 1)
            dve.wait_ge(consts, 10)
            dve.tensor_scalar(steps[:], steps[:], SEARCH_BITS - 2, None, ALU.logical_shift_left)
            dve.memset(found[:], 0)
            dve.memset(digit_bits[:], 0)
            dve.tensor_copy(slot_base_f[:], slot_base[:])
            dve.wait_ge(pe_s, 3)
            dve.reciprocal(inv_sum[:], ps[:, 2, 0:1])
            dve.drain()
            dve.tensor_scalar(p[:], p[:], inv_sum[:, 0:1], None, ALU.mult).then_inc(d, 1)
            dve.tensor_copy(trials[:], steps[:])
            dve.wait_ge(pe_s, 4)
            dve.tensor_copy(by_token[:].rearrange("q c k e -> q k e c"),
                            ps[0:TILE, 3, 0:384].rearrange("q (k e c) -> q k e c", k=3, e=EXPERTS)).then_inc(d, 1)

            with dve.Fori(0, SEARCHES // TURN) as it:
                for j in range(TURN):
                    dve.drain()
                    dve.tensor_tensor(found[:], found[:], digit_bits[:], ALU.bitwise_or)
                    for m in range(3):
                        count = dve.tensor_scalar(junk[m][:], p[:], trials[:].bitcast(F32)[:, m:m + 1], None, ALU.is_ge, ALU.add,
                                                  accum_out=counts16[:, m:m + 1])
                    count.then_inc(counted, 1)
                    dve.tensor_scalar(step_f[:], step_f[:], 0.25, None, ALU.mult)
                    dve.tensor_scalar(steps[:], steps[:], 2, None, ALU.logical_shift_right)
                    dve.wait_ge(summed, TURN * it + j + 1)
                    dve.tensor_scalar(reached[:], ps[:, 4, 0:3], float(CAPACITY), None, ALU.is_ge, ALU.add, accum_out=digit[:])
                    dve.drain()
                    dve.tensor_scalar(digit_bits[:], digit[:], step_f[:, 0:1], None, ALU.mult)
                    dve.drain()
                    dve.scalar_tensor_tensor(trials[:], steps[:], digit_bits[:, 0:1], found[:, :].to_broadcast([128, 3]),
                                             ALU.bitwise_or, ALU.bitwise_or)
            dve.drain()
            dve.tensor_tensor(found[:], found[:], digit_bits[:], ALU.bitwise_or)
            dve.drain()
            least = found[:].bitcast(F32)
            dve.tensor_scalar(above[:], p[:], least[:, 0:1], None, ALU.is_gt, ALU.add, accum_out=n_above[:]).then_inc(d, 1)
            dve.tensor_scalar(equal[:], p[:], least[:, 0:1], None, ALU.is_equal)
            dve.wait_ge(pe_s, 5)
            dve.tensor_scalar(need[:], ps[:, 5, 0:1], -1.0, float(CAPACITY), ALU.mult, ALU.add)
            dve.drain()
            dve.tensor_tensor_scan(rank[:], equal[:], zeros[:], 0.0, ALU.add, ALU.add).then_inc(d, 1)
            dve.wait_ge(pe_s, 6)
            dve.scalar_tensor_tensor(limit[:], ps[:, 6, 0:1], -1.0, need[:], ALU.mult, ALU.add)
            dve.drain()
            dve.scalar_tensor_tensor(chosen[:], rank[:], limit[:, 0:1], equal[:], ALU.is_le, ALU.mult)
            dve.drain()
            dve.tensor_tensor(chosen[:], chosen[:], above[:], ALU.add)
            dve.drain()
            dve.tensor_tensor_scan(rank[:], chosen[:], zeros[:], 0.0, ALU.add, ALU.add).then_inc(d, 1)
            dve.tensor_copy(expert_start_f[:], T.expert_start[:])
            dve.tensor_copy(table[:, HALF:HALF + 1], T.chunk_of[:])
            dve.wait_ge(pe_s, 7)
            dve.drain()
            dve.tensor_tensor(starts[:], ps[:, 7, 0:1], expert_start_f[:], ALU.add)
            dve.drain()
            dve.tensor_scalar(table[:, 0:HALF], rank[:], starts[:, 0:1], None, ALU.add).then_inc(d, 1)
            dve.tensor_scalar(T.start_of[:], slot_base_f[:], -1.0, starts[:, 0:1], ALU.mult, ALU.add)
            dve.wait_ge(pe_s, 8)
            dve.tensor_copy(T.steps[:], ps[:, 0, 0:HALF + 1])
            dve.drain()


def experts_by_token_choice(nc, T, x2_rows, h2_rows, w1, b1, w2, b2):
    GROUP = 4
    GROUPS = EXPERTS * CAPACITY // (GROUP * 128)
    TURN = 4
    LOOK_AHEAD, GATHER_AHEAD = 2, 3
    with ExitStack() as ctx:
        def sb(name, shape, dt=F32):
            return ctx.enter_context(nc.sbuf_tensor(name, shape, dt))

        def sem(name):
            return ctx.enter_context(nc.semaphore(name))

        w1_sb = [sb(f"c_w1_{i}", [D, HIDDEN]) for i in range(2)]
        w2_sb = [sb(f"c_w2_{i}", [128, F_TILES, D]) for i in range(2)]
        b2_sb = [sb(f"c_b2_{i}", [128, D]) for i in range(2)]
        b1_sb = [sb(f"c_b1_{i}", [128, F_TILES]) for i in range(2)]
        reached = [sb(f"reached_{i}", [128, CAPACITY], FP16) for i in range(2)]
        junk = sb("c_junk", [128, HALF], BF16)
        count = sb("c_count", [128, 2])
        ids = sb("c_ids", [128, TURN, GROUP], I32)
        ids_out = sb("c_ids_out", [128, TURN, GROUP], I32)
        xs = sb("c_xs", [128, TURN, GROUP, ROW0])
        xsT = sb("c_xsT", [D, GROUP * 128])
        hT = sb("c_hT", [128, 2, F_TILES, GROUP * 128])
        ysum = sb("c_ysum", [128, GROUP, D])
        ys = sb("c_ys", [128, TURN, GROUP, D])

        ps = ctx.enter_context(nc.psum_tensor("c_ps", [128, 8, 512], F32))
        ps_look = ps[:, 0:2, 0:HALF + 1]
        ps_x = ps[:, 2, :]
        ps_h = ps[:, 4:6, :]
        ps_y = ps[:, 6:8, :]

        w_loaded = [sem(f"c_w_loaded_{i}") for i in range(2)]
        reached_ready = sem("c_reached_ready")
        look_done, ids_ready = sem("c_look_done"), sem("c_ids_ready")
        gathered = [sem(f"c_gathered_{i}") for i in range(TURN)]
        scattered = [sem(f"c_scattered_{i}") for i in range(TURN)]
        xT_done, xT_ready = sem("c_xT_done"), sem("c_xT_ready")
        h_done, h_ready = sem("c_h_done"), sem("c_h_ready")
        y_done, y_read, y_scaled = sem("c_y_done"), sem("c_y_read"), sem("c_y_scaled")
        block = ctx.enter_context(nc.Block())

        def wait(eng, semaphore, value):
            if not isinstance(value, int) or value > 0:
                eng.wait_ge(semaphore, value)

        def turns(eng, turn):
            turn(0, True, False)
            with eng.Fori(1, GROUPS // TURN - 1) as it:
                turn(it, False, False)
            turn(GROUPS // TURN - 1, False, True)

        @block.sync
        def _(sp):
            def load(e, parity):
                e = bass.ds(e, 1)
                sp.dma_start(b1_sb[parity][:], b1[e].rearrange("a p f -> (a p) f")).then_inc(w_loaded[parity], 16)
                sp.dma_start(w1_sb[parity][:], w1[e].rearrange("a d f -> (a d) f")).then_inc(w_loaded[parity], 16)
                sp.dma_start(w2_sb[parity][:], w2[e].rearrange("a (f p) d -> p (a f) d", p=128)).then_inc(w_loaded[parity], 16)
                sp.dma_start(b2_sb[parity][:], b2[e, :].rearrange("a d -> (a d)").partition_broadcast(128)).then_inc(w_loaded[parity], 16)

            load(0, 0)
            load(1, 1)
            with sp.Fori(1, GROUPS // TURN) as it:
                for parity in range(2):
                    sp.wait_ge(y_read, TURN * (it - 1) + 2 * parity + 2)
                    load(2 * it + parity, parity)

        @block.gpsimd
        def _(pool):
            found_next = pool.alloc_register("found_next")
            scaled_next = pool.alloc_register("scaled_next")
            pool.reg_mov(found_next, GROUP)
            pool.reg_mov(scaled_next, 1)

            def gather(it, j):
                G = TURN * it + j
                wait(pool, y_scaled, G - TURN + 1)
                pool.wait_ge(ids_ready, found_next)
                pool.reg_add(found_next, found_next, GROUP)
                for i in range(GROUP):
                    pool.indirect_dma_start(
                        out=xs[:, j, i, :], out_offset=None, in_=x2_rows[:, :],
                        in_offset=bass.IndirectOffsetOnAxis(ap=ids[:, j, i:i + 1], axis=0)).then_inc(gathered[j], 16)

            def scatter(it, j):
                G = TURN * it + j
                if j % 2 == 0:
                    before = (j - 1) % TURN
                    for last in (before, before - 1):
                        wait(pool, scattered[last], 64 * (it + 1 if j else it))
                pool.wait_ge(y_scaled, G + 1 if isinstance(G, int) and it else scaled_next)
                pool.reg_add(scaled_next, scaled_next, 1)
                for i in range(GROUP):
                    pool.indirect_dma_start(
                        out=h2_rows[:, :], out_offset=bass.IndirectOffsetOnAxis(ap=ids_out[:, j, i:i + 1], axis=0),
                        in_=ys[:, j, i, :], in_offset=None, compute_op=ALU.add).then_inc(scattered[j], 16)

            def turn(it, first, last):
                for j in range(TURN):
                    if not (last and j + GATHER_AHEAD >= TURN):
                        ahead = j + GATHER_AHEAD
                        gather(it + ahead // TURN, ahead % TURN)
                    scatter(it, j)

            for j in range(GATHER_AHEAD):
                gather(0, j)
            turns(pool, turn)
            for j in range(TURN):
                pool.wait_ge(scattered[j], 64 * (GROUPS // TURN))

        @block.tensor
        def _(pe):
            def look(it, j, i):
                G = TURN * it + j
                t = GROUP * G + i
                if i == 0 and j % 2 == 0:
                    pe.wait_ge(reached_ready, 2 * it + j // 2 + 1)
                wait(pe, ids_ready, t - 1)
                at = 128 * (GROUP * (j % 2) + i)
                pe.matmul(ps_look[:, i % 2, :], reached[j // 2][:, at:at + 128], T.steps[:], start=True, stop=True)\
                    .then_inc(look_done, 1)

            def turn_x(it, j):
                G = TURN * it + j
                pe.wait_ge(gathered[j], 64 * (it + 1))
                wait(pe, xT_ready, G)
                for i in range(GROUP):
                    mm = pe.transpose(ps_x[:, 128 * i:128 * i + 128], xs[:, j, i, 0:D], T.ident[:])
                mm.then_inc(xT_done, 1)

            def hidden(it, j, f):
                G = TURN * it + j
                n = F_TILES * G + f
                if f == 0:
                    pe.wait_ge(xT_ready, G + 1)
                    pe.wait_ge(w_loaded[j // 2], 64 * (it + 1))
                wait(pe, h_ready, n - 1)
                pe.matmul(ps_h[:, f % 2, :], w1_sb[j // 2][:, 128 * f:128 * f + 128], xsT[:], start=True, stop=True)\
                    .then_inc(h_done, 1)

            def output(it, j):
                G = TURN * it + j
                pe.wait_ge(h_ready, F_TILES * (G + 1))
                wait(pe, y_read, G - 1)
                for i in range(GROUP):
                    for f in range(F_TILES):
                        mm = pe.matmul(ps_y[:, j % 2, 128 * i:128 * i + 128], hT[:, j % 2, f, 128 * i:128 * i + 128],
                                       w2_sb[j // 2][:, f, :], start=(f == 0), stop=(f == F_TILES - 1))
                mm.then_inc(y_done, 1)

            def turn(it, first, last):
                for j in range(TURN):
                    for f in range(F_TILES):
                        hidden(it, j, f)
                        if not (last and j + LOOK_AHEAD >= TURN):
                            ahead = j + LOOK_AHEAD
                            look(it + ahead // TURN, ahead % TURN, f)
                    if not (last and j == TURN - 1):
                        turn_x(it + (j + 1) // TURN, (j + 1) % TURN)
                    if not (first and j == 0):
                        output(it - (j == 0), (j - 1) % TURN)

            for j in range(LOOK_AHEAD):
                for i in range(GROUP):
                    look(0, j, i)
            turn_x(0, 0)
            turns(pe, turn)
            output(GROUPS // TURN - 1, TURN - 1)

        @block.scalar
        def _(act):
            def move_x(it, j):
                act.wait_ge(xT_done, TURN * it + j + 1)
                act.copy(xsT[:], ps_x).then_inc(xT_ready, 1)

            def turn(it, first, last):
                for j in range(TURN):
                    G = TURN * it + j
                    for f in range(F_TILES):
                        if f == 0:
                            wait(act, y_done, G - 1)
                        act.wait_ge(h_done, F_TILES * G + f + 1)
                        act.activation(hT[:, j % 2, f, :], ps_h[:, f % 2, :], ACT.Gelu,
                                       bias=b1_sb[j // 2][:, f:f + 1]).then_inc(h_ready, 1)
                    if not (last and j == TURN - 1):
                        move_x(it + (j + 1) // TURN, (j + 1) % TURN)

            move_x(0, 0)
            turns(act, turn)

        @block.vector
        def _(dve):
            def reach(it, parity):
                e = 2 * it + parity
                wait(dve, look_done, SLOT_TILES * (e - 1))
                dve.tensor_scalar(reached[parity][:], T.slot_row[:], T.start_of[:, bass.ds(e, 1)], None, ALU.is_ge)\
                    .then_inc(reached_ready, 1)

            def find(it, j):
                G = TURN * it + j
                for i in range(GROUP):
                    t = GROUP * G + i
                    dve.wait_ge(look_done, t + 1)
                    dve.tensor_scalar(junk[:], ps_look[:, i % 2, 0:HALF], T.slot_col[:, bass.ds(t, 1)], None,
                                      ALU.is_le, ALU.add, accum_out=count[:, i % 2:i % 2 + 1])
                    dve.drain()
                    if i == 0:
                        wait(dve, gathered[j], 64 * it)
                    dve.scalar_tensor_tensor(ids[:, j, i:i + 1], ps_look[:, i % 2, HALF:HALF + 1], float(HALF),
                                             count[:, i % 2:i % 2 + 1], ALU.mult, ALU.add).then_inc(ids_ready, 1)

            def scale(it, j):
                G = TURN * it + j
                wait(dve, y_scaled, G)
                dve.wait_ge(y_done, G + 1)
                dve.tensor_tensor(ysum[:], ps_y[:, j % 2, :].rearrange("p (i d) -> p i d", d=D),
                                  b2_sb[j // 2][:, :].unsqueeze(1).to_broadcast([128, GROUP, D]), ALU.add).then_inc(y_read, 1)
                dve.drain()
                wait(dve, scattered[j], 64 * it)
                dve.tensor_copy(ids_out[:, j, :], ids[:, j, :])
                dve.tensor_tensor(ys[:, j], ysum[:], xs[:, j, :, bass.ds(D + 2 * it + j // 2, 1)].to_broadcast([128, GROUP, D]),
                                  ALU.mult).then_inc(y_scaled, 1)

            def turn(it, first, last):
                for j in range(TURN):
                    if not (last and j + LOOK_AHEAD >= TURN):
                        ahead = j + LOOK_AHEAD
                        find(it + ahead // TURN, ahead % TURN)
                    if not (first and j == 0):
                        scale(it - (j == 0), (j - 1) % TURN)
                    if j % 2 and not last:
                        reach(it + 1, j // 2)

            for j in range(LOOK_AHEAD):
                reach(0, j)
                find(0, j)
            turns(dve, turn)
            scale(GROUPS // TURN - 1, TURN - 1)


def sigmoid_attention(nc, T, h3_rows, w_q, b_q, w_k, b_k, w_v, b_v, w_o, b_o, w_r, b_r, split_q, split_k, moe_rows,
                      w1, w1_sb, w2, w2_sb):
    with ExitStack() as ctx:
        def sb(name, shape, dt=F32):
            return ctx.enter_context(nc.sbuf_tensor(name, shape, dt))

        def sem(name):
            return ctx.enter_context(nc.semaphore(name))

        STEPS = 2 * STEPS_OF_GROUP
        GROUP_HEADS = HEADS // 2
        WEIGHT_RING = 3
        CUT = 188
        MAKE_AT = (5, 6, 7, 8, 9, 10, 11, 12, 13)
        CLOSE_AT = (2, 3, 4, 6, 7, 8, 10, 12)
        SPLIT_AT = ((9, 10), (14, 15))
        MAKES, CLOSES = 9, 8
        LOADS = 10

        wq_sb, wk_sb, wv_sb = sb("d_w_q", [D, D]), sb("d_w_k", [D, D]), sb("d_w_v", [D, D])
        bq_sb, bk_sb = sb("d_b_q", [D, 1]), sb("d_b_k", [D, 1])
        bv_sb, bo_sb = sb("d_b_v", [TILE, D]), sb("d_b_o", [TILE, D])
        wo_sb = sb("d_w_o", [128, 2, D])
        wr_sb = sb("d_w_r", [D, 64])
        br_sb = sb("d_b_r", [TILE, EXPERTS])

        xn = sb("d_xn", [TILE, TILES, D])
        xnT = sb("d_xnT", [D, SEQ])
        qk = sb("d_qk", [D, 2, SEQ])
        rest = sb("d_rest", [D, SEQ])
        parts = sb("d_parts", [D, 2, PARTS, SEQ], BF16)
        qs = sb("d_qs", [HEAD_D * SLOTS, HEADS, SEQ], BF16)
        ks = sb("d_ks", [HEAD_D * SLOTS, HEADS, SEQ], BF16)
        v = sb("d_v", [TILE, TILES, D])
        v_wide = sb("d_v_wide", [TILE, TILES, HEADS, 32])
        weights = sb("d_weights", [TILE, WEIGHT_RING, GROUP_HEADS, HALF])
        ao = sb("d_ao", [128, 2, SEQ])
        hb = sb("d_hb", [TILE, TILES, D])
        rows = sb("d_rows", [TILE, TILES, ROW1])
        x4T = sb("d_x4T", [D, SEQ])
        st1, st2 = sb("d_st1", [TILE, TILES, 6]), sb("d_st2", [TILE, TILES, 6])
        mv1, mv2 = sb("d_mv1", [TILE, TILES, 2]), sb("d_mv2", [TILE, TILES, 2])
        ve1, ve2 = sb("d_ve1", [TILE, TILES]), sb("d_ve2", [TILE, TILES])
        rs1, rs2 = sb("d_rs1", [TILE, TILES]), sb("d_rs2", [TILE, TILES])
        logits = sb("d_logits", [TILE, TILES, EXPERTS])
        best = sb("d_best", [TILE, TILES])
        first = sb("d_first", [TILE, TILES, EXPERTS])
        backwards = sb("d_backwards", [TILE, EXPERTS])
        chosen = sb("d_chosen", [TILE, TILES, EXPERTS], BF16)
        filled = sb("d_filled", [128, TILES + 1, EXPERTS])
        place_f = sb("d_place_f", [TILE, TILES])
        place = sb("d_place", [TILE, TILES], I32)
        region_i = sb("d_region_i", [128, EXPERTS], I32)
        backwards_i = sb("d_backwards_i", [TILE, EXPERTS], I32)
        token_i = sb("d_token_i", [TILE, TILES], I32)
        earlier = sb("d_earlier", [TILE, TILE], BF16)
        ones = sb("d_ones", [TILE, 128], BF16)

        ps = ctx.enter_context(nc.psum_tensor("d_ps", [128, 8, 512], F32))
        ps_scores = [ps[0:TILE, 2 * u:2 * u + 2, 0:HALF] for u in range(2)]
        ps_ao = [ps[:, 4 + m, 0:HALF] for m in range(2)]
        ps_make, ps_close = ps[:, 6, :], ps[:, 7, :]

        loaded = sem("d_loaded")
        h3_first_loaded, h3_loaded = sem("d_h3_first_loaded"), sem("d_h3_loaded")
        experts_loaded = sem("d_experts_loaded")
        zeroed, consts = sem("d_zeroed"), sem("d_consts")
        ve1_done, rs1_done = sem("d_ve1_done"), sem("d_rs1_done")
        ve2_done, rs2_done = sem("d_ve2_done"), sem("d_rs2_done")
        xn_ready = sem("d_xn_ready")
        make_done, make_read = sem("d_make_done"), sem("d_make_read")
        close_done, close_read = sem("d_close_done"), sem("d_close_read")
        split_ready = sem("d_split_ready")
        split_stored = sem("d_split_stored")
        stack_loaded = [sem(f"d_stack_loaded_{g}") for g in range(2)]
        v_ready = sem("d_v_ready")
        scores_done, weights_ready = sem("d_scores_done"), sem("d_weights_ready")
        av_done, ao_ready = sem("d_av_done"), sem("d_ao_ready")
        hb_ready, h4_ready = sem("d_hb_ready"), sem("d_h4_ready")
        x4_ready, chosen_ready = sem("d_x4_ready"), sem("d_chosen_ready")
        place_ready, placed = sem("d_place_ready"), sem("d_placed")
        block = ctx.enter_context(nc.Block())

        def wait(eng, semaphore, value):
            if not isinstance(value, int) or value > 0:
                eng.wait_ge(semaphore, value)

        def make_bank(n, alone):
            return ps[:, 0, :] if alone and n % 2 else ps_make

        def sequences(eng, step, needs_residual=False):
            step(-1, True, False, False)
            if needs_residual:
                eng.wait_ge(h3_loaded, 16 * (BATCH - 1))
                eng.wait_ge(loaded, 16 * LOADS)
            step(0, True, True, False)
            step(1, True, True, True)
            with eng.Fori(2, BATCH - 1) as b:
                step(b, True, True, True)
            step(BATCH - 1, False, True, True)
            step(BATCH, False, False, True)

        @block.sync
        def _(sp):
            for n in range(BATCH):
                sp.dma_start(T.resid[:, n * TILES:(n + 1) * TILES, :], tile_layout(h3_rows[n * SEQ:(n + 1) * SEQ, :]))\
                    .then_inc(h3_loaded if n else h3_first_loaded, 16)
                if n == 0:
                    sp.dma_start(wq_sb[:], w_q[:, :]).then_inc(loaded, 16)
                    sp.dma_start(wk_sb[:], w_k[:, :]).then_inc(loaded, 16)
                    sp.dma_start(wv_sb[:], w_v[:, :]).then_inc(loaded, 16)
                    sp.dma_start(bq_sb[:], b_q[:, :]).then_inc(loaded, 16)
                    sp.dma_start(bk_sb[:], b_k[:, :]).then_inc(loaded, 16)
                    sp.dma_start(bv_sb[:], b_v.partition_broadcast(TILE)).then_inc(loaded, 16)
                    sp.dma_start(bo_sb[:], b_o.partition_broadcast(TILE)).then_inc(loaded, 16)
                    sp.dma_start(br_sb[:], b_r.partition_broadcast(TILE)).then_inc(loaded, 16)
                    sp.wait_ge(zeroed, 3)
                    sp.dma_start(wo_sb[:], w_o[:, :, :]).then_inc(loaded, 16)
                    with nc.allow_non_contiguous_dma(reason="8 columns of 64"):
                        sp.dma_start(wr_sb[:, 0:EXPERTS], w_r[:, :]).then_inc(loaded, 16)

            def store_split(b):
                wait(sp, stack_loaded[0], 96 * b)
                wait(sp, stack_loaded[1], 96 * b)
                for n, to in enumerate((split_q, split_k)):
                    sp.wait_ge(split_ready, 2 * b + n + 1)
                    sp.dma_start(to.rearrange("s r t -> r s t"), parts[:, n]).then_inc(split_stored, 16)

            def load_stack(b, g):
                sp.wait_ge(split_stored, 32 * (b + 1))
                wait(sp, scores_done, 2 * (STEPS * (b - 1) + STEPS_OF_GROUP * (g + 1)))
                heads = slice(GROUP_HEADS * g, GROUP_HEADS * (g + 1))
                q_rows = split_q.rearrange("s (r h) t -> (s r) h t", h=HEADS)
                k_rows = split_k.rearrange("s (r h) t -> (s r) h t", h=HEADS)
                R = HEAD_D
                for at, n, k_from in ((0, 3, 0), (3, 2, 1), (5, 1, 2)):
                    sp.dma_start(qs[R * at:R * (at + n), heads, :], q_rows[0:R * n, heads, :]).then_inc(stack_loaded[g], 16)
                    sp.dma_start(ks[R * at:R * (at + n), heads, :], k_rows[R * k_from:R * (k_from + n), heads, :])\
                        .then_inc(stack_loaded[g], 16)

            def step(b, has_make, has_attend, has_close):
                if has_make:
                    store_split(b + 1)
                    load_stack(b + 1, 0)
                    load_stack(b + 1, 1)

            step(-1, True, False, False)
            sp.dma_start(w1_sb[:].rearrange("p (e f) -> p e f", e=EXPERTS), w1.rearrange("e p f -> p e f"))\
                .then_inc(experts_loaded, 16)
            sp.dma_start(w2_sb[:].rearrange("p (e f d) -> p e f d", e=EXPERTS, f=F_TILES),
                         w2.rearrange("e (f p) d -> p e f d", p=128)).then_inc(experts_loaded, 16)
            step(0, True, True, False)
            step(1, True, True, True)
            with sp.Fori(2, BATCH - 1) as b:
                step(b, True, True, True)
            sp.wait_ge(experts_loaded, 32)

        @block.tensor
        def _(pe):
            def make(b, n, alone):
                bank = make_bank(n, alone)
                wait(pe, make_read, MAKES * b + (n if not alone else max(n - 1, 3 if n >= 3 else 0)))
                if n < 3:
                    pe.wait_ge(xn_ready, PAIRS * b + n + 1)
                    for i in (2 * n, 2 * n + 1):
                        mm = pe.transpose(bank[:, 128 * (i % 2):128 * (i % 2) + TILE], xn[:, i, :], T.ident[0:TILE, 0:TILE])
                elif n < 7:
                    w, h = (wq_sb, wk_sb)[(n - 3) // 2], (n - 3) % 2
                    mm = pe.matmul(bank[:, 0:HALF], w[:], xnT[:, h * HALF:(h + 1) * HALF], start=True, stop=True)
                else:
                    for i in range(3):
                        at = TILE * (3 * (n - 7) + i)
                        mm = pe.matmul(bank[0:TILE, 128 * i:128 * i + 128], xnT[:, at:at + TILE], wv_sb[:], start=True, stop=True)
                mm.then_inc(make_done, 1)

            def close(b, n):
                wait(pe, close_read, CLOSES * b + n)
                if n < 3:
                    pe.wait_ge(ao_ready, 4 * (b + 1))
                    for i in (2 * n, 2 * n + 1):
                        for g in range(2):
                            mm = pe.matmul(ps_close[0:TILE, 128 * (i % 2):128 * (i % 2) + 128], ao[:, g, i * TILE:(i + 1) * TILE],
                                           wo_sb[:, g, :], start=(g == 0), stop=(g == 1))
                elif n < 6:
                    pe.wait_ge(x4_ready, PAIRS * b + n - 2)
                    for i in (2 * n - 6, 2 * n - 5):
                        mm = pe.transpose(ps_close[:, 128 * (i % 2):128 * (i % 2) + TILE], rows[:, i, 0:D], T.ident[0:TILE, 0:TILE])
                elif n == 6:
                    for i in range(TILES):
                        mm = pe.matmul(ps_close[0:TILE, 64 * i:64 * i + 64], x4T[:, i * TILE:(i + 1) * TILE], wr_sb[:], start=True, stop=True)
                else:
                    pe.wait_ge(chosen_ready, b + 1)
                    which = chosen[:].rearrange("p i e -> p (i e)")
                    pe.matmul(ps_close[0:TILE, 0:TILES * EXPERTS], earlier[:], which, start=True, stop=True)
                    mm = pe.matmul(ps_close[:, 64:64 + TILES * EXPERTS], ones[:], which, start=True, stop=True)
                mm.then_inc(close_done, 1)

            def scores(b, s, u):
                g, half, i = s // STEPS_OF_GROUP, s % STEPS_OF_GROUP // TILES, s % TILES
                if s % STEPS_OF_GROUP == 0 and u == 0:
                    pe.wait_ge(stack_loaded[g], 96 * (b + 1))
                wait(pe, weights_ready, 2 * (STEPS * b + s) + u - 1)
                for j in range(2):
                    head = GROUP_HEADS * g + 2 * u + j
                    mm = pe.matmul(ps_scores[u][:, j, :], ks[:, head, i * TILE:(i + 1) * TILE],
                                   qs[:, head, half * HALF:(half + 1) * HALF], start=True, stop=True)
                mm.then_inc(scores_done, 1)

            def values(b, s, u):
                g, i = s // STEPS_OF_GROUP, s % TILES
                m = s // TILES
                if u == 0:
                    if s % STEPS_OF_GROUP == 0:
                        pe.wait_ge(v_ready, 2 * b + g + 1)
                    if i == 0:
                        wait(pe, ao_ready, 4 * b + m - 1)
                    pe.wait_ge(weights_ready, 2 * (STEPS * b + s) + 2)
                columns = (slice(0, CUT), slice(CUT, HALF))[u]
                if i == 0:
                    if u == 1:
                        return
                    columns = slice(0, HALF)
                for j in range(GROUP_HEADS):
                    mm = pe.matmul(ps_ao[m % 2][32 * j:32 * j + 32, columns], v_wide[:, i, GROUP_HEADS * g + j, :],
                                   weights[:, s % WEIGHT_RING, j, columns], start=(i == 0), stop=(i == TILES - 1 and u == 1),
                                   tile_position=(0, 32 * j))
                if u == 1 or i == 0:
                    mm.then_inc(av_done, 1)

            def step(b, has_make, has_attend, has_close):
                for s in range(STEPS):
                    for u in range(2):
                        if has_attend and s < STEPS - 1:
                            scores(b, s + 1, u)
                        elif has_attend and has_make:
                            scores(b + 1, 0, u)
                        if s == 0 and has_close:
                            values(b - 1, STEPS - 1, u)
                        if s > 0 and has_attend:
                            values(b, s - 1, u)
                    if has_make and s in MAKE_AT:
                        make(b + 1, MAKE_AT.index(s), not has_attend)
                    if has_close and s in CLOSE_AT:
                        close(b - 1, CLOSE_AT.index(s))
                if has_make and not has_attend:
                    pe.wait_ge(make_read, MAKES)
                    for u in range(2):
                        scores(b + 1, 0, u)

            pe.wait_ge(loaded, 16 * LOADS)
            pe.wait_ge(consts, 5)
            sequences(pe, step)

        @block.scalar
        def _(act):
            def step(b, has_make, has_attend, has_close):
                if not has_attend:
                    return
                for s in range(STEPS):
                    n = STEPS * b + s
                    for u in range(2):
                        if u == 0:
                            wait(act, av_done, n - WEIGHT_RING + 1)
                        act.wait_ge(scores_done, 2 * n + u + 1)
                        act.activation(weights[:, s % WEIGHT_RING, 2 * u:2 * u + 2, :], ps_scores[u], ACT.Sigmoid, scale=HEAD_D ** -0.5)\
                            .then_inc(weights_ready, 1)

            sequences(act, step)

        @block.gpsimd
        def _(pool):
            for to in (wo_sb, wr_sb, v_wide):
                pool.memset(to[:], 0.0).then_inc(zeroed, 1)
            pool.memset(ones[:], 1.0).then_inc(zeroed, 1)
            pool.iota(region_i[:], pattern=[[REGION, EXPERTS]], base=0, channel_multiplier=0).then_inc(consts, 1)
            pool.iota(backwards_i[:], pattern=[[-1, EXPERTS]], base=EXPERTS, channel_multiplier=0).then_inc(consts, 1)
            pool.iota(token_i[:], pattern=[[TILE, TILES]], base=0, channel_multiplier=1).then_inc(consts, 1)
            pool.wait_ge(zeroed, 4)
            pool.affine_select(out=earlier[:], in_=ones[:, 0:TILE], compare_op=ALU.is_gt, fill=0.0, base=0,
                               pattern=[[1, TILE]], channel_multiplier=-1).then_inc(consts, 1)
            pool.memset(T.blank[:], 0.0).then_inc(zeroed, 1)
            pool.wait_ge(zeroed, 5)
            pool.memset(T.blank[:, 2 * D:ROW1], float(NO_TOKEN)).then_inc(consts, 1)

            place_next = pool.alloc_register("place_next")
            pool.reg_mov(place_next, 1)

            def step(b, has_make, has_attend, has_close):
                if has_close:
                    c = b - 1
                    wait(pool, h4_ready, PAIRS * c)
                    pool.tensor_tensor(hb[:], T.resid[:, bass.ds(TILES * c, TILES), :],
                                       bo_sb[:, :].unsqueeze(1).to_broadcast([TILE, TILES, D]), ALU.add).then_inc(hb_ready, 1)
                if has_make:
                    pool.wait_ge(ve1_done, b + 2)
                    pool.tensor_tensor(rs1[:], ve1[:], T.minus_half[0:TILE, 0:TILES], ALU.pow).then_inc(rs1_done, 1)
                if has_close:
                    c = b - 1
                    for g in range(PAIRS):
                        pool.wait_ge(ve2_done, PAIRS * c + g + 1)
                        pool.tensor_tensor(rs2[:, 2 * g:2 * g + 2], ve2[:, 2 * g:2 * g + 2],
                                           T.minus_half[0:TILE, 0:2], ALU.pow).then_inc(rs2_done, 1)
                    pool.wait_ge(place_ready, b if isinstance(b, int) and b == BATCH else place_next)
                    pool.reg_add(place_next, place_next, 1)
                    for i in range(TILES):
                        pool.indirect_dma_start(
                            out=moe_rows[:, :], out_offset=bass.IndirectOffsetOnAxis(ap=place[:, i:i + 1], axis=0),
                            in_=rows[:, i, :], in_offset=None,
                            bounds_check=EXPERTS * REGION - 1, oob_is_err=False).then_inc(placed, 16)

            sequences(pool, step, needs_residual=True)
            pool.wait_ge(placed, 16 * ALL_TILES)

        @block.vector
        def _(dve):
            def resid_tile(n):
                return T.resid[:, bass.ds(n, 1), :].rearrange("p a d -> p (a d)")

            def pair(ap, g):
                return ap[:, 2 * g:2 * g + 2]

            def make_stats(b):
                dve.drain()
                for t in range(TILES):
                    dve.bn_stats(st1[:, t, :], resid_tile(TILES * b + t))
                dve.drain()
                for t in range(TILES):
                    dve.bn_aggr(mv1[:, t, :], st1[:, t, :])
                dve.drain()
                dve.tensor_scalar(ve1[:], mv1[:, :, 1], LN_EPS, None, ALU.add).then_inc(ve1_done, 1)

            def make_norm(b):
                dve.wait_ge(rs1_done, b + 1)
                wait(dve, make_done, MAKES * (b - 1) + PAIRS)
                for t in range(TILES):
                    norm = dve.tensor_scalar(xn[:, t, :], resid_tile(TILES * b + t), mv1[:, t, 0:1], rs1[:, t:t + 1],
                                             ALU.subtract, ALU.mult)
                    if t % 2:
                        norm.then_inc(xn_ready, 1)

            def make(b, n, alone):
                bank = make_bank(n, alone)
                dve.wait_ge(make_done, MAKES * b + n + 1)
                if n < 3:
                    dve.tensor_copy(xnT[:, 2 * n * TILE:(2 * n + 2) * TILE].rearrange("p (s t) -> p s t", s=2),
                                    bank[:, 0:256].rearrange("p (s t) -> p s t", s=2)[:, :, 0:TILE]).then_inc(make_read, 1)
                elif n < 7:
                    which, h = (n - 3) // 2, (n - 3) % 2
                    dve.tensor_scalar(qk[:, which, h * HALF:(h + 1) * HALF], bank[:, 0:HALF], (bq_sb, bk_sb)[which][:, 0:1],
                                      None, ALU.add).then_inc(make_read, 1)
                else:
                    i = 3 * (n - 7)
                    dve.tensor_tensor(v[:, i:i + 3, :], bank[0:TILE, 0:3 * D].rearrange("p (i d) -> p i d", d=D),
                                      bv_sb[:, :].unsqueeze(1).to_broadcast([TILE, 3, D]), ALU.add).then_inc(make_read, 1)

            def split(b, which, stage):
                order = (0, 1, 2) if which == 0 else (2, 1, 0)
                part = [parts[:, which, n, :] for n in order]
                dve.drain()
                if stage == 0:
                    wait(dve, split_stored, 32 * b)
                    dve.tensor_copy(part[0], qk[:, which, :])
                    dve.drain()
                    dve.tensor_tensor(rest[:], qk[:, which, :], part[0], ALU.subtract)
                else:
                    dve.tensor_copy(part[1], rest[:])
                    dve.drain()
                    dve.tensor_tensor(part[2], rest[:], part[1], ALU.subtract).then_inc(split_ready, 1)

            def widen_v(b, g):
                dve.drain()
                wait(dve, av_done, STEPS * (b - 1) + STEPS_OF_GROUP * (g + 1))
                dve.tensor_copy(v_wide[:, :, GROUP_HEADS * g:GROUP_HEADS * (g + 1), 0:HEAD_D],
                                v[:, :, 64 * g:64 * g + 64].rearrange("p i (h d) -> p i h d", d=HEAD_D)).then_inc(v_ready, 1)

            def take_ao(b, m):
                dve.wait_ge(av_done, STEPS * b + TILES * (m + 1))
                if m == 0:
                    wait(dve, close_done, CLOSES * (b - 1) + PAIRS)
                g, half = m // 2, m % 2
                dve.tensor_copy(ao[:, g, half * HALF:(half + 1) * HALF], ps_ao[half]).then_inc(ao_ready, 1)

            def close(b, n):
                dve.wait_ge(close_done, CLOSES * b + n + 1)
                if n < 3:
                    if n == 0:
                        dve.wait_ge(hb_ready, b + 1)
                        wait(dve, placed, 16 * TILES * b)
                    dve.tensor_tensor(pair(rows, n)[:, :, D:2 * D], ps_close[0:TILE, 0:256].rearrange("p (i d) -> p i d", d=D),
                                      pair(hb, n), ALU.add).then_inc(close_read, 1)
                    dve.drain()
                    for t in (2 * n, 2 * n + 1):
                        stats = dve.bn_stats(st2[:, t, :], rows[:, t, D:2 * D])
                    stats.then_inc(h4_ready, 1)
                    dve.drain()
                    for t in (2 * n, 2 * n + 1):
                        dve.bn_aggr(mv2[:, t, :], st2[:, t, :])
                    dve.drain()
                    dve.tensor_scalar(pair(ve2, n), mv2[:, 2 * n:2 * n + 2, 1], LN_EPS, None, ALU.add).then_inc(ve2_done, 1)
                elif n < 6:
                    g = n - 3
                    dve.tensor_copy(x4T[:, 2 * g * TILE:(2 * g + 2) * TILE].rearrange("p (s t) -> p s t", s=2),
                                    ps_close[:, 0:256].rearrange("p (s t) -> p s t", s=2)[:, :, 0:TILE]).then_inc(close_read, 1)
                elif n == 6:
                    dve.tensor_tensor(logits[:], ps_close[0:TILE, 0:384].rearrange("p (i e) -> p i e", e=64)[:, :, 0:EXPERTS],
                                      br_sb[:, :].unsqueeze(1).to_broadcast([TILE, TILES, EXPERTS]), ALU.add).then_inc(close_read, 1)
                    wide = [TILE, TILES, EXPERTS]
                    dve.drain()
                    dve.tensor_reduce(best[:], logits[:], AX.X, ALU.max)
                    dve.drain()
                    dve.tensor_tensor(first[:], logits[:], best[:, :].unsqueeze(2).to_broadcast(wide), ALU.is_equal)
                    dve.drain()
                    dve.tensor_tensor(first[:], first[:], backwards[:, :].unsqueeze(1).to_broadcast(wide), ALU.mult)
                    dve.drain()
                    dve.tensor_reduce(best[:], first[:], AX.X, ALU.max)
                    dve.drain()
                    dve.tensor_tensor(chosen[:], first[:], best[:, :].unsqueeze(2).to_broadcast(wide), ALU.is_equal)\
                        .then_inc(chosen_ready, 1)
                else:
                    for i in range(TILES):
                        dve.tensor_tensor(filled[:, i + 1, :], filled[:, i, :],
                                          ps_close[:, 64 + EXPERTS * i:64 + EXPERTS * (i + 1)], ALU.add)
                        dve.drain()
                    dve.tensor_tensor(first[:], filled[0:TILE, 0:TILES, :],
                                      ps_close[0:TILE, 0:TILES * EXPERTS].rearrange("p (i e) -> p i e", e=EXPERTS), ALU.add)\
                        .then_inc(close_read, 1)
                    dve.drain()
                    dve.tensor_tensor(first[:], first[:], chosen[:], ALU.mult)
                    dve.tensor_copy(filled[:, 0, :], filled[:, TILES, :])
                    dve.tensor_scalar(rows[:, :, 2 * D], rows[:, :, 2 * D], float(SEQ), None, ALU.add)
                    dve.drain()
                    dve.tensor_reduce(place_f[:], first[:], AX.X, ALU.add)
                    dve.drain()
                    dve.tensor_copy(place[:], place_f[:]).then_inc(place_ready, 1)

            def close_norm(b, g):
                dve.wait_ge(rs2_done, PAIRS * b + g + 1)
                for t in (2 * g, 2 * g + 1):
                    norm = dve.tensor_scalar(rows[:, t, 0:D], rows[:, t, D:2 * D], mv2[:, t, 0:1], rs2[:, t:t + 1],
                                             ALU.subtract, ALU.mult)
                norm.then_inc(x4_ready, 1)


            def step(b, has_make, has_attend, has_close):
                for s in range(STEPS):
                    if s == 0 and has_make:
                        make_stats(b + 1)
                    if s == 1 and has_close:
                        take_ao(b - 1, 3)
                        if has_attend:
                            widen_v(b, 1)
                    if s == 1 and has_make:
                        make_norm(b + 1)
                        if not has_attend:
                            dve.wait_ge(loaded, 16 * LOADS)
                    if has_attend and s in (7, 13, 19):
                        take_ao(b, s // 6 - 1)
                    if has_make:
                        if s in MAKE_AT:
                            make(b + 1, MAKE_AT.index(s), not has_attend)
                        if s == 14:
                            widen_v(b + 1, 0)
                            if not has_attend:
                                widen_v(b + 1, 1)
                    if has_close:
                        if s in CLOSE_AT:
                            close(b - 1, CLOSE_AT.index(s))
                        if s in (3, 4, 5):
                            close_norm(b - 1, s - 3)
                    if has_make:
                        for which in range(2):
                            for stage in range(2):
                                if s == (SPLIT_AT[which][stage] if has_attend else MAKE_AT[4 + 2 * which]):
                                    split(b + 1, which, stage)

            dve.wait_ge(consts, 5)
            dve.wait_ge(zeroed, 4)
            dve.wait_ge(h3_first_loaded, 16)
            dve.tensor_copy(filled[:, 0, :], region_i[:])
            dve.tensor_copy(backwards[:], backwards_i[:])
            dve.tensor_scalar(rows[:, :, 2 * D], token_i[:], 1.0, float(-SEQ), ALU.mult, ALU.add)
            sequences(dve, step, needs_residual=True)
            dve.drain()
            dve.tensor_copy(T.ends[:], filled[0:1, 0, :])
            dve.drain()


def experts_by_router(nc, T, moe_rows, w1_sb, w2_sb, b1, b2, out_rows):
    RING = 6
    TURNS = MAX_TILES // RING
    assert TURNS * RING == MAX_TILES
    with ExitStack() as ctx:
        def sb(name, shape, dt=F32):
            return ctx.enter_context(nc.sbuf_tensor(name, shape, dt))

        def sem(name):
            return ctx.enter_context(nc.semaphore(name))

        b1_sb = sb("e_b1", [128, EXPERTS * F_TILES])
        b2_sb = sb("e_b2", [128, EXPERTS * D])
        region_i = sb("e_region_i", [1, EXPERTS], I32)
        region = sb("e_region", [1, EXPERTS])
        tile_i = sb("e_tile_i", [1, MAX_TILES], I32)
        tile_f = sb("e_tile_f", [1, MAX_TILES])
        ends_f = sb("e_ends_f", [1, EXPERTS])
        tiles = sb("e_tiles", [1, EXPERTS])
        tiles_i = sb("e_tiles_i", [1, EXPERTS], I32)
        tiles_to = sb("e_tiles_to", [1, EXPERTS])
        nought = sb("e_nought", [1, EXPERTS])
        passed = sb("e_passed", [1, MAX_TILES, EXPERTS])
        passed_tiles = sb("e_passed_tiles", [1, MAX_TILES, EXPERTS])
        expert_f = sb("e_expert_f", [1, MAX_TILES])
        before_f = sb("e_before_f", [1, MAX_TILES])
        row_f = sb("e_row_f", [1, MAX_TILES])
        expert_of = sb("e_expert_of", [1, MAX_TILES], I32)
        row_of = sb("e_row_of", [1, MAX_TILES], I32)

        rows = [sb(f"e_rows_{r}", [128, ROW1]) for r in range(RING)]
        xT = sb("e_xT", [D, 128])
        h = sb("e_h", [128, HIDDEN])
        hT = sb("e_hT", [128, F_TILES, 128])
        base = sb("e_base", [128, D])
        out = [sb(f"e_out_{r}", [128, D]) for r in range(RING)]
        token = [sb(f"e_token_{r}", [128, 1], I32) for r in range(RING)]

        ps = ctx.enter_context(nc.psum_tensor("e_ps", [128, 8, 512], F32))
        ps_x, ps_h = ps[:, 0, 0:128], ps[:, 1, :]
        ps_y = [ps[:, 2 + n, 0:D] for n in range(2)]
        ps_hT = [ps[:, 4 + n // 2, 128 * (n % 2):128 * (n % 2) + 128] for n in range(F_TILES)]

        loaded, consts = sem("e_loaded"), sem("e_consts")
        table_ready, blanks_stored = sem("e_table_ready"), sem("e_blanks_stored")
        rows_loaded = [sem(f"e_rows_loaded_{r}") for r in range(RING)]
        stored = [sem(f"e_stored_{r}") for r in range(RING)]
        x_done, x_ready = sem("e_x_done"), sem("e_x_ready")
        h_done, h_ready = sem("e_h_done"), sem("e_h_ready")
        hT_done = sem("e_hT_done")
        hT_ready = [sem("e_hT_ready_vector"), sem("e_hT_ready_scalar")]
        y_done, out_ready = sem("e_y_done"), sem("e_out_ready")
        block = ctx.enter_context(nc.Block())

        def wait(eng, semaphore, value):
            if not isinstance(value, int) or value > 0:
                eng.wait_ge(semaphore, value)

        def turns(eng, turn):
            turn(0, True, False)
            with eng.Fori(1, TURNS - 1) as it:
                turn(it, False, False)
            turn(TURNS - 1, False, True)

        def expert(eng, j):
            return eng.value_load(expert_of[0:1, bass.ds(j, 1)], min_val=0, max_val=EXPERTS - 1)

        def store_blanks(eng, experts):
            for e in experts:
                at = eng.value_load(T.ends[0:1, e:e + 1], min_val=0, max_val=EXPERTS * REGION)
                eng.dma_start(moe_rows[bass.ds(at, 128), :], T.blank[:]).then_inc(blanks_stored, 16)

        @block.sync
        def _(sp):
            store_blanks(sp, range(0, EXPERTS, 2))
            sp.dma_start(moe_rows[EXPERTS * REGION:EXPERTS * REGION + 128, :], T.blank[:]).then_inc(blanks_stored, 16)
            sp.dma_start(b1_sb[:].rearrange("p (e f) -> p e f", f=F_TILES), b1.rearrange("e p f -> p e f")).then_inc(loaded, 16)
            sp.dma_start(b2_sb[:], b2.rearrange("e d -> (e d)").partition_broadcast(128)).then_inc(loaded, 16)
            sp.wait_ge(table_ready, 1)
            sp.wait_ge(blanks_stored, 16 * (EXPERTS + 1))

            def turn(it, first, last):
                for r in range(RING):
                    j = RING * it + r
                    at = sp.value_load(row_of[0:1, bass.ds(j, 1)], min_val=0, max_val=EXPERTS * REGION)
                    src = moe_rows[bass.ds(at, 128), :]
                    wait(sp, out_ready, j - RING + 1)
                    sp.dma_start(rows[r][:], src).then_inc(rows_loaded[r], 16)

            turns(sp, turn)

        @block.gpsimd
        def _(pool):
            pool.iota(region_i[:], pattern=[[REGION, EXPERTS]], base=0, channel_multiplier=0).then_inc(consts, 1)
            pool.iota(tile_i[:], pattern=[[1, MAX_TILES]], base=0, channel_multiplier=0).then_inc(consts, 1)
            pool.memset(nought[:], 0.0).then_inc(consts, 1)
            out_next = pool.alloc_register("out_next")
            pool.reg_mov(out_next, 1)

            def turn(it, first, last):
                for r in range(RING):
                    j = RING * it + r
                    pool.wait_ge(out_ready, j + 1 if isinstance(j, int) else out_next)
                    pool.reg_add(out_next, out_next, 1)
                    pool.indirect_dma_start(
                        out=out_rows[:, :], out_offset=bass.IndirectOffsetOnAxis(ap=token[r][:], axis=0),
                        in_=out[r][:], in_offset=None, bounds_check=TOKENS - 1, oob_is_err=False).then_inc(stored[r], 16)

            turns(pool, turn)
            for r in range(RING):
                pool.wait_ge(stored[r], 16 * TURNS)

        @block.tensor
        def _(pe):
            def turn_x(it, r):
                pe.wait_ge(rows_loaded[r], 16 * (it + 1))
                pe.transpose(ps_x, rows[r][:, 0:D], T.ident[:]).then_inc(x_done, 1)

            def hidden(it, r, e):
                j = RING * it + r
                pe.wait_ge(x_ready, j + 1)
                pe.matmul(ps_h, xT[:], w1_sb[:, bass.ds(e * HIDDEN, HIDDEN)], start=True, stop=True).then_inc(h_done, 1)

            def turn_h(it, r):
                j = RING * it + r
                pe.wait_ge(h_ready, j + 1)
                for f in range(F_TILES):
                    mm = pe.transpose(ps_hT[f], h[:, 128 * f:128 * f + 128], T.ident[:])
                mm.then_inc(hT_done, 1)

            def output(it, r, e):
                j = RING * it + r
                for half in hT_ready:
                    pe.wait_ge(half, j + 1)
                wait(pe, out_ready, j - 1)
                for f in range(F_TILES):
                    mm = pe.matmul(ps_y[r % 2], hT[:, f, :], w2_sb[:, bass.ds(e * (F_TILES * D) + f * D, D)],
                                   start=(f == 0), stop=(f == F_TILES - 1))
                mm.then_inc(y_done, 1)

            def turn(it, first, last):
                for r in range(RING):
                    j = RING * it + r
                    hidden(it, r, expert(pe, j))
                    if not (last and r == RING - 1):
                        turn_x(it + (r + 1) // RING, (r + 1) % RING)
                    if not (first and r == 0):
                        output(it - (r == 0), (r - 1) % RING, expert(pe, j - 1))
                    turn_h(it, r)

            pe.wait_ge(table_ready, 1)
            turn_x(0, 0)
            turns(pe, turn)
            output(TURNS - 1, RING - 1, expert(pe, MAX_TILES - 1))

        @block.scalar
        def _(act):
            def move_x(j):
                act.wait_ge(x_done, j + 1)
                act.copy(xT[:], ps_x).then_inc(x_ready, 1)

            def turn(it, first, last):
                for r in range(RING):
                    j = RING * it + r
                    act.wait_ge(h_done, j + 1)
                    act.copy(h[:], ps_h).then_inc(h_ready, 1)
                    if not (last and r == RING - 1):
                        move_x(j + 1)
                    e = expert(act, j)
                    act.wait_ge(hT_done, j + 1)
                    at = act.snap(e * F_TILES)
                    for f in (2, 3):
                        step = act.activation(hT[:, f, :], ps_hT[f], ACT.Relu, bias=b1_sb[:, bass.ds(at + f, 1)])
                    step.then_inc(hT_ready[1], 1)

            store_blanks(act, range(1, EXPERTS, 2))
            act.wait_ge(table_ready, 1)
            act.wait_ge(loaded, 32)
            move_x(0)
            turns(act, turn)

        @block.vector
        def _(dve):
            dve.wait_ge(consts, 3)
            dve.tensor_copy(region[:], region_i[:])
            dve.tensor_copy(tile_f[:], tile_i[:])
            dve.tensor_copy(ends_f[:], T.ends[:])
            dve.drain()
            dve.tensor_tensor(tiles[:], ends_f[:], region[:], ALU.subtract)
            dve.drain()
            dve.tensor_scalar(tiles_i[:], tiles[:], 127.0, None, ALU.add)
            dve.drain()
            dve.tensor_scalar(tiles_i[:], tiles_i[:], 7, None, ALU.logical_shift_right)
            dve.drain()
            dve.tensor_copy(tiles[:], tiles_i[:])
            dve.drain()
            dve.tensor_tensor_scan(tiles_to[:], tiles[:], nought[:], 0.0, ALU.add, ALU.add)
            dve.drain()
            wide = [1, MAX_TILES, EXPERTS]
            dve.tensor_tensor(passed[:], tiles_to[:, :].unsqueeze(1).to_broadcast(wide),
                              tile_f[:, :].unsqueeze(2).to_broadcast(wide), ALU.is_le)
            dve.drain()
            dve.tensor_tensor(passed_tiles[:], passed[:], tiles[:, :].unsqueeze(1).to_broadcast(wide), ALU.mult)
            dve.tensor_reduce(expert_f[:], passed[:], AX.X, ALU.add)
            dve.drain()
            dve.tensor_reduce(before_f[:], passed_tiles[:], AX.X, ALU.add)
            dve.tensor_scalar(expert_of[:], expert_f[:], float(EXPERTS - 1), None, ALU.min)
            dve.drain()
            dve.tensor_tensor(row_f[:], tile_f[:], before_f[:], ALU.subtract)
            dve.drain()
            dve.tensor_scalar(row_f[:], row_f[:], 128.0, None, ALU.mult)
            dve.drain()
            dve.scalar_tensor_tensor(row_f[:], expert_f[:], float(REGION), row_f[:], ALU.mult, ALU.add)
            dve.drain()
            dve.tensor_scalar(row_of[:], row_f[:], float(EXPERTS * REGION), None, ALU.min)
            dve.drain()
            dve.sem_inc(table_ready, 1)
            dve.wait_ge(loaded, 32)

            def relu(it, r, e):
                j = RING * it + r
                dve.wait_ge(hT_done, j + 1)
                for f in (0, 1):
                    step = dve.tensor_scalar(hT[:, f, :], ps_hT[f], b1_sb[:, bass.ds(e * F_TILES + f, 1)],
                                             0.0, ALU.add, ALU.max)
                step.then_inc(hT_ready[0], 1)

            def finish(it, r, e):
                j = RING * it + r
                dve.drain()
                wait(dve, stored[r], 16 * it)
                dve.tensor_tensor(base[:], rows[r][:, D:2 * D], b2_sb[:, bass.ds(e * D, D)], ALU.add)
                dve.tensor_copy(token[r][:], rows[r][:, 2 * D:ROW1])
                dve.drain()
                dve.wait_ge(y_done, j + 1)
                dve.tensor_tensor(out[r][:], ps_y[r % 2], base[:], ALU.add).then_inc(out_ready, 1)

            def turn(it, first, last):
                for r in range(RING):
                    j = RING * it + r
                    relu(it, r, expert(dve, j))
                    if not (first and r == 0):
                        finish(it - (r == 0), (r - 1) % RING, expert(dve, j - 1))

            turns(dve, turn)
            finish(TURNS - 1, RING - 1, expert(dve, MAX_TILES - 1))


def build(nc, x, conv_w, conv_b, a0, f0, a1, f1, out_rows):
    def scratch(name, shape, dt=F32):
        return nc.dram_tensor(name, shape, dt, kind="Internal").ap()

    x2_rows = scratch("x2_rows", [TOKENS, ROW0])
    residual_rows = scratch("residual_rows", [TOKENS, D])
    logits_rows = scratch("logits_rows", [EXPERTS, TOKENS])
    split_q = scratch("split_q", [PARTS, D, SEQ], BF16)
    split_k = scratch("split_k", [PARTS, D, SEQ], BF16)
    moe_rows = scratch("moe_rows", [EXPERTS * REGION + 128, ROW1])
    with ExitStack() as ctx:
        T = constants(nc, ctx)
        prepare(nc, T)
        conv_and_causal_attention(nc, T, x, conv_w, conv_b, a0["Wq"], a0["bq"], a0["Wk"], a0["bk"], a0["Wv"], a0["bv"],
                                  a0["gamma"], a0["beta"], f0["Wr"], residual_rows, x2_rows[:, 0:D], logits_rows)
        select_tokens(nc, T, logits_rows, x2_rows)
        experts_by_token_choice(nc, T, x2_rows, residual_rows, f0["W1"], f0["b1"], f0["W2"], f0["b2"])
        w1_sb = ctx.enter_context(nc.sbuf_tensor("experts_w1", [D, EXPERTS * HIDDEN], F32))
        w2_sb = ctx.enter_context(nc.sbuf_tensor("experts_w2", [128, EXPERTS * F_TILES * D], F32))
        sigmoid_attention(nc, T, residual_rows, a1["Wq"], a1["bq"], a1["Wk"], a1["bk"], a1["Wv"], a1["bv"],
                          a1["Wo"], a1["bo"], f1["Wr"], f1["br"], split_q, split_k, moe_rows,
                          f1["W1"], w1_sb, f1["W2"], w2_sb)
        experts_by_router(nc, T, moe_rows, w1_sb, w2_sb, f1["b1"], f1["b2"], out_rows)


def by_head_dimension(w):
    return np.ascontiguousarray(w.reshape(-1, HEADS, HEAD_D).transpose(0, 2, 1).reshape(-1, D))


def hidden_on_partitions(b):
    return np.ascontiguousarray(b.reshape(EXPERTS, F_TILES, 128).transpose(0, 2, 1))


def heads_apart(w):
    apart = np.zeros((4, 32, 2, D), w.dtype)
    apart[:, 0:HEAD_D] = w.reshape(2, 4, HEAD_D, D).transpose(1, 2, 0, 3)
    return apart.reshape(128, 2, D)


def kernel(**inputs):
    import concourse.bacc as bacc
    from concourse.bass_utils import run_bass_kernel_spmd

    inputs = {name: np.asarray(a) for name, a in inputs.items()}
    arrays = {"x": inputs["x"], "conv_b": inputs["L0_tok_bias"],
              "conv_w": np.ascontiguousarray(inputs["L0_tok_weight"].transpose(2, 1, 0).reshape(TAPS * C_IN, D))}
    for layer in ("L0_attn", "L0_ffn", "L1_attn", "L1_ffn"):
        arrays.update({name: a for name, a in inputs.items() if name.startswith(layer)})
    for name in ("L0_ffn_b1", "L1_ffn_b1"):
        arrays[name] = hidden_on_partitions(arrays[name])
    for name in ("L1_attn_Wq", "L1_attn_Wk"):
        arrays[name] = by_head_dimension(arrays[name])
    for name in ("L1_attn_bq", "L1_attn_bk"):
        arrays[name] = by_head_dimension(arrays[name]).reshape(D, 1)
    arrays["L1_attn_Wo"] = heads_apart(arrays["L1_attn_Wo"])

    nc = bacc.Bacc("TRN2", target_bir_lowering=False, num_devices=1)
    aps = {name: nc.dram_tensor(name, a.shape, mybir.dt.from_np(a.dtype), kind="ExternalInput").ap()
           for name, a in arrays.items()}
    out = nc.dram_tensor("out", [TOKENS, D], F32, kind="ExternalOutput").ap()

    def of(layer):
        return {name[len(layer) + 1:]: ap for name, ap in aps.items() if name.startswith(layer)}

    build(nc, aps["x"], aps["conv_w"], aps["conv_b"], of("L0_attn"), of("L0_ffn"), of("L1_attn"), of("L1_ffn"), out)
    got = run_bass_kernel_spmd(nc, [arrays], core_ids=[0])
    return got.results[0]["out"].reshape(BATCH, SEQ, D)
```
